# Optimizing a Trainium2 kernel written in Bass

```python
import numpy as np
import jax
import jax.numpy as jnp

def _softmax(x, axis=-1):
    return jax.nn.softmax(x, axis=axis)
def _gelu(x):
    return jax.nn.gelu(x, approximate=True)
def _silu(x):
    return jax.nn.silu(x)
def _sigmoid(x):
    return jax.nn.sigmoid(x)
def _layernorm(x, axis=-1, eps=1e-5):
    m = jnp.mean(x, axis=axis, keepdims=True)
    v = jnp.var(x, axis=axis, keepdims=True)
    return (x - m) / jnp.sqrt(v + eps)
def _scatter_add(tgt, idx, src, axis=0):
    return tgt.at[idx].add(src)
def _segment_sum(src, seg, n):
    return jax.ops.segment_sum(src, seg, n)

kernel_name = 'mk_conv_preact_d4_conv_nhwc256_a6b0e0'

def setup_inputs(seed: int = 0):
    np.random.seed(seed)
    _w = jnp.asarray
    def _rec_inputs():
        import jax
        import jax.numpy as jnp
        _gk = jax.random.key(seed)
        x = -0.000929 + 1 * jax.random.normal(jax.random.fold_in(_gk, 1), (1, 64, 64, 256), jnp.float32)
        return x
    x = _rec_inputs()
    def _L0_conv_setup():
        import jax, jax.numpy as jnp
        import numpy as np
        from jax import lax
        B, H, W, C, NH = (1, 64, 64, 256, 8)
        DN = ('NCHW', 'OIHW', 'NCHW')

        def _conv(x, w, pad, groups=1):
            return lax.conv_general_dilated(x, w, window_strides=(1, 1), padding=[(pad, pad), (pad, pad)], dimension_numbers=DN, feature_group_count=groups)
        key = jax.random.key(seed)
        ks = jax.random.split(key, 7)
        s = 0.05
        return {'x': jax.random.normal(ks[0], (B, H, W, C), jnp.float32), 'W1': jax.random.normal(ks[1], (C, C, 1, 1), jnp.float32) * s, 'W3': jax.random.normal(ks[2], (C, C, 3, 3), jnp.float32) * s, 'W5': jax.random.normal(ks[3], (C, C, 5, 5), jnp.float32) * s, 'Wdw': jax.random.normal(ks[4], (3 * C, 1, 3, 3), jnp.float32) * s, 'Wproj': jax.random.normal(ks[5], (C, C, 1, 1), jnp.float32) * s, 'temperature': jnp.ones((NH, 1, 1), jnp.float32)}
    _L0_conv_all = _L0_conv_setup()
    _L0_conv_in = {k: v for k, v in _L0_conv_all.items() if k in ('W1', 'W3', 'W5', 'Wdw', 'Wproj', 'temperature', )}
    del _L0_conv_all

    def _L1_conv_setup():
        import jax, jax.numpy as jnp
        import numpy as np
        B, H, W, C = (32, 64, 64, 256)
        CROP = 48
        ITER_N = 5

        def _conv2d_same(y, w, b):
            out = jax.lax.conv_general_dilated(y, w, window_strides=(1, 1), padding='SAME', dimension_numbers=('NHWC', 'HWIO', 'NHWC'))
            return out + b
        key = jax.random.key(seed)
        k0, k1, k2 = jax.random.split(key, 3)
        x = jax.random.normal(k0, (B, H, W, C), dtype=jnp.float32)
        w1 = jax.random.normal(k1, (3, 3, C, C), dtype=jnp.float32) * 0.02
        b1 = jnp.zeros((C,), dtype=jnp.float32)
        w2 = jax.random.normal(k2, (3, 3, C, C), dtype=jnp.float32) * 0.02
        b2 = jnp.zeros((C,), dtype=jnp.float32)
        return {'x': x, 'w1': w1, 'b1': b1, 'w2': w2, 'b2': b2}
    _L1_conv_all = _L1_conv_setup()
    _L1_conv_in = {k: v for k, v in _L1_conv_all.items() if k in ('w1', 'b1', 'w2', 'b2', )}
    del _L1_conv_all

    def _L2_conv_setup():
        import jax, jax.numpy as jnp
        import numpy as np
        from jax import lax
        K_SIZE = 3
        STRIDE = 1
        PADDING = 1

        def _dcnv2(x, offset_w, offset_b, dcn_weight):
            k, stride, padding = (K_SIZE, STRIDE, PADDING)
            N, H, W, C = x.shape
            kk = k * k
            om = lax.conv_general_dilated(x, offset_w, window_strides=(stride, stride), padding='SAME', dimension_numbers=('NHWC', 'HWIO', 'NHWC')) + offset_b
            offset = om[..., :2 * kk]
            mask = jax.nn.sigmoid(om[..., 2 * kk:])
            oH = (H + 2 * padding - (k - 1)) // stride
            oW = (W + 2 * padding - (k - 1)) // stride
            pad_x = jnp.pad(x, ((0, 0), (padding, padding + 1), (padding, padding + 1), (0, 0)))
            base_y = jnp.arange(oH, dtype=x.dtype) * stride + padding
            base_x = jnp.arange(oW, dtype=x.dtype) * stride + padding
            kr = jnp.arange(k, dtype=x.dtype) - (k - 1) / 2.0
            inner_y = jnp.repeat(kr, k)
            inner_x = jnp.tile(kr, k)
            off_yx = offset.reshape(N, oH, oW, kk, 2)
            pos_y = base_y[None, :, None, None] + inner_y[None, None, None, :] + off_yx[..., 0]
            pos_x = base_x[None, None, :, None] + inner_x[None, None, None, :] + off_yx[..., 1]
            pos_y = jnp.clip(pos_y, 0.0, H + 2 * padding - 1.0)
            pos_x = jnp.clip(pos_x, 0.0, W + 2 * padding - 1.0)
            y1 = jnp.floor(pos_y)
            x1 = jnp.floor(pos_x)
            y1i = y1.astype(jnp.int32)
            x1i = x1.astype(jnp.int32)
            y2i = y1i + 1
            x2i = x1i + 1
            gather = jax.vmap(lambda px, yi, xi: px[yi, xi])
            v1 = gather(pad_x, y1i, x1i)
            v2 = gather(pad_x, y1i, x2i)
            v3 = gather(pad_x, y2i, x1i)
            v4 = gather(pad_x, y2i, x2i)
            lh = (pos_y - y1)[..., None]
            lw = (pos_x - x1)[..., None]
            hh = 1.0 - lh
            hw = 1.0 - lw
            value = (hh * hw * v1 + hh * lw * v2 + lh * hw * v3 + lh * lw * v4) * mask[..., None]
            value = jnp.transpose(value, (0, 1, 2, 4, 3)).reshape(N, oH, oW, C * kk)
            w = jnp.transpose(dcn_weight, (1, 2, 3, 0)).reshape(C * kk, -1)
            return jnp.einsum('nhwc,cf->nhwf', value, w)
        key = jax.random.key(seed)
        k1, k2, k3 = jax.random.split(key, 3)
        x = jax.random.normal(k1, (4, 64, 64, 256), dtype=jnp.float32)
        offset_w = jax.random.normal(k2, (3, 3, 256, 27), dtype=jnp.float32) * 0.01
        offset_b = jnp.zeros((1, 1, 1, 27), dtype=jnp.float32)
        dcn_weight = jax.random.normal(k3, (256, 256, 3, 3), dtype=jnp.float32) * 0.02
        return {'x': x, 'offset_w': offset_w, 'offset_b': offset_b, 'dcn_weight': dcn_weight}
    _L2_conv_all = _L2_conv_setup()
    _L2_conv_in = {k: v for k, v in _L2_conv_all.items() if k in ('offset_w', 'offset_b', 'dcn_weight', )}
    del _L2_conv_all

    def _L3_conv_setup():
        import jax, jax.numpy as jnp
        import numpy as np
        from jax import lax
        NUM_HEADS = 8
        KEY_DIM = 32
        key = jax.random.key(seed)
        ks = jax.random.split(key, 13)
        B, H, W, C = (8, 64, 64, 256)

        def nrm(k, shape, s):
            return jax.random.normal(k, shape, jnp.float32) * s
        return {'x': jax.random.normal(ks[0], (B, H, W, C), jnp.float32), 'mask_h': nrm(ks[1], (NUM_HEADS, H, H), 1.0), 'mask_w': nrm(ks[2], (NUM_HEADS, W, W), 1.0), 'Wq': nrm(ks[3], (C, C), 0.02), 'bq': jnp.zeros((C,), jnp.float32), 'Wk': nrm(ks[4], (C, C), 0.02), 'bk': jnp.zeros((C,), jnp.float32), 'Wv': nrm(ks[5], (C, C), 0.02), 'bv': jnp.zeros((C,), jnp.float32), 'Wlepe': nrm(ks[6], (5, 5, 1, C), 0.05), 'blepe': jnp.zeros((C,), jnp.float32), 'Wo': nrm(ks[7], (C, C), 0.02), 'bo': jnp.zeros((C,), jnp.float32)}
    _L3_conv_all = _L3_conv_setup()
    _L3_conv_in = {k: v for k, v in _L3_conv_all.items() if k in ('mask_h', 'mask_w', 'Wq', 'bq', 'Wk', 'bk', 'Wv', 'bv', 'Wlepe', 'blepe', 'Wo', 'bo', )}
    del _L3_conv_all

    return {
        "x": x,
        "L0_conv_W1": _L0_conv_in["W1"],
        "L0_conv_W3": _L0_conv_in["W3"],
        "L0_conv_W5": _L0_conv_in["W5"],
        "L0_conv_Wdw": _L0_conv_in["Wdw"],
        "L0_conv_Wproj": _L0_conv_in["Wproj"],
        "L0_conv_temperature": _L0_conv_in["temperature"],
        "L1_conv_w1": _L1_conv_in["w1"],
        "L1_conv_b1": _L1_conv_in["b1"],
        "L1_conv_w2": _L1_conv_in["w2"],
        "L1_conv_b2": _L1_conv_in["b2"],
        "L2_conv_offset_w": _L2_conv_in["offset_w"],
        "L2_conv_offset_b": _L2_conv_in["offset_b"],
        "L2_conv_dcn_weight": _L2_conv_in["dcn_weight"],
        "L3_conv_mask_h": _L3_conv_in["mask_h"],
        "L3_conv_mask_w": _L3_conv_in["mask_w"],
        "L3_conv_Wq": _L3_conv_in["Wq"],
        "L3_conv_bq": _L3_conv_in["bq"],
        "L3_conv_Wk": _L3_conv_in["Wk"],
        "L3_conv_bk": _L3_conv_in["bk"],
        "L3_conv_Wv": _L3_conv_in["Wv"],
        "L3_conv_bv": _L3_conv_in["bv"],
        "L3_conv_Wlepe": _L3_conv_in["Wlepe"],
        "L3_conv_blepe": _L3_conv_in["blepe"],
        "L3_conv_Wo": _L3_conv_in["Wo"],
        "L3_conv_bo": _L3_conv_in["bo"],
    }

def reference(x, L0_conv_W1, L0_conv_W3, L0_conv_W5, L0_conv_Wdw, L0_conv_Wproj, L0_conv_temperature, L1_conv_w1, L1_conv_b1, L1_conv_w2, L1_conv_b2, L2_conv_offset_w, L2_conv_offset_b, L2_conv_dcn_weight, L3_conv_mask_h, L3_conv_mask_w, L3_conv_Wq, L3_conv_bq, L3_conv_Wk, L3_conv_bk, L3_conv_Wv, L3_conv_bv, L3_conv_Wlepe, L3_conv_blepe, L3_conv_Wo, L3_conv_bo):
    import jax
    import jax.numpy as jnp
    def _L0_conv_ref(x, W1, W3, W5, Wdw, Wproj, temperature):
        import jax, jax.numpy as jnp
        import numpy as np
        from jax import lax
        B, H, W, C, NH = (1, 64, 64, 256, 8)
        DN = ('NCHW', 'OIHW', 'NCHW')

        def _conv(x, w, pad, groups=1):
            return lax.conv_general_dilated(x, w, window_strides=(1, 1), padding=[(pad, pad), (pad, pad)], dimension_numbers=DN, feature_group_count=groups)
        b, h, w, c = x.shape
        xc = jnp.transpose(x, (0, 3, 1, 2))
        qkv = jnp.concatenate([_conv(xc, W1, 0), _conv(xc, W3, 1), _conv(xc, W5, 2)], axis=1)
        qkv = _conv(qkv, Wdw, 1, groups=3 * c)
        q, k, v = jnp.split(qkv, 3, axis=1)

        def heads(t):
            return jnp.transpose(t.reshape(b, NH, c // NH, h * w), (0, 1, 3, 2))
        q, k, v = (heads(q), heads(k), heads(v))

        def l2n(t):
            n = jnp.sqrt(jnp.sum(t * t, axis=-1, keepdims=True))
            return t / jnp.maximum(n, 1e-12)
        q, k = (l2n(q), l2n(k))
        attn = jnp.einsum('bhnc,bhmc->bhnm', q, k) * temperature
        attn = jax.nn.softmax(attn, axis=-1)
        o = jnp.einsum('bhnm,bhmc->bhnc', attn, v)
        o = jnp.transpose(o, (0, 1, 3, 2)).reshape(b, c, h, w)
        o = _conv(o, Wproj, 0)
        return jnp.transpose(o, (0, 2, 3, 1))

    def _L1_conv_ref(x, w1, b1, w2, b2):
        import jax, jax.numpy as jnp
        import numpy as np
        B, H, W, C = (32, 64, 64, 256)
        CROP = 48
        ITER_N = 5

        def _conv2d_same(y, w, b):
            out = jax.lax.conv_general_dilated(y, w, window_strides=(1, 1), padding='SAME', dimension_numbers=('NHWC', 'HWIO', 'NHWC'))
            return out + b
        b, h, w_, c = x.shape
        ch, cw = (min(CROP, h), min(CROP, w_))
        oh, ow = ((h - ch) // 2, (w_ - cw) // 2)
        x_sub = x[:, oh:oh + ch, ow:ow + cw, :]
        M = ch * cw
        xs = x_sub.reshape(b, c, M)
        Minv = jnp.float32(1.0 / M)
        I_hat = Minv * (jnp.eye(M, dtype=x.dtype) - Minv * jnp.ones((M, M), dtype=x.dtype))
        cov = jnp.einsum('bcm,mn,bdn->bcd', xs, I_hat, xs)
        I3 = 3.0 * jnp.eye(c, dtype=x.dtype)
        normA = jnp.einsum('bii->b', cov)
        A = cov / normA[:, None, None]
        ZY = 0.5 * (I3 - A)
        Y = jnp.matmul(A, ZY)
        Z = ZY
        for _ in range(1, ITER_N - 1):
            ZY = 0.5 * (I3 - jnp.matmul(Z, Y))
            Y = jnp.matmul(Y, ZY)
            Z = jnp.matmul(ZY, Z)
        ZY = 0.5 * jnp.matmul(Y, I3 - jnp.matmul(Z, Y))
        y = ZY * jnp.sqrt(normA)[:, None, None]
        y = jnp.mean(y, axis=-1).reshape(b, 1, 1, c)
        y = jax.nn.relu(_conv2d_same(y, w1, b1))
        y = jax.nn.sigmoid(_conv2d_same(y, w2, b2))
        return y * x

    def _L2_conv_ref(x, offset_w, offset_b, dcn_weight):
        import jax, jax.numpy as jnp
        import numpy as np
        from jax import lax
        K_SIZE = 3
        STRIDE = 1
        PADDING = 1

        def _dcnv2(x, offset_w, offset_b, dcn_weight):
            k, stride, padding = (K_SIZE, STRIDE, PADDING)
            N, H, W, C = x.shape
            kk = k * k
            om = lax.conv_general_dilated(x, offset_w, window_strides=(stride, stride), padding='SAME', dimension_numbers=('NHWC', 'HWIO', 'NHWC')) + offset_b
            offset = om[..., :2 * kk]
            mask = jax.nn.sigmoid(om[..., 2 * kk:])
            oH = (H + 2 * padding - (k - 1)) // stride
            oW = (W + 2 * padding - (k - 1)) // stride
            pad_x = jnp.pad(x, ((0, 0), (padding, padding + 1), (padding, padding + 1), (0, 0)))
            base_y = jnp.arange(oH, dtype=x.dtype) * stride + padding
            base_x = jnp.arange(oW, dtype=x.dtype) * stride + padding
            kr = jnp.arange(k, dtype=x.dtype) - (k - 1) / 2.0
            inner_y = jnp.repeat(kr, k)
            inner_x = jnp.tile(kr, k)
            off_yx = offset.reshape(N, oH, oW, kk, 2)
            pos_y = base_y[None, :, None, None] + inner_y[None, None, None, :] + off_yx[..., 0]
            pos_x = base_x[None, None, :, None] + inner_x[None, None, None, :] + off_yx[..., 1]
            pos_y = jnp.clip(pos_y, 0.0, H + 2 * padding - 1.0)
            pos_x = jnp.clip(pos_x, 0.0, W + 2 * padding - 1.0)
            y1 = jnp.floor(pos_y)
            x1 = jnp.floor(pos_x)
            y1i = y1.astype(jnp.int32)
            x1i = x1.astype(jnp.int32)
            y2i = y1i + 1
            x2i = x1i + 1
            gather = jax.vmap(lambda px, yi, xi: px[yi, xi])
            v1 = gather(pad_x, y1i, x1i)
            v2 = gather(pad_x, y1i, x2i)
            v3 = gather(pad_x, y2i, x1i)
            v4 = gather(pad_x, y2i, x2i)
            lh = (pos_y - y1)[..., None]
            lw = (pos_x - x1)[..., None]
            hh = 1.0 - lh
            hw = 1.0 - lw
            value = (hh * hw * v1 + hh * lw * v2 + lh * hw * v3 + lh * lw * v4) * mask[..., None]
            value = jnp.transpose(value, (0, 1, 2, 4, 3)).reshape(N, oH, oW, C * kk)
            w = jnp.transpose(dcn_weight, (1, 2, 3, 0)).reshape(C * kk, -1)
            return jnp.einsum('nhwc,cf->nhwf', value, w)
        return _dcnv2(x, offset_w, offset_b, dcn_weight)

    def _L3_conv_ref(x, mask_h, mask_w, Wq, bq, Wk, bk, Wv, bv, Wlepe, blepe, Wo, bo):
        import jax, jax.numpy as jnp
        import numpy as np
        from jax import lax
        NUM_HEADS = 8
        KEY_DIM = 32
        B, H, W, C = x.shape
        scaling = KEY_DIM ** (-0.5)
        q = x @ Wq.T + bq
        k = (x @ Wk.T + bk) * scaling
        v = x @ Wv.T + bv
        lepe = lax.conv_general_dilated(v, Wlepe, window_strides=(1, 1), padding=((2, 2), (2, 2)), dimension_numbers=('NHWC', 'HWIO', 'NHWC'), feature_group_count=C) + blepe
        qr = q.reshape(B, H, W, NUM_HEADS, KEY_DIM)
        kr = k.reshape(B, H, W, NUM_HEADS, KEY_DIM)
        vr = v.reshape(B, H, W, NUM_HEADS, -1)
        attn_w = jax.nn.softmax(jnp.einsum('bhqnd,bhknd->bhnqk', qr, kr) + mask_w[None, None], axis=-1)
        v1 = jnp.einsum('bhnqk,bhknd->bhqnd', attn_w, vr)
        attn_h = jax.nn.softmax(jnp.einsum('bqwnd,bkwnd->bwnqk', qr, kr) + mask_h[None, None], axis=-1)
        out = jnp.einsum('bwnqk,bkwnd->bqwnd', attn_h, v1)
        out = out.reshape(B, H, W, C) + lepe
        return out @ Wo.T + bo

    def _gn(v, G=32, eps=1e-5):
        B_, H_, W_, C_ = v.shape
        g = v.reshape(B_, H_, W_, G, C_ // G)
        m = jnp.mean(g, axis=(1, 2, 4), keepdims=True)
        s = jnp.var(g, axis=(1, 2, 4), keepdims=True)
        return ((g - m) / jnp.sqrt(s + eps)).reshape(v.shape)

    def _ln_c(v, eps=1e-6):
        m = jnp.mean(v, axis=-1, keepdims=True)
        s = jnp.var(v, axis=-1, keepdims=True)
        return (v - m) / jnp.sqrt(s + eps)

    def _ln_t(v, eps=1e-5):
        m = jnp.mean(v, axis=-1, keepdims=True)
        s = jnp.var(v, axis=-1, keepdims=True)
        return (v - m) / jnp.sqrt(s + eps)

    def _to_tokens(v):
        B_, H_, W_, C_ = v.shape
        return v.reshape(B_, H_ * W_, C_)
    def _from_tokens(t, like):
        return t.reshape(like.shape)

    x = x + _L0_conv_ref(_gn(x), L0_conv_W1, L0_conv_W3, L0_conv_W5, L0_conv_Wdw, L0_conv_Wproj, L0_conv_temperature)
    x = x + _L1_conv_ref(_gn(x), L1_conv_w1, L1_conv_b1, L1_conv_w2, L1_conv_b2)
    x = x + _L2_conv_ref(_gn(x), L2_conv_offset_w, L2_conv_offset_b, L2_conv_dcn_weight)
    x = x + _L3_conv_ref(_gn(x), L3_conv_mask_h, L3_conv_mask_w, L3_conv_Wq, L3_conv_bq, L3_conv_Wk, L3_conv_bk, L3_conv_Wv, L3_conv_bv, L3_conv_Wlepe, L3_conv_blepe, L3_conv_Wo, L3_conv_bo)
    return x


_drawn_inputs = setup_inputs


def setup_inputs(seed=0):
    import zlib

    import numpy as np

    out = dict(_drawn_inputs(seed))
    spreads = {'L0_conv_temperature': (1.0, 0.6),
     'L1_conv_b1': (0.0, 0.8),
     'L1_conv_b2': (0.0, 1.754),
     'L2_conv_offset_b': (0.0, 0.8),
     'L3_conv_bq': (0.0, 2.0),
     'L3_conv_bk': (0.0, 2.0),
     'L3_conv_bv': (0.0, 0.383),
     'L3_conv_blepe': (0.0, 1.051),
     'L3_conv_bo': (0.0, 0.311)}
    factors = {'L0_conv_W1': 8.0,
     'L0_conv_W3': 8.0,
     'L0_conv_W5': 8.0,
     'L0_conv_Wdw': 8.0,
     'L0_conv_Wproj': 7.599,
     'L1_conv_w1': 38.642,
     'L1_conv_w2': 8.0,
     'L3_conv_mask_h': 21.339,
     'L3_conv_mask_w': 21.378,
     'L3_conv_Wq': 29.319,
     'L3_conv_Wk': 28.365,
     'L3_conv_Wv': 3.418,
     'L3_conv_Wlepe': 3.334}
    for name, (base, spread) in spreads.items():
        noise = np.random.default_rng([zlib.crc32(name.encode()), seed]).standard_normal(out[name].shape)
        drawn = base * np.exp(spread * noise) if base else spread * noise
        out[name] = jnp.asarray(drawn.astype(out[name].dtype))
    for name, factor in factors.items():
        out[name] = (out[name] * factor).astype(out[name].dtype)
    return out
```

```python
import numpy as np
import concourse.bass as bass
from concourse import mybir
from contextlib import ExitStack

F32, F32R, F16 = mybir.dt.float32, mybir.dt.float32r, mybir.dt.float16
I32 = mybir.dt.int32
ALU = mybir.AluOpType
ACT = mybir.ActivationFunctionType
AX = mybir.AxisListType
ds = bass.ds

P = 128
SIDE = 64
PX = SIDE * SIDE
C = 256
CB = C // P
GROUP = 8
CH = 512
ROWS = CH // SIDE
NCH = PX // CH
HEADS, HD = 8, 32
HPB = P // HD
PAD5 = SIDE + 4
PAD3 = SIDE + 2

class Names:

    def __init__(self, nc, stack, stage):
        self.nc, self.stack, self.stage = nc, stack, stage

    def sb(self, name, shape, dt=F32):
        return self.stack.enter_context(self.nc.sbuf_tensor(f"{self.stage}_{name}", shape, dt))

    def ps(self, name, shape, dt=F32):
        return self.stack.enter_context(self.nc.psum_tensor(f"{self.stage}_{name}", shape, dt))

    def sem(self, name):
        return self.stack.enter_context(self.nc.semaphore(f"{self.stage}_{name}"))

class GroupNorm:

    def __init__(self, n, eps=1e-5):
        self.eps = eps
        self.stats = n.sb("gn_stats", [P, CB, NCH, 6])
        self.mv = n.sb("gn_mv", [P, CB, 2])
        self.m12 = n.sb("gn_m12", [P, CB, 2])
        self.g12 = n.sb("gn_g12", [P, CB, 2])
        self.var = n.sb("gn_var", [P, CB])
        self.std = n.sb("gn_std", [P, CB])
        self.scale = n.sb("gn_scale", [P, CB])
        self.shift = n.sb("gn_shift", [P, CB])
        self.step = n.sem("gn_step")
        self.moments = n.sem("gn_moments")
        self.joined = n.sem("gn_joined")
        self.var_ready = n.sem("gn_var_ready")
        self.std_ready = n.sem("gn_std_ready")
        self.ready = n.sem("gn_ready")

    def vector_stats(self, dve, x, wait_chunk):
        for b in range(CB):
            for c in range(NCH):
                wait_chunk(b, c)
                dve.bn_stats(self.stats[:, b, c, :], x[:, b, c * CH:(c + 1) * CH]).then_inc(self.step, 1)
        dve.wait_ge(self.step, CB * NCH)
        for b in range(CB):
            dve.bn_aggr(self.mv[:, b, :], self.stats[:, b, :, :].rearrange("p c s -> p (c s)")).then_inc(self.step, 1)
        dve.wait_ge(self.step, CB * NCH + 2)
        dve.tensor_copy(self.m12[:, :, 0], self.mv[:, :, 0]).then_inc(self.moments, 1)
        dve.tensor_tensor(self.var[:, :], self.mv[:, :, 0], self.mv[:, :, 0], ALU.mult).then_inc(self.step, 1)
        dve.wait_ge(self.step, CB * NCH + 3)
        dve.tensor_tensor(self.m12[:, :, 1], self.var[:, :], self.mv[:, :, 1], ALU.add).then_inc(self.moments, 1)

    def tensor_join(self, pe, ps, group_mean):
        pe.wait_ge(self.moments, 2)
        pe.matmul(ps, group_mean, self.m12[:, :, :].rearrange("p b s -> p (b s)"),
                  start=True, stop=True).then_inc(self.joined, 1)

    def vector_affine(self, dve, ps):
        base = CB * NCH + 3
        dve.wait_ge(self.joined, 1)
        dve.tensor_copy(self.g12[:, :, :].rearrange("p b s -> p (b s)"), ps).then_inc(self.step, 1)
        dve.wait_ge(self.step, base + 1)
        dve.tensor_tensor(self.std[:, :], self.g12[:, :, 0], self.g12[:, :, 0], ALU.mult).then_inc(self.step, 1)
        dve.wait_ge(self.step, base + 2)
        dve.tensor_tensor(self.var[:, :], self.g12[:, :, 1], self.std[:, :], ALU.subtract).then_inc(self.step, 1)
        dve.wait_ge(self.step, base + 3)
        dve.tensor_scalar(self.var[:, :], self.var[:, :], self.eps, None, ALU.add).then_inc(self.var_ready, 1)
        dve.wait_ge(self.std_ready, 1)
        dve.reciprocal(self.scale[:, :], self.std[:, :]).then_inc(self.step, 1)
        dve.wait_ge(self.step, base + 4)
        dve.scalar_tensor_tensor(out=self.shift[:, :], in0=self.g12[:, :, 0], scalar=-1.0, in1=self.scale[:, :],
                                 op0=ALU.mult, op1=ALU.mult).then_inc(self.ready, 1)

    def scalar_std(self, act):
        act.wait_ge(self.var_ready, 1)
        act.activation(self.std[:, :], self.var[:, :], ACT.Sqrt).then_inc(self.std_ready, 1)

def apart(eng, sem):
    eng.wait_ge(sem, 1)

def padded(t, side):
    return t.rearrange("p (y x) -> p y x", x=side)

def norm_and_split(nc, x_dram, group_mean_dram, XH, XL):
    with ExitStack() as stack:
        n = Names(nc, stack, "norm0")
        x = n.sb("x", [P, CB, PX])
        gm = n.sb("group_mean", [P, P])
        xn = n.sb("xn", [P, 2, CH])
        ps = n.ps("ps", [P, CB * 2])
        gn = GroupNorm(n)
        loads = [n.sem(f"x_loaded{i}") for i in range(2 * CB)]
        gm_loaded = n.sem("gm_loaded")
        borders = n.sem("borders")
        whole = n.sem("whole_ready")
        high = n.sem("high_ready")
        low = n.sem("low_ready")
        half = PX // 2
        with nc.Block() as block:

            @block.sync
            def _(sp):
                sp.dma_start(gm[:, :], group_mean_dram).then_inc(gm_loaded, 16)
                for b in range(CB):
                    for h in range(2):
                        sp.dma_start(x[:, b, h * half:(h + 1) * half],
                                     x_dram[b * P:(b + 1) * P, h * half:(h + 1) * half]).then_inc(loads[2 * b + h], 16)

            @block.gpsimd
            def _(pool):
                for t in (XH, XL):
                    pool.memset(t[:, :, :].bitcast(F32), 0.0).then_inc(borders, 1)

            @block.vector
            def _(dve):
                gn.vector_stats(dve, x, lambda b, c: dve.wait_ge(loads[2 * b + c // (NCH // 2)], 16))
                gn.vector_affine(dve, ps[:, :])
                dve.wait_ge(borders, 2)
                for b in range(CB):
                    for c in range(NCH):
                        i = b * NCH + c
                        dve.wait_ge(whole, i + 1)
                        dve.wait_ge(high, i + 1)
                        y = 2 + c * ROWS
                        dst = padded(XL[:, b, :], PAD5)[:, y:y + ROWS, 2:2 + SIDE]
                        hi = padded(XH[:, b, :], PAD5)[:, y:y + ROWS, 2:2 + SIDE]
                        dve.tensor_tensor(dst, xn[:, i % 2, :].rearrange("p (y x) -> p y x", x=SIDE),
                                          hi.bitcast(F32), ALU.subtract).then_inc(low, 1)

            @block.tensor
            def _(pe):
                pe.wait_ge(gm_loaded, 16)
                gn.tensor_join(pe, ps[:, :], gm[:, :])

            @block.scalar
            def _(act):
                gn.scalar_std(act)
                act.wait_ge(gn.ready, 1)
                act.wait_ge(borders, 2)
                for b in range(CB):
                    for c in range(NCH):
                        i = b * NCH + c
                        if i >= 2:
                            act.wait_ge(low, i - 1)
                        src = x[:, b, c * CH:(c + 1) * CH]
                        act.activation(xn[:, i % 2, :], src, ACT.Identity, scale=gn.scale[:, b:b + 1],
                                       bias=gn.shift[:, b:b + 1]).then_inc(whole, 1)
                        y = 2 + c * ROWS
                        dst = padded(XH[:, b, :], PAD5)[:, y:y + ROWS, 2:2 + SIDE]
                        act.activation(dst, src.rearrange("p (y x) -> p y x", x=SIDE), ACT.Identity,
                                       scale=gn.scale[:, b:b + 1], bias=gn.shift[:, b:b + 1]).then_inc(high, 1)

PIECE = 5
KERNELS = (1, 3, 5)
UNIT_SCALE = 64.0

def conv_qkv(nc, w_dram, wdw_dram, head_sum_dram, dw_dram, parts_dram, XH, XL):
    with ExitStack() as stack:
        n = Names(nc, stack, "conv")
        SLOTS = 3
        WH = n.sb("w_high", [P, SLOTS, 25 * P], F32R)
        WL = n.sb("w_low", [P, SLOTS, 25 * P], F32R)
        raw = n.sb("w_raw", [P, 4, PIECE * P])
        co = n.sb("conv_out", [P, PAD3 * PAD3])
        cov = padded(co[:, :], PAD3)
        acc = n.sb("dw_out", [P, 2, CH])
        wdw = n.sb("wdw", [P, 6, 9])
        head_sum = n.sb("head_sum", [P, P])
        qd = n.sb("qk_in", [P, CB, CH])
        sq = n.sb("squares", [P, CB, CH])
        nrm = n.sb("norms", [P, CB, CH])
        unit = n.sb("unit", [P, CH])
        half = n.sb("halves", [P, CB, 2, CH], F16)
        pc = n.ps("pc", [P, 2, CH])
        pn = n.ps("pn", [P, CB, CH])

        raw_loaded = [n.sem(f"raw_loaded{i}") for i in range(4)]
        consts = n.sem("consts_loaded")
        w_high = n.sem("w_high_ready")
        w_low = n.sem("w_low_ready")
        chunk_done = n.sem("conv_chunk_done")
        moved = n.sem("conv_chunk_moved")
        border = n.sem("border_zeroed")
        tap = n.sem("dw_tap")
        stored = [n.sem(f"dw_stored{i}") for i in range(2)]
        qk_loaded = [n.sem(f"qk_loaded{i}") for i in range(CB)]
        squared = n.sem("squared")
        summed = n.sem("summed")
        rooted = n.sem("rooted")
        nstep = n.sem("norm_step")
        half_stored = [n.sem(f"half_stored{i}") for i in range(CB)]
        STEPS = 5

        blocks = [(k, ob) for k in range(3) for ob in range(CB)]
        units = [(blk, ib) for blk in range(len(blocks)) for ib in range(CB)]
        pieces = []
        last_piece = []
        for u, (blk, ib) in enumerate(units):
            taps = KERNELS[blocks[blk][0]] ** 2
            for t0 in range(0, taps, PIECE):
                pieces.append((u, t0, min(PIECE, taps - t0)))
            last_piece.append(len(pieces))

        def steps(eng, step):
            step(0)
            step(1)
            with eng.Fori(0, NCH // 2 - 1) as i:
                for u in range(2):
                    step(i * 2 + (2 + u), u)

        with nc.Block() as block:

            @block.sync
            def _(sp):
                sp.dma_start(wdw[:, :, :], wdw_dram).then_inc(consts, 16)
                sp.dma_start(head_sum[:, :], head_sum_dram).then_inc(consts, 16)
                for i, (u, t0, nt) in enumerate(pieces):
                    blk, ib = units[u]
                    k, ob = blocks[blk]
                    if i >= 4:
                        sp.wait_ge(w_low, i - 3)
                    sp.dma_start(raw[:, i % 4, 0:nt * P],
                                 w_dram[k][ob, ib, :, t0 * P:(t0 + nt) * P]).then_inc(raw_loaded[i % 4], 16)

            @block.gpsimd
            def _(pool):
                pool.memset(co[:, :], 0.0).then_inc(border, 1)
                for i, (u, t0, nt) in enumerate(pieces):
                    s = u % SLOTS
                    if t0 == 0 and u >= SLOTS:
                        pool.wait_ge(chunk_done, NCH * (units[u - SLOTS][0] + 1))
                    pool.wait_ge(raw_loaded[i % 4], 16 * (i // 4 + 1))
                    w = raw[:, i % 4, 0:nt * P]
                    hi = WH[:, s, t0 * P:(t0 + nt) * P]
                    pool.tensor_copy(hi, w).then_inc(w_high, 1)
                    pool.wait_ge(w_high, i + 1)
                    pool.tensor_tensor(WL[:, s, t0 * P:(t0 + nt) * P], w, hi.bitcast(F32),
                                       ALU.subtract).then_inc(w_low, 1)

            @block.tensor
            def _(pe):
                def conv(blk, c, slot):
                    k, ob = blocks[blk]
                    side = KERNELS[k]
                    off = 2 - side // 2
                    if blk or not isinstance(c, int) or c >= 2:
                        pe.wait_ge(moved, c + (blk * NCH - 1))
                    first = True
                    for ib in range(CB):
                        s = (blk * CB + ib) % SLOTS
                        for t in range(side * side):
                            y, x = off + t // side, off + t % side
                            for w, xs in ((WH, XH), (WH, XL), (WL, XH)):
                                last = ib == CB - 1 and t == side * side - 1 and w is WL
                                mm = pe.matmul(pc[:, slot, :], w[:, s, t * P:(t + 1) * P],
                                               padded(xs[:, ib, :], PAD5)[:, ds(c * ROWS + y, ROWS), x:x + SIDE],
                                               start=first, stop=last)
                                first = False
                    mm.then_inc(chunk_done, 1)

                def head_sums(which, j):
                    for a in range(CB):
                        m = j * CB + (which * NCH * CB + a)
                        pe.wait_ge(squared, m + 1)
                        pe.matmul(pn[:, a, :], head_sum[:, :], sq[:, a, :], start=True, stop=True).then_inc(summed, 1)

                pe.wait_ge(consts, 32)
                for blk, (k, ob) in enumerate(blocks):
                    pe.wait_ge(w_low, last_piece[blk * CB + CB - 1])
                    if blk == 0:
                        for c in range(NCH):
                            conv(blk, c, c % 2)
                        continue
                    with pe.Fori(0, NCH // 2) as c2:
                        for u in range(2):
                            conv(blk, c2 * 2 + u, u)
                            if k == 2:
                                head_sums(ob, c2 * 2 + u)

            @block.scalar
            def _(act):
                def move(blk, c, slot):
                    act.wait_ge(chunk_done, c + (blk * NCH + 1))
                    if blk:
                        act.wait_ge(tap, (c + ((blk - 1) * NCH + 2)) * 9)
                    apart(act, border)
                    act.activation(cov[:, ds(c * ROWS + 1, ROWS), 1:1 + SIDE],
                                   pc[:, slot, :].rearrange("p (y x) -> p y x", x=SIDE),
                                   ACT.Identity).then_inc(moved, 1)

                def store(blk, c, slot):
                    act.wait_ge(tap, (c + (blk * NCH + 1)) * 9)
                    act.dma_start(dw_dram[blk, :, ds(c * CH, CH)], acc[:, slot, :]).then_inc(stored[slot], 16)

                def store_halves(which, j):
                    for a in range(CB):
                        m = j * CB + (which * NCH * CB + a)
                        act.wait_ge(nstep, (m + 1) * STEPS)
                        act.dma_start(parts_dram[which, :, a * P:(a + 1) * P, ds(j * CH, CH)].rearrange("s p n -> p s n"),
                                      half[:, a, :, :]).then_inc(half_stored[a], 16)

                def block_steps(blk, k, ob):
                    def step(c, u=None):
                        slot = c if u is None else u
                        if k == 2:
                            if not isinstance(c, int) or c:
                                store_halves(ob, c - 1)
                            elif ob:
                                store_halves(0, NCH - 1)
                            for a in range(CB):
                                m = c * CB + (ob * NCH * CB + a)
                                if not isinstance(m, int) or m >= CB:
                                    act.wait_ge(nstep, (m - CB + 1) * STEPS)
                                act.dma_start(qd[:, a, :], dw_dram[2 * ob + a, :, ds(c * CH, CH)]).then_inc(qk_loaded[a], 16)
                            for a in range(CB):
                                act.wait_ge(qk_loaded[a], (c + (ob * NCH + 1)) * 16)
                                act.activation(sq[:, a, :], qd[:, a, :], ACT.Square).then_inc(squared, 1)
                        move(blk, c, slot)
                        if k == 2:
                            for a in range(CB):
                                act.wait_ge(summed, c * CB + (ob * NCH * CB + a + 1))
                                act.activation(nrm[:, a, :], pn[:, a, :], ACT.Sqrt).then_inc(rooted, 1)
                        if not isinstance(c, int) or c >= 2:
                            store(blk, c - 2, slot)
                    return step

                act.wait_ge(border, 1)
                for blk, (k, ob) in enumerate(blocks):
                    if k == 2 and ob == 0:
                        for u in range(2):
                            act.wait_ge(stored[u], blk * (NCH // 2) * 16)
                    steps(act, block_steps(blk, k, ob))
                    store(blk, NCH - 2, 0)
                    store(blk, NCH - 1, 1)
                store_halves(1, NCH - 1)
                for u in range(2):
                    act.wait_ge(stored[u], len(blocks) * (NCH // 2) * 16)
                for a in range(CB):
                    act.wait_ge(half_stored[a], CB * NCH * 16)

            @block.vector
            def _(dve):
                def depthwise(blk, c, slot):
                    done = c + blk * NCH
                    last = isinstance(c, int) and c == NCH - 1
                    dve.wait_ge(moved, done + (1 if last else 2))
                    if blk or not isinstance(c, int) or c >= 2:
                        dve.wait_ge(stored[slot], (c - slot + blk * NCH) * 8)
                    out = acc[:, slot, :].rearrange("p (y x) -> p y x", x=SIDE)
                    for t in range(9):
                        src = cov[:, ds(c * ROWS + t // 3, ROWS), t % 3:t % 3 + SIDE]
                        w = wdw[:, blk, t:t + 1]
                        if t == 0:
                            ins = dve.tensor_scalar(out, src, w, None, ALU.mult)
                        else:
                            dve.wait_ge(tap, done * 9 + t)
                            ins = dve.scalar_tensor_tensor(out=out, in0=src, scalar=w, in1=out,
                                                           op0=ALU.mult, op1=ALU.add)
                        ins.then_inc(tap, 1)

                def unit_halves(which, j):
                    for a in range(CB):
                        m = j * CB + (which * NCH * CB + a)
                        dve.wait_ge(rooted, m + 1)
                        dve.tensor_scalar(nrm[:, a, :], nrm[:, a, :], 1e-12, None, ALU.max).then_inc(nstep, 1)
                        dve.wait_ge(nstep, m * STEPS + 1)
                        dve.reciprocal(nrm[:, a, :], nrm[:, a, :]).then_inc(nstep, 1)
                        dve.wait_ge(nstep, m * STEPS + 2)
                        dve.scalar_tensor_tensor(out=unit[:, :], in0=qd[:, a, :], scalar=UNIT_SCALE, in1=nrm[:, a, :],
                                                 op0=ALU.mult, op1=ALU.mult).then_inc(nstep, 1)
                        dve.wait_ge(nstep, m * STEPS + 3)
                        if which or not isinstance(j, int) or j:
                            dve.wait_ge(half_stored[a], (j + which * NCH) * 16)
                        dve.tensor_copy(half[:, a, 0, :], unit[:, :]).then_inc(nstep, 1)
                        dve.wait_ge(nstep, m * STEPS + 4)
                        dve.tensor_tensor(half[:, a, 1, :], unit[:, :], half[:, a, 0, :], ALU.subtract).then_inc(nstep, 1)

                dve.wait_ge(consts, 32)
                for blk, (k, ob) in enumerate(blocks):
                    def step(c, u=None):
                        if k == 2:
                            unit_halves(ob, c)
                        if not isinstance(c, int) or c:
                            depthwise(blk, c - 1, (c - 1) % 2 if u is None else 1 - u)
                    steps(dve, step)
                    depthwise(blk, NCH - 1, 1)

NB = 1024
NNB = PX // NB
NG = HEADS * NNB
SCORE_RANGE = 60.0
MT = PX // P
VW = 3 * HD

def transpose_v(nc, dw_dram, vt_dram, ident_dram):
    with ExitStack() as stack:
        n = Names(nc, stack, "vt")
        v = n.sb("v", [P, CB, PX])
        ident = n.sb("ident", [P, P])
        vt = n.sb("vt", [P, HPB, MT, VW], F32R)
        ps = n.ps("ps", [P, 2, 4, P])
        v_loaded = [n.sem(f"v_loaded{i}") for i in range(CB)]
        ident_loaded = n.sem("ident_loaded")
        ones_set = n.sem("ones_set")
        turned = n.sem("turned")
        high = n.sem("high_ready")
        low = n.sem("low_ready")
        kept = n.sem("kept")
        GR = MT // 4
        with nc.Block() as block:

            @block.sync
            def _(sp):
                sp.dma_start(ident[:, :], ident_dram).then_inc(ident_loaded, 16)
                for b in range(CB):
                    sp.dma_start(v[:, b, :], dw_dram[2 * CB + b, :, :]).then_inc(v_loaded[b], 16)
                for b in range(CB):
                    sp.wait_ge(low, GR * (b + 1))
                    sp.wait_ge(ones_set, 1)
                    for h in range(HPB):
                        sp.dma_start(vt_dram[b * HPB + h, :, :, :].rearrange("p m c -> p (m c)"),
                                     vt[:, h, :, :].bitcast(F32).rearrange("p m c -> p (m c)")).then_inc(kept, 16)
                    sp.wait_ge(kept, 16 * HPB * (b + 1))

            @block.gpsimd
            def _(pool):
                pool.memset(vt[:, :, :, 2 * HD:VW].bitcast(F32), 1.0).then_inc(ones_set, 1)

            @block.tensor
            def _(pe):
                pe.wait_ge(ident_loaded, 16)
                for b in range(CB):
                    pe.wait_ge(v_loaded[b], 16)
                    for g in range(GR):
                        i = b * GR + g
                        if i >= 2:
                            pe.wait_ge(low, i - 1)
                        for j in range(4):
                            t = 4 * g + j
                            mm = pe.transpose(ps[:, i % 2, j, :], v[:, b, t * P:(t + 1) * P], ident[:, :])
                        mm.then_inc(turned, 1)

            def part(b, g, lo):
                return vt[:, :, 4 * g:4 * g + 4, lo * HD:(lo + 1) * HD].rearrange("p h m c -> p m h c")

            @block.scalar
            def _(act):
                for i in range(CB * GR):
                    b, g = divmod(i, GR)
                    if g == 0 and b:
                        act.wait_ge(kept, 16 * HPB * b)
                    act.wait_ge(turned, i + 1)
                    act.activation(part(b, g, 0), ps[:, i % 2, :, :].rearrange("p m (h c) -> p m h c", c=HD),
                                   ACT.Identity).then_inc(high, 1)

            @block.vector
            def _(dve):
                for i in range(CB * GR):
                    b, g = divmod(i, GR)
                    dve.wait_ge(high, i + 1)
                    dve.tensor_tensor(part(b, g, 1), ps[:, i % 2, :, :].rearrange("p m (h c) -> p m h c", c=HD),
                                      part(b, g, 0).bitcast(F32), ALU.subtract).then_inc(low, 1)

def attention(nc, parts_dram, vt_dram, temp_dram, o_dram):
    with ExitStack() as stack:
        n = Names(nc, stack, "att")
        R = 4
        LAG = 3
        qs = n.sb("q_stack", [P, 2, PX], F16)
        ks = n.sb("k_stack", [P, 2, PX], F16)
        vs = [n.sb(f"v_stack{i}", [P, MT, VW], F32R) for i in range(2)]
        e = n.sb("exp", [P, R, NB])
        eh = n.sb("exp_high", [P, R, NB], F32R)
        el = n.sb("exp_low", [P, R, NB], F32R)
        out = n.sb("out", [VW, 2, NB])
        temp = n.sb("temp", [P, HEADS * NNB])
        affine = n.sb("affine", [P, NG, 2])
        scale, shift = affine[:, :, 0], affine[:, :, 1]
        cur = n.sb("affine_now", [P, 2, 2])
        spare = n.sb("spare", [P, 2])
        sc = n.ps("scores", [P, 2, NB])
        pv = n.ps("pv", [P, 2, NB])

        temp_loaded = n.sem("temp_loaded")
        tstep = n.sem("temp_step")
        loaded = [n.sem(f"stack_loaded{i}") for i in range(2)]
        scored = n.sem("scored")
        exped = n.sem("exped")
        high_act = n.sem("exp_high_by_act")
        high_dve = n.sem("exp_high_by_dve")
        low = n.sem("exp_low_ready")
        summed = n.sem("pv_done")
        pv_free = n.sem("pv_free")
        tneg = n.sem("temp_neg")
        cur_ready = n.sem("affine_now_ready")
        stored = [n.sem(f"out_stored{i}") for i in range(2)]
        LOADS = 9
        ON_ACT = [m for m in range(MT - 1) if m % 5 in (1, 3)]

        with nc.Block() as block:

            @block.sync
            def _(sp):
                sp.dma_start(temp[:, :], temp_dram).then_inc(temp_loaded, 16)

                def load(head, s):
                    at = head * HD
                    for i, (a, b) in enumerate(((0, 0), (0, 1), (1, 0), (1, 1))):
                        rows = slice(i * HD, (i + 1) * HD)
                        sp.dma_start(qs[rows, s, :], parts_dram[0, a, ds(at, HD), :]).then_inc(loaded[s], 16)
                        sp.dma_start(ks[rows, s, :], parts_dram[1, b, ds(at, HD), :]).then_inc(loaded[s], 16)
                    sp.dma_start(vs[s][:, :, :].bitcast(F32).rearrange("p m c -> p (m c)"),
                                 vt_dram[ds(head, 1), :, :, :].rearrange("h p m c -> (h p) (m c)")).then_inc(loaded[s], 16)

                load(0, 0)
                load(1, 1)
                with sp.Fori(0, HEADS // 2 - 1) as hp:
                    for s in range(2):
                        sp.wait_ge(summed, (hp * 2 + (s + 1)) * (NNB * MT))
                        load(hp * 2 + (2 + s), s)
                sp.wait_ge(summed, (HEADS - 1) * NNB * MT)
                load(0, 0)
                sp.wait_ge(loaded[0], 16 * LOADS * (HEADS // 2 + 1))

            @block.tensor
            def _(pe):
                def scores(s, n0, mt):
                    for c in range(2):
                        mm = pe.matmul(sc[:, mt % 2, c * CH:(c + 1) * CH], ks[:, s, mt * P:(mt + 1) * P],
                                       qs[:, s, n0 + c * CH:n0 + (c + 1) * CH], start=True, stop=True)
                    mm.then_inc(scored, 1)

                def tiles(g, s, nb, s_next, nb_next, next_loaded=None):
                    slot = nb % 2
                    for mt in range(MT):
                        ahead = mt + LAG
                        if ahead == MT and next_loaded is not None:
                            pe.wait_ge(loaded[s_next], next_loaded)
                        pe.wait_ge(exped, g * MT + (ahead - 1))
                        if ahead < MT:
                            scores(s, nb * NB, ahead)
                        else:
                            scores(s_next, nb_next * NB, ahead - MT)
                        if mt in ON_ACT:
                            pe.wait_ge(high_act, g * len(ON_ACT) + (ON_ACT.index(mt) + 1))
                        else:
                            pe.wait_ge(high_dve, g * (MT - len(ON_ACT)) + (mt + 1 - sum(m < mt for m in ON_ACT)))
                        for part in (eh, el):
                            if part is el:
                                pe.wait_ge(low, g * MT + (mt + 1))
                            for c in range(2):
                                mm = pe.matmul(pv[0:VW, slot, c * CH:(c + 1) * CH], vs[s][:, mt, :],
                                               part[:, mt % R, c * CH:(c + 1) * CH],
                                               start=mt == 0 and part is eh, stop=mt == MT - 1 and part is el)
                        mm.then_inc(summed, 1)

                pe.wait_ge(loaded[0], 16 * LOADS)
                for mt in range(LAG):
                    if mt >= 2:
                        pe.wait_ge(exped, mt - 1)
                    scores(0, 0, mt)
                with pe.Fori(0, HEADS // 2) as hp:
                    for s in range(2):
                        for nb in range(NNB):
                            g = hp * (2 * NNB) + (s * NNB + nb)
                            pe.wait_ge(pv_free, g + 1)
                            if nb < NNB - 1:
                                tiles(g, s, nb, s, nb + 1)
                            else:
                                tiles(g, s, nb, 1 - s, 0, (hp + (1 + s)) * (16 * LOADS))

            @block.scalar
            def _(act):
                def move(g, slot):
                    act.wait_ge(summed, (g + 1) * MT)
                    if not isinstance(g, int) or g >= 2:
                        act.wait_ge(stored[slot], (g - slot) * 8)
                    act.activation(out[:, slot, :], pv[0:VW, slot, :], ACT.Identity).then_inc(pv_free, 1)

                def store(g, slot):
                    act.wait_ge(pv_free, g + 3)
                    act.dma_start(o_dram[ds(g, 1), :, :].rearrange("g c n -> (g c) n"), out[:, slot, :]).then_inc(stored[slot], 16)

                def body(g, slot):
                    act.activation(cur[:, slot, :], affine[:, ds(g, 1), :].rearrange("p g a -> p (g a)"),
                                   ACT.Identity).then_inc(cur_ready, 1)
                    act.wait_ge(cur_ready, g + 1)
                    for mt in range(MT):
                        act.wait_ge(scored, g * MT + (mt + 1))
                        if not isinstance(g, int) or g * MT + mt >= R:
                            act.wait_ge(low, g * MT + (mt + 1 - R))
                        act.activation(e[:, mt % R, :], sc[:, mt % 2, :], ACT.Exp, scale=cur[:, slot, 0:1],
                                       bias=cur[:, slot, 1:2]).then_inc(exped, 1)
                        if mt - 1 in ON_ACT:
                            if not isinstance(g, int) or g * MT + mt - 1 >= R:
                                act.wait_ge(summed, g * MT + (mt - R))
                            act.wait_ge(exped, g * MT + mt)
                            act.activation(eh[:, (mt - 1) % R, :], e[:, (mt - 1) % R, :], ACT.Identity).then_inc(high_act, 1)
                        if not isinstance(g, int) or g:
                            if mt == LAG + 2:
                                move(g - 1, 1 - slot)
                            if mt == LAG + 4:
                                store(g - 1, 1 - slot)

                act.wait_ge(tstep, 4)
                body(0, 0)
                body(1, 1)
                with act.Fori(0, NG // 2 - 1) as i:
                    for s in range(2):
                        body(i * 2 + (2 + s), s)
                act.wait_ge(scored, NG * MT + 1)
                act.wait_ge(low, NG * MT + 1 - R)
                act.activation(e[:, 0, :], sc[:, 0, :], ACT.Exp, scale=cur[:, 0, 0:1], bias=cur[:, 0, 1:2]).then_inc(exped, 1)
                move(NG - 1, 1)
                store(NG - 1, 1)
                for s in range(2):
                    act.wait_ge(stored[s], 16 * (NG // 2))

            @block.vector
            def _(dve):
                dve.wait_ge(temp_loaded, 16)
                dve.tensor_scalar(scale, temp[:, :], 1.0 / (UNIT_SCALE * UNIT_SCALE), None, ALU.mult).then_inc(tstep, 1)
                dve.tensor_scalar(shift, temp[:, :], -1.0, None, ALU.mult).then_inc(tstep, 1)
                dve.wait_ge(tstep, 2)
                dve.tensor_tensor(shift, shift, temp[:, :], ALU.max).then_inc(tstep, 1)
                dve.wait_ge(tstep, 3)
                dve.tensor_scalar(temp[:, :], shift, -1.0, SCORE_RANGE, ALU.mult, ALU.add).then_inc(tneg, 1)
                dve.wait_ge(tneg, 1)
                dve.tensor_scalar(shift, temp[:, :], 0.0, None, ALU.min).then_inc(tstep, 1)
                dve.memset(spare[:, 0:1], 0.0).then_inc(pv_free, 1)
                dve.memset(spare[:, 1:2], 0.0).then_inc(pv_free, 1)

                def body(g):
                    for mt in range(MT):
                        if not isinstance(g, int) or g * MT + mt >= R:
                            dve.wait_ge(summed, g * MT + (mt + 1 - R))
                        if mt in ON_ACT:
                            dve.wait_ge(high_act, g * len(ON_ACT) + (ON_ACT.index(mt) + 1))
                        else:
                            k = mt - sum(m < mt for m in ON_ACT)
                            dve.wait_ge(exped, g * MT + (mt + 1))
                            dve.tensor_copy(eh[:, mt % R, :], e[:, mt % R, :]).then_inc(high_dve, 1)
                            dve.wait_ge(high_dve, g * (MT - len(ON_ACT)) + (k + 1))
                        dve.tensor_tensor(el[:, mt % R, :], e[:, mt % R, :], eh[:, mt % R, :].bitcast(F32),
                                          ALU.subtract).then_inc(low, 1)

                body(0)
                with dve.Fori(0, NG - 1) as i:
                    body(i + 1)

CROP = 48
M1 = CROP * CROP
SEG = M1 // C
NEWTON = 5

def project(nc, x_dram, o_dram, w_dram, X):
    with ExitStack() as stack:
        n = Names(nc, stack, "proj")
        w = n.sb("w", [P, CB, C])
        sums = n.sb("sums", [P, 2, 3, NB])
        o = n.sb("o", [P, 2, CB, NB])
        ps = n.ps("ps", [P, 2, CB, CH])
        x_loaded = n.sem("x_loaded")
        w_loaded = n.sem("w_loaded")
        sums_loaded = [n.sem(f"sums_loaded{i}") for i in range(2)]
        step = n.sem("step")
        projected = n.sem("projected")
        added = n.sem("added")
        with nc.Block() as block:

            @block.sync
            def _(sp):
                sp.dma_start(w[:, :, :], w_dram).then_inc(w_loaded, 16)
                for b in range(CB):
                    sp.dma_start(X[:, b, :], x_dram[b * P:(b + 1) * P, :]).then_inc(x_loaded, 16)
                for i in range(CB * NNB):
                    nb, b = divmod(i, CB)
                    if i >= 2:
                        sp.wait_ge(step, 3 * (i - 1))
                    for h in range(HPB):
                        g = (b * HPB + h) * NNB + nb
                        sp.dma_start(sums[h * HD:(h + 1) * HD, b, :, :],
                                     o_dram[g, :, :].rearrange("(k c) n -> c k n", c=HD)).then_inc(sums_loaded[b], 16)

            @block.vector
            def _(dve):
                def add(c):
                    dve.wait_ge(projected, c + 1)
                    for ob in range(CB):
                        xs = X[:, ob, c * CH:(c + 1) * CH]
                        dve.tensor_tensor(xs, ps[:, c % 2, ob, :], xs, ALU.add).then_inc(added, 1)

                dve.wait_ge(x_loaded, 32)
                for i in range(CB * NNB):
                    nb, b = divmod(i, CB)
                    dve.wait_ge(sums_loaded[b], 16 * HPB * (nb + 1))
                    dve.tensor_tensor(sums[:, b, 0, :], sums[:, b, 0, :], sums[:, b, 1, :], ALU.add).then_inc(step, 1)
                    dve.reciprocal(sums[:, b, 2, :], sums[:, b, 2, :]).then_inc(step, 1)
                    dve.wait_ge(step, 3 * i + 2)
                    if nb >= 2:
                        dve.wait_ge(projected, 2 * (nb - 1))
                    dve.tensor_tensor(o[:, nb % 2, b, :], sums[:, b, 0, :], sums[:, b, 2, :], ALU.mult).then_inc(step, 1)
                    if b == 1 and nb:
                        add(2 * nb - 2)
                        add(2 * nb - 1)
                add(NCH - 2)
                add(NCH - 1)

            @block.tensor
            def _(pe):
                pe.wait_ge(w_loaded, 16)
                for c in range(NCH):
                    nb, h = divmod(c, 2)
                    pe.wait_ge(step, 3 * CB * (nb + 1))
                    if c >= 2:
                        pe.wait_ge(added, 2 * (c - 1))
                    for ob in range(CB):
                        for ib in range(CB):
                            mm = pe.matmul(ps[:, c % 2, ob, :], w[:, ib, ob * P:(ob + 1) * P],
                                           o[:, nb % 2, ib, h * CH:(h + 1) * CH], start=ib == 0, stop=ib == CB - 1)
                    mm.then_inc(projected, 1)

class Count:

    def __init__(self, n, name):
        self.sem, self.value = n.sem(name), 0

    def up(self, ins):
        ins.then_inc(self.sem, 1)
        self.value += 1
        return self.value

def covariance_gate(nc, gm_dram, eye_dram, w1_dram, b1_dram, w2_dram, b2_dram, X):
    with ExitStack() as stack:
        n = Names(nc, stack, "cov")
        gm = n.sb("group_mean", [P, P])
        eye = n.sb("eye", [P, CB, C])
        ones = n.sb("ones", [P, P])
        w = n.sb("w", [P, 2, CB, C])
        bias = n.sb("bias", [P, 2, CB])
        xn = n.sb("xn", [P, CB, PX])
        xc = n.sb("xc", [P, CB, M1])
        rows = n.sb("row_sums", [1, 2, C])
        mats = {k: n.sb(k, [P, CB, C]) for k in ("cov", "A", "Y", "Y2", "Z", "Z2", "ZY", "diag")}
        small = n.sb("small", [P, 16])
        ps_gn = n.ps("ps_gn", [P, CB * 2])
        ps_g = n.ps("ps_g", [P, CB, C])
        ps_r = n.ps("ps_r", [P, C])
        ps_y = n.ps("ps_y", [P, CB, C])
        ps_z = n.ps("ps_z", [P, CB, C])
        ps_s = n.ps("ps_s", [P, 8])
        gn = GroupNorm(n)
        loaded = n.sem("loaded")
        ones_set = n.sem("ones_set")
        crop = n.sem("crop_ready")
        normed = n.sem("xn_ready")
        T = Count(n, "tensor_done")
        V = Count(n, "vector_done")
        A = Count(n, "scalar_done")
        at = {}

        nt = nv = na = 0
        for name in ("sums", "gram", "trace", "Y0") + tuple(f"{m}{i}" for i in range(1, NEWTON - 1) for m in "TYZ") + (
                "TF", "YF", "FC1", "FC2"):
            nt += 1
            at["t", name] = nt
        with nc.Block() as block:

            @block.sync
            def _(sp):
                for t, d in ((gm[:, :], gm_dram), (eye[:, :, :], eye_dram), (w[:, 0], w1_dram), (w[:, 1], w2_dram),
                             (bias[:, 0], b1_dram), (bias[:, 1], b2_dram)):
                    sp.dma_start(t, d).then_inc(loaded, 16)

            @block.gpsimd
            def _(pool):
                pool.memset(ones[:, :], 1.0).then_inc(ones_set, 1)

            @block.vector
            def _(dve):
                gn.vector_stats(dve, X, lambda b, c: None)
                gn.vector_affine(dve, ps_gn[:, :])
                v = dict()

                def made(name, ins):
                    v[name] = at["v", name] = V.up(ins)

                def after(name):
                    dve.wait_ge(V.sem, v[name])

                dve.wait_ge(loaded, 96)
                dve.wait_ge(T.sem, at["t", "sums"])
                made("row", dve.tensor_copy(rows[0:1, 0, :], ps_r[0:1, :]))
                made("nrow", dve.tensor_scalar(rows[0:1, 1, :], ps_r[0:1, :], -1.0 / M1, None, ALU.mult))
                dve.wait_ge(T.sem, at["t", "gram"])
                made("cov", dve.tensor_scalar(mats["cov"][:, :, :], ps_g[:, :, :], 1.0 / M1, None, ALU.mult))
                after("cov")
                made("diag", dve.tensor_tensor(mats["diag"][:, :, :], mats["cov"][:, :, :], eye[:, :, :], ALU.mult))
                after("diag")
                made("diag_sum", dve.reduce_sum(small[:, 0:1], mats["diag"][:, :, :].rearrange("p b c -> p (b c)"), AX.X))
                dve.wait_ge(T.sem, at["t", "trace"])
                made("trace", dve.tensor_copy(small[:, 1:2], ps_s[:, 0:1]))
                after("trace")
                made("inv", dve.reciprocal(small[:, 2:3], small[:, 1:2]))
                after("inv")
                made("A", dve.tensor_scalar(mats["A"][:, :, :], mats["cov"][:, :, :], small[:, 2:3], None, ALU.mult))
                made("eye15", dve.tensor_scalar(mats["diag"][:, :, :], eye[:, :, :], 1.5, None, ALU.mult))
                after("eye15")
                e15 = mats["diag"]
                made("Z0", dve.scalar_tensor_tensor(out=mats["Z"][:, :, :], in0=mats["A"][:, :, :], scalar=-0.5,
                                                    in1=e15[:, :, :], op0=ALU.mult, op1=ALU.add))
                dve.wait_ge(T.sem, at["t", "Y0"])
                made("Y0", dve.tensor_copy(mats["Y"][:, :, :], ps_y[:, :, :]))
                for i in range(1, NEWTON):
                    dve.wait_ge(T.sem, at["t", f"T{i}" if i < NEWTON - 1 else "TF"])
                    made(f"ZY{i}", dve.scalar_tensor_tensor(out=mats["ZY"][:, :, :], in0=ps_y[:, :, :], scalar=-0.5,
                                                            in1=e15[:, :, :], op0=ALU.mult, op1=ALU.add))
                    if i == NEWTON - 1:
                        break
                    dve.wait_ge(T.sem, at["t", f"Y{i}"])
                    made(f"Y{i}", dve.tensor_copy(mats["Y"][:, :, :], ps_z[:, :, :]))
                    dve.wait_ge(T.sem, at["t", f"Z{i}"])
                    made(f"Z{i}", dve.tensor_copy(mats["Z"][:, :, :], ps_g[:, :, :]))
                dve.wait_ge(T.sem, at["t", "YF"])
                made("mean", dve.reduce_sum(small[:, 4:6], ps_z[:, :, :], AX.X))
                after("mean")
                dve.wait_ge(A.sem, 1)
                made("y", dve.tensor_scalar(small[:, 6:8], small[:, 4:6], small[:, 3:4], 1.0 / C, ALU.mult, ALU.mult))
                dve.wait_ge(T.sem, at["t", "FC1"])
                made("h0", dve.tensor_tensor(small[:, 8:10], ps_s[:, 2:4], bias[:, 0, :], ALU.add))
                after("h0")
                made("h", dve.tensor_scalar(small[:, 8:10], small[:, 8:10], 0.0, None, ALU.max))
                dve.wait_ge(T.sem, at["t", "FC2"])
                made("g0", dve.tensor_tensor(small[:, 10:12], ps_s[:, 4:6], bias[:, 1, :], ALU.add))
                dve.wait_ge(A.sem, 2)
                dve.wait_ge(normed, CB)
                for b in range(CB):
                    made(f"x{b}", dve.scalar_tensor_tensor(out=X[:, b, :], in0=xn[:, b, :], scalar=small[:, 12 + b:13 + b],
                                                           in1=X[:, b, :], op0=ALU.mult, op1=ALU.add))

            @block.tensor
            def _(pe):
                def product(name, out, left, right):
                    for m in range(CB):
                        for k in range(CB):
                            mm = pe.matmul(out[:, m, :], left[:, k, m * P:(m + 1) * P], right[:, k, :],
                                           start=k == 0, stop=k == CB - 1)
                    assert T.up(mm) == at["t", name]

                def after(name):
                    pe.wait_ge(V.sem, at["v", name])

                pe.wait_ge(loaded, 96)
                gn.tensor_join(pe, ps_gn[:, :], gm[:, :])
                pe.wait_ge(ones_set, 1)
                pe.wait_ge(crop, CB)
                tiles = [xc[:, b, j::SEG] for b in range(CB) for j in range(SEG)]
                for i, t in enumerate(tiles):
                    mm = pe.matmul(ps_r[0:1, :], ones[:, 0:1], t, start=i == 0, stop=i == len(tiles) - 1)
                T.up(mm)
                for m in range(CB):
                    for i, t in enumerate(tiles):
                        pe.matmul(ps_g[:, m, :], t[:, m * P:(m + 1) * P], t, start=i == 0, stop=False)
                    if m == 0:
                        after("nrow")
                    mm = pe.matmul(ps_g[:, m, :], rows[0:1, 0, m * P:(m + 1) * P], rows[0:1, 1, :], start=False, stop=True)
                T.up(mm)
                after("diag_sum")
                T.up(pe.matmul(ps_s[:, 0:1], ones[:, :], small[:, 0:1], start=True, stop=True))
                after("Z0")
                product("Y0", ps_y, mats["A"], mats["Z"])
                after("Y0")
                for i in range(1, NEWTON - 1):
                    product(f"T{i}", ps_y, mats["Z"], mats["Y"])
                    after(f"ZY{i}")
                    product(f"Y{i}", ps_z, mats["Y"], mats["ZY"])
                    product(f"Z{i}", ps_g, mats["ZY"], mats["Z"])
                    after(f"Z{i}")
                product("TF", ps_y, mats["Z"], mats["Y"])
                after(f"ZY{NEWTON - 1}")
                product("YF", ps_z, mats["Y"], mats["ZY"])
                for layer, (name, src, col) in enumerate((("y", 6, 2), ("h", 8, 4))):
                    after(name)
                    for ob in range(CB):
                        for ib in range(CB):
                            mm = pe.matmul(ps_s[:, col + ob:col + ob + 1], w[:, layer, ib, ob * P:(ob + 1) * P],
                                           small[:, src + ib:src + ib + 1], start=ib == 0, stop=ib == CB - 1)
                    T.up(mm)

            @block.scalar
            def _(act):
                gn.scalar_std(act)
                act.wait_ge(gn.ready, 1)
                lo = (SIDE - CROP) // 2
                for b in range(CB):
                    act.activation(xc[:, b, :].rearrange("p (y x) -> p y x", x=CROP),
                                   padded(X[:, b, :], SIDE)[:, lo:lo + CROP, lo:lo + CROP], ACT.Identity,
                                   scale=gn.scale[:, b:b + 1], bias=gn.shift[:, b:b + 1]).then_inc(crop, 1)
                for b in range(CB):
                    act.activation(xn[:, b, :], X[:, b, :], ACT.Identity, scale=gn.scale[:, b:b + 1],
                                   bias=gn.shift[:, b:b + 1]).then_inc(normed, 1)
                act.wait_ge(V.sem, at["v", "trace"])
                A.up(act.activation(small[:, 3:4], small[:, 1:2], ACT.Sqrt))
                act.wait_ge(V.sem, at["v", "g0"])
                A.up(act.activation(small[:, 12:14], small[:, 10:12], ACT.Sigmoid))

TAPS = 9
TAB = SIDE + 2
TILES = PX // P
OM = 3 * TAPS

def offsets_and_table(nc, gm_dram, ident_dram, ow_dram, ob_dram, base_dram, table_dram, X, IDX, CW):
    with ExitStack() as stack:
        n = Names(nc, stack, "off")
        gm = n.sb("group_mean", [P, P])
        ident = n.sb("ident", [P, P])
        xp = n.sb("x_padded", [P, CB, PAD3 * PAD3])
        xn = n.sb("xn", [P, CB, PX])
        ow = n.sb("offset_w", [P, CB, TAPS * OM])
        obias = n.sb("offset_b", [OM, 1])
        base = n.sb("base", [P, 2, TILES * TAPS])
        om = n.sb("om", [OM, PX])
        omt = n.sb("om_t", [P, TILES, OM])
        zero = n.sb("zero", [P, C])
        xt = n.sb("x_turned", [P, 2, C])
        F = {k: n.sb(k, [P, TILES, TAPS]) for k in ("py", "px", "fy", "fx", "ly", "lx", "hy", "hx", "gy", "gx", "mask")}
        whole = n.sb("whole", [P, 2, TILES * TAPS], I32)
        ps_gn = n.ps("ps_gn", [P, CB * 2])
        ps_o = n.ps("ps_o", [P, 2, CH])
        ps_t = n.ps("ps_t", [P, 2, CH])
        ps_m = n.ps("ps_m", [P, 2, CH])
        gn = GroupNorm(n)
        loaded = n.sem("loaded")
        border = n.sem("border")
        zero_set = n.sem("zero_set")
        normed = n.sem("normed")
        conv = n.sem("om_conv")
        om_ready = n.sem("om_ready")
        om_turned = n.sem("om_turned")
        turned = n.sem("turned")
        xt_ready = n.sem("xt_ready")
        kept = [n.sem(f"kept{i}") for i in range(2)]
        zeroed = n.sem("table_zeroed")
        masked = n.sem("masked")
        V = Count(n, "vector_done")
        corner = table_dram.rearrange("(y x) (q c) -> q y x c", x=TAB, c=C)
        HB = TILES // 2

        with nc.Block() as block:

            @block.sync
            def _(sp):
                for t, d in ((gm[:, :], gm_dram), (ident[:, :], ident_dram), (ow[:, :, :], ow_dram),
                             (obias[:, :], ob_dram), (base[:, :, :], base_dram)):
                    sp.dma_start(t, d).then_inc(loaded, 16)
                with sp.Fori(0, TILES // 2) as i:
                    for u in range(2):
                        sp.wait_ge(xt_ready, i * 2 + (u + 1))
                        for q in range(4):
                            dy, dx = divmod(q, 2)
                            for r in range(2):
                                sp.dma_start(corner[q, ds(i * 4 + (2 * u + r + 1 - dy), 1), 1 - dx:1 - dx + SIDE, :].rearrange("y x c -> (y x) c"),
                                             xt[r * SIDE:(r + 1) * SIDE, u, :]).then_inc(kept[u], 16)
                for u in range(2):
                    sp.wait_ge(kept[u], 16 * 8 * TILES // 2)

            @block.gpsimd
            def _(pool):
                pool.memset(xp[:, :, :], 0.0).then_inc(border, 1)
                pool.memset(zero[:, :], 0.0).then_inc(zero_set, 1)
                pool.wait_ge(zero_set, 1)
                done = 0
                for q in range(4):
                    dy, dx = divmod(q, 2)
                    for line in ({0, TAB - 1} if not dy else {TAB - 2, TAB - 1}):
                        pool.dma_start(corner[q, line, :, :], zero[0:TAB, :]).then_inc(zeroed, 16)
                        done += 16
                    rows = slice(1 - dy, 1 - dy + SIDE)
                    for line in ({0, TAB - 1} if not dx else {TAB - 2, TAB - 1}):
                        pool.dma_start(corner[q, rows, line, :], zero[0:SIDE, :]).then_inc(zeroed, 16)
                        done += 16
                pool.wait_ge(zeroed, done)

            @block.scalar
            def _(act):
                gn.scalar_std(act)
                act.wait_ge(gn.ready, 1)
                act.wait_ge(border, 1)
                for b in range(CB):
                    act.activation(xn[:, b, :], X[:, b, :], ACT.Identity, scale=gn.scale[:, b:b + 1],
                                   bias=gn.shift[:, b:b + 1]).then_inc(normed, 1)
                    act.activation(padded(xp[:, b, :], PAD3)[:, 1:1 + SIDE, 1:1 + SIDE], padded(X[:, b, :], SIDE),
                                   ACT.Identity, scale=gn.scale[:, b:b + 1], bias=gn.shift[:, b:b + 1]).then_inc(normed, 1)
                for t in range(TILES):
                    act.wait_ge(turned, t + 1)
                    if t >= 2:
                        act.wait_ge(kept[t % 2], 16 * 8 * (t // 2))
                    act.activation(xt[:, t % 2, :], ps_t[:, t % 2, 0:C], ACT.Identity).then_inc(xt_ready, 1)
                act.wait_ge(V.sem, 1)
                act.activation(F["mask"][:, :, :], omt[:, :, 2 * TAPS:], ACT.Sigmoid).then_inc(masked, 1)

            @block.tensor
            def _(pe):
                pe.wait_ge(loaded, 16 * 5)
                gn.tensor_join(pe, ps_gn[:, :], gm[:, :])
                pe.wait_ge(normed, 2 * CB)

                def turn(t):
                    if t >= 2:
                        pe.wait_ge(xt_ready, t - 1)
                    for b in range(CB):
                        mm = pe.transpose(ps_t[:, t % 2, b * P:(b + 1) * P],
                                          xn[:, b, t * P:(t + 1) * P], ident[:, :])
                    mm.then_inc(turned, 1)

                for c in range(NCH):
                    if c >= 2:
                        pe.wait_ge(om_ready, c - 1)
                    for b in range(CB):
                        for t in range(TAPS):
                            mm = pe.matmul(ps_o[0:OM, c % 2, :], ow[:, b, t * OM:(t + 1) * OM],
                                           padded(xp[:, b, :], PAD3)[:, c * ROWS + t // 3:c * ROWS + t // 3 + ROWS, t % 3:t % 3 + SIDE],
                                           start=b == 0 and t == 0, stop=b == CB - 1 and t == TAPS - 1)
                    mm.then_inc(conv, 1)
                    for t in range(4 * c, 4 * c + 4):
                        turn(t)
                pe.wait_ge(om_ready, NCH)
                for t in range(TILES):
                    h, i = divmod(t, HB)
                    mm = pe.transpose(ps_m[:, h, i * OM:(i + 1) * OM], om[:, t * P:(t + 1) * P], ident[0:OM, 0:OM])
                mm.then_inc(om_turned, 1)

            @block.vector
            def _(dve):
                gn.vector_stats(dve, X, lambda b, c: None)
                gn.vector_affine(dve, ps_gn[:, :])
                dve.wait_ge(loaded, 16 * 5)
                for c in range(NCH):
                    dve.wait_ge(conv, c + 1)
                    dve.tensor_scalar(om[:, c * CH:(c + 1) * CH], ps_o[0:OM, c % 2, :], obias[:, 0:1], None,
                                      ALU.add).then_inc(om_ready, 1)
                dve.wait_ge(om_turned, 1)

                def made(ins):
                    V.up(ins)
                    dve.wait_ge(V.sem, V.value)

                made(dve.tensor_copy(omt[:, :, :].rearrange("p (h t) m -> p h (t m)", h=2), ps_m[:, :, 0:HB * OM]))
                for k, (pos, frac, hi, fl, gap) in enumerate((("py", "ly", "hy", "fy", "gy"), ("px", "lx", "hx", "fx", "gx"))):
                    bs = base[:, k, :].rearrange("p (t a) -> p t a", a=TAPS)
                    wh = whole[:, k, :].rearrange("p (t a) -> p t a", a=TAPS)
                    made(dve.tensor_tensor(F[pos][:, :, :], omt[:, :, k:2 * TAPS:2], bs, ALU.add))
                    made(dve.tensor_scalar(F[pos][:, :, :], F[pos][:, :, :], 0.0, float(SIDE + 1), ALU.max, ALU.min))
                    made(dve.tensor_copy(wh, F[pos][:, :, :]))
                    made(dve.tensor_copy(F[fl][:, :, :], wh))
                    made(dve.tensor_tensor(F[gap][:, :, :], F[fl][:, :, :], F[pos][:, :, :], ALU.is_gt))
                    made(dve.tensor_tensor(F[fl][:, :, :], F[fl][:, :, :], F[gap][:, :, :], ALU.subtract))
                    made(dve.tensor_tensor(F[frac][:, :, :], F[pos][:, :, :], F[fl][:, :, :], ALU.subtract))
                    made(dve.tensor_scalar(F[hi][:, :, :], F[frac][:, :, :], -1.0, 1.0, ALU.mult, ALU.add))
                made(dve.scalar_tensor_tensor(out=F["gy"][:, :, :], in0=F["fy"][:, :, :], scalar=float(TAB),
                                              in1=F["fx"][:, :, :], op0=ALU.mult, op1=ALU.add))
                made(dve.tensor_copy(IDX[:, :].rearrange("p (t a) -> p t a", a=TAPS), F["gy"][:, :, :]))
                dve.wait_ge(masked, 1)
                for q, (a, b) in enumerate((("hy", "hx"), ("hy", "lx"), ("ly", "hx"), ("ly", "lx"))):
                    made(dve.tensor_tensor(F["gx"][:, :, :], F[a][:, :, :], F[b][:, :, :], ALU.mult))
                    made(dve.tensor_tensor(CW[:, :, q].rearrange("p (t a) -> p t a", a=TAPS), F["gx"][:, :, :],
                                           F["mask"][:, :, :], ALU.mult))

def deform(nc, ident_dram, dw_dram, table_dram, X, IDX, CW):
    with ExitStack() as stack:
        n = Names(nc, stack, "dcn")
        GT = 4
        NGR = TILES // GT
        GS = 6
        ident = n.sb("ident", [P, P])
        w = n.sb("w", [P, CB, TAPS, C])
        cur_idx = n.sb("cur_idx", [P, 2, TAPS], I32)
        g = n.sb("gathered", [P, GS, 4 * C])
        HALF = GS // 2
        tick = n.sb("tick", [P, 2])
        tick_set = n.sem("tick_set")
        ticked = n.sem("ticked")
        val = n.sb("val", [P, 3, C])
        vt = n.sb("val_turned", [P, 2, TAPS, CB, GT * P])
        ps_t = n.ps("ps_t", [P, 2, 2 * CB, P])
        ps_o = n.ps("ps_o", [P, 2, CB, CH])
        loaded = n.sem("loaded")
        idx_ready = n.sem("idx_ready")
        got = [n.sem(f"gathered{i}") for i in range(GS)]
        first = n.sem("first_product")
        step = n.sem("step")
        turned = n.sem("turned")
        kept = n.sem("turned_moved")
        product = n.sem("product")
        added = n.sem("added")

        def groups(eng, body):
            body(0, 0)
            body(1, 1)
            with eng.Fori(0, NGR // 2 - 2) as i:
                for u in range(2):
                    body(i * 2 + (2 + u), u)
            body(NGR - 2, 0)
            body(NGR - 1, 1)

        def static(v):
            return isinstance(v, int)

        with nc.Block() as block:

            @block.sync
            def _(sp):
                sp.dma_start(ident[:, :], ident_dram).then_inc(loaded, 16)
                sp.dma_start(w[:, :, :, :], dw_dram).then_inc(loaded, 16)

            @block.gpsimd
            def _(pool):
                pool.memset(tick[:, :], 0.0).then_inc(tick_set, 1)
                pool.wait_ge(tick_set, 1)

                TICKS = 2 + 2 * TAPS // HALF

                def passed(t2, k, sem, value):
                    if not static(t2):
                        pool.wait_ge(ticked, (t2 - 1) * TICKS + k)
                        pool.wait_ge(sem, value)
                        pool.tensor_tensor(tick[:, 1:2], tick[:, 0:1], tick[:, 0:1], ALU.add).then_inc(ticked, 1)
                    else:
                        pool.wait_ge(sem, value)

                def gathers(t2):
                    for u in range(2):
                        passed(t2, u * (TICKS // 2), idx_ready, t2 * 2 + (u + 1))
                        for k in range(TAPS):
                            i = u * TAPS + k
                            if i % HALF == 0 and (not static(t2) or i >= GS):
                                passed(t2, u * (TICKS // 2) + 1 + k // HALF, step, (t2 * (2 * TAPS) + (i + HALF - GS)) * 3)
                            pool.indirect_dma_start(g[:, i % GS, :], None, table_dram,
                                                    bass.IndirectOffsetOnAxis(ap=cur_idx[:, u, k:k + 1], axis=0)).then_inc(
                                                        got[i % GS], 16)
                gathers(0)
                with pool.Fori(0, TILES // 2 - 1) as t:
                    gathers(t + 1)

            def gather_count(t2, i):
                return (t2 * (2 * TAPS // GS) + (i // GS + 1)) * 16

            @block.scalar
            def _(act):
                def pair(t2, gt, gslot):
                    for u in range(2):
                        for k in range(TAPS):
                            i = u * TAPS + k
                            m = t2 * (2 * TAPS) + i
                            act.wait_ge(got[i % GS], gather_count(t2, i))
                            if not static(t2) or i >= 3:
                                act.wait_ge(turned, m - 2)
                            if not static(t2):
                                apart(act, turned)
                            act.activation(val[:, i % 3, :], g[:, i % GS, 0:C], ACT.Identity,
                                           scale=CW[:, ds(m, 1), 0]).then_inc(first, 1)
                            if i >= 1:
                                move(t2, i - 1, gt, gslot)
                    move(t2, 2 * TAPS - 1, gt, gslot)

                def move(t2, i, gt, gslot):
                    u, k = divmod(i, TAPS)
                    act.wait_ge(turned, t2 * (2 * TAPS) + (i + 1))
                    at = (gt + u) * P
                    act.activation(vt[:, gslot, k, :, at:at + P], ps_t[:, i % 2, 0:CB, :], ACT.Identity).then_inc(kept, 1)

                def group(gr, slot):
                    if not static(gr) or gr >= 2:
                        act.wait_ge(product, gr - 1)
                    for h in range(GT // 2):
                        pair(gr * (GT // 2) + h, 2 * h, slot)

                groups(act, group)

            @block.vector
            def _(dve):
                def put(t2, u):
                    if not static(t2) or t2:
                        dve.wait_ge(got[(u * TAPS + TAPS - 1) % GS],
                                    ((t2 - 1) * (2 * TAPS // GS) + ((u * TAPS + TAPS - 1) // GS + 1)) * 16)
                    dve.tensor_copy(cur_idx[:, u, :], IDX[:, ds(t2 * (2 * TAPS) + u * TAPS, TAPS)]).then_inc(idx_ready, 1)

                def pair(t2, last=False):
                    for i in range(2 * TAPS):
                        if i % TAPS == 0 and i and not last:
                            put(t2 + 1, 0)
                        m = t2 * (2 * TAPS) + i
                        s = i % GS
                        dve.wait_ge(first, m + 1)
                        for q in range(1, 4):
                            if q > 1:
                                dve.wait_ge(step, m * 3 + (q - 1))
                            dve.scalar_tensor_tensor(out=val[:, i % 3, :], in0=g[:, s, q * C:(q + 1) * C],
                                                     scalar=CW[:, ds(m, 1), q], in1=val[:, i % 3, :],
                                                     op0=ALU.mult, op1=ALU.add).then_inc(step, 1)
                    if not last:
                        put(t2 + 1, 1)

                def add(gr, slot):
                    for ob in range(CB):
                        dve.wait_ge(product, gr + 1)
                        xs = X[:, ob, ds(gr * CH, CH)]
                        dve.tensor_tensor(xs, ps_o[:, slot, ob, :], xs, ALU.add).then_inc(added, 1)

                def group(gr, slot):
                    for h in range(GT // 2):
                        t2 = gr * (GT // 2) + h
                        pair(t2, static(gr) and gr == NGR - 1 and h == 1)
                    if not static(gr) or gr:
                        add(gr - 1, 1 - slot)

                for u in range(2):
                    put(0, u)
                groups(dve, group)
                add(NGR - 1, 1)

            @block.tensor
            def _(pe):
                def turn(gr, gt):
                    for k in range(TAPS):
                        i = (gt % 2) * TAPS + k
                        m = gr * (GT * TAPS) + (gt * TAPS + k)
                        pe.wait_ge(step, (m + 1) * 3)
                        if not static(m) or m >= 2:
                            pe.wait_ge(kept, m - 1)
                        for b in range(CB):
                            mm = pe.transpose(ps_t[:, i % 2, b, :], val[:, i % 3, b * P:(b + 1) * P], ident[:, :])
                        mm.then_inc(turned, 1)

                def products(gr, slot, part):
                    ob, b = divmod(part, CB)
                    if part == 0:
                        pe.wait_ge(kept, (gr + 1) * (GT * TAPS))
                        if not static(gr) or gr >= 2:
                            pe.wait_ge(added, (gr - 1) * CB)
                    for k in range(TAPS):
                        mm = pe.matmul(ps_o[:, slot, ob, :], w[:, b, k, ob * P:(ob + 1) * P], vt[:, slot, k, b, :],
                                       start=b == 0 and k == 0, stop=b == CB - 1 and k == TAPS - 1)
                    if part == GT - 1:
                        mm.then_inc(product, 1)

                def group(gr, slot):
                    for gt in range(GT):
                        turn(gr, gt)
                        if not static(gr) or gr:
                            products(gr - 1, 1 - slot, gt)

                pe.wait_ge(loaded, 32)
                groups(pe, group)
                for part in range(GT):
                    products(NGR - 1, 1, part)

LT = 25
UNIT = 16
UNITS = SIDE // UNIT
KEY_SCALE = float(HD) ** -0.5

def qkv_linear(nc, gm_dram, w_dram, b_dram, x3_dram, X, Q, K, V_):
    with ExitStack() as stack:
        n = Names(nc, stack, "lin")
        gm = n.sb("group_mean", [P, P])
        w = n.sb("w", [P, 3, CB, C])
        bias = n.sb("bias", [P, 3, CB])
        xn = n.sb("xn", [P, CB, PX])
        ps_gn = n.ps("ps_gn", [P, CB * 2])
        ps = n.ps("ps", [P, 4, CH])
        gn = GroupNorm(n)
        loaded = n.sem("loaded")
        aside = n.sem("x_aside")
        normed = n.sem("normed")
        done = n.sem("product_done")
        moved = n.sem("moved")
        work = [(c, m, ob) for c in range(NCH) for m in range(3) for ob in range(CB)]
        with nc.Block() as block:

            @block.sync
            def _(sp):
                for t, d in ((gm[:, :], gm_dram), (w[:, :, :, :], w_dram), (bias[:, :, :], b_dram)):
                    sp.dma_start(t, d).then_inc(loaded, 16)
                for b in range(CB):
                    sp.dma_start(x3_dram[:, b, :], X[:, b, :]).then_inc(aside, 16)
                sp.wait_ge(aside, 16 * CB)

            @block.scalar
            def _(act):
                gn.scalar_std(act)
                act.wait_ge(gn.ready, 1)
                for c in range(NCH):
                    for b in range(CB):
                        act.activation(xn[:, b, c * CH:(c + 1) * CH], X[:, b, c * CH:(c + 1) * CH], ACT.Identity,
                                       scale=gn.scale[:, b:b + 1], bias=gn.shift[:, b:b + 1]).then_inc(normed, 1)

            @block.tensor
            def _(pe):
                pe.wait_ge(loaded, 48)
                gn.tensor_join(pe, ps_gn[:, :], gm[:, :])
                for i, (c, m, ob) in enumerate(work):
                    pe.wait_ge(normed, CB * (c + 1))
                    if i >= 4:
                        pe.wait_ge(moved, i - 3)
                    for b in range(CB):
                        mm = pe.matmul(ps[:, i % 4, :], w[:, m, b, ob * P:(ob + 1) * P], xn[:, b, c * CH:(c + 1) * CH],
                                       start=b == 0, stop=b == CB - 1)
                    mm.then_inc(done, 1)

            @block.vector
            def _(dve):
                gn.vector_stats(dve, X, lambda b, c: None)
                gn.vector_affine(dve, ps_gn[:, :])
                dve.wait_ge(loaded, 48)
                for i, (c, m, ob) in enumerate(work):
                    dve.wait_ge(done, i + 1)
                    out = (Q, K, V_)[m][:, ob, c * CH:(c + 1) * CH]
                    dve.tensor_scalar(out, ps[:, i % 4, :], bias[:, m, ob:ob + 1], KEY_SCALE if m == 1 else 1.0,
                                      ALU.add, ALU.mult).then_inc(moved, 1)

def axial_attention(nc, ident_dram, mask_dram, wl_dram, bl_dram, Q, K, V_, L):
    with ExitStack() as stack:
        n = Names(nc, stack, "axial")
        R = 2
        ident = n.sb("ident", [P, P])
        mask = n.sb("mask", [P, 2, HEADS, SIDE])
        wl = n.sb("wl", [P, CB, LT])
        bl = n.sb("bl", [P, CB])
        turned_v = n.sb("turned_v", [P, TILES, P])
        v1 = n.sb("v1", [P, PX])
        s = n.sb("s", [P, R, CH])
        e = n.sb("e", [P, R, CH])
        pr = n.sb("prob", [P, R, CH])
        pt = n.sb("prob_turned", [P, R, CH])
        mx = n.sb("max", [P, R, 8])
        sm = n.sb("sum", [P, R, 8])
        ps_s = n.ps("ps_s", [P, HPB, CH])
        ps_t = n.ps("ps_t", [P, 2, CH])
        ps_v = n.ps("ps_v", [P, 2, CH])

        loaded = n.sem("loaded")
        scored = n.sem("scored")
        shifted = n.sem("dve_softmax")
        exped = n.sem("exped")
        probs = n.sem("probs")
        turned = n.sem("turned")
        moved = n.sem("moved")
        v_turned = n.sem("v_turned")
        v_moved = n.sem("v_moved")
        product = n.sem("product")
        line = n.sem("lines_moved")
        added = n.sem("lines_added")
        lepe = n.sem("lepe")

        passes = [(b, d) for b in range(CB) for d in range(2)]
        items = [(p, u, j) for p in range(len(passes)) for u in range(UNITS) for j in range(HPB)]
        NI = UNITS * HPB

        def group_line(u, g, r):
            return u * UNIT + 4 * (g // 2) + 2 * r + g % 2

        taps = [(b, c, t) for b in range(CB) for c in range(NCH) for t in [LT // 2] + [t for t in range(LT) if t != LT // 2]]
        per_item = -(-len(taps) // (len(items) - 2 * NI // 2))

        with nc.Block() as block:

            @block.sync
            def _(sp):
                for t, d in ((ident[:, :], ident_dram), (mask[:, :, :, :], mask_dram), (wl[:, :, :], wl_dram),
                             (bl[:, :], bl_dram)):
                    sp.dma_start(t, d).then_inc(loaded, 16)

            @block.tensor
            def _(pe):
                def scores(i):
                    p, u, j = items[i]
                    b, d = passes[p]
                    if i >= HPB:
                        pe.wait_ge(shifted, 5 * (i - HPB) + 1)
                    hd = slice(j * HD, (j + 1) * HD)
                    for g in range(8):
                        for r in range(2):
                            at = group_line(u, g, r)
                            px = slice(at * SIDE, (at + 1) * SIDE) if d == 0 else slice(at, PX, SIDE)
                            mm = pe.matmul(ps_s[r * SIDE:(r + 1) * SIDE, j, g * SIDE:(g + 1) * SIDE],
                                           Q[hd, b, px], K[hd, b, px], start=True, stop=True)
                    mm.then_inc(scored, 1)

                def turn_v(p):
                    b, d = passes[p]
                    src = V_[:, b, :] if d == 0 else v1[:, :]
                    if d == 1:
                        pe.wait_ge(line, 2 * UNITS * (b + 1))
                    for g in range(TILES // 4):
                        k = p * (TILES // 4) + g
                        pe.wait_ge(moved, p * NI) if g == 0 and p else None
                        if g >= 2:
                            pe.wait_ge(v_moved, k - 1)
                        for t in range(4):
                            mm = pe.transpose(ps_t[:, g % 2, t * P:(t + 1) * P],
                                              src[:, (4 * g + t) * P:(4 * g + t + 1) * P], ident[:, :])
                        mm.then_inc(v_turned, 1)
                    pe.wait_ge(v_moved, (p + 1) * (TILES // 4))

                def turn(i):
                    pe.wait_ge(probs, i + 1)
                    if i >= 2:
                        pe.wait_ge(moved, i - 1)
                    for t in range(4):
                        mm = pe.transpose(ps_t[:, i % 2, t * P:(t + 1) * P], pr[:, i % R, t * P:(t + 1) * P], ident[:, :])
                    mm.then_inc(turned, 1)

                def values(i):
                    p, u, j = items[i]
                    b, d = passes[p]
                    pe.wait_ge(moved, i + 1)
                    if j == 0:
                        units = p * UNITS + u
                        rows = sum(1 for q in range(units) if passes[q // UNITS][1] == 0)
                        if rows:
                            pe.wait_ge(line, 2 * rows)
                        if units - rows:
                            pe.wait_ge(added, 2 * (units - rows))
                    for g in range(8):
                        for r in range(2):
                            at = group_line(u, g, r)
                            k = slice((at % 2) * SIDE, (at % 2 + 1) * SIDE)
                            slot = (at % UNIT) // 2
                            mm = pe.matmul(ps_v[j * HD:(j + 1) * HD, at % 2, slot * SIDE:(slot + 1) * SIDE],
                                           turned_v[k, at // 2, j * HD:(j + 1) * HD],
                                           pt[k, i % R, (g // 2) * P + r * SIDE:(g // 2) * P + (r + 1) * SIDE],
                                           start=True, stop=True)
                    mm.then_inc(product, 1)

                pe.wait_ge(loaded, 64)
                for p in range(len(passes)):
                    if passes[p][1]:
                        turn_v(p)
                        scores(p * NI)
                        scores(p * NI + 1)
                    else:
                        scores(p * NI)
                        scores(p * NI + 1)
                        turn_v(p)
                    for i in range(p * NI, (p + 1) * NI):
                        if i + 2 < (p + 1) * NI:
                            scores(i + 2)
                        turn(i)
                        if i > p * NI:
                            values(i - 1)
                    values((p + 1) * NI - 1)

            @block.scalar
            def _(act):
                def exp(i):
                    act.wait_ge(shifted, 5 * i + 3)
                    if i >= R:
                        act.wait_ge(probs, i - R + 1)
                    act.activation(e[:, i % R, :], s[:, i % R, :], ACT.Exp).then_inc(exped, 1)

                def move(i):
                    act.wait_ge(turned, i + 1)
                    if i >= R:
                        act.wait_ge(product, i - R + 1)
                    act.activation(pt[:, i % R, :], ps_t[:, i % 2, :], ACT.Identity).then_inc(moved, 1)

                def lines(i):
                    p, u, j = items[i]
                    act.wait_ge(product, i + 1)
                    for par in range(2):
                        dst = v1[:, :].rearrange("p (x y) -> p y x", y=SIDE)[:, u * UNIT + par:(u + 1) * UNIT:2, :]
                        act.activation(dst, ps_v[:, par, :].rearrange("p (y x) -> p y x", x=SIDE), ACT.Identity).then_inc(line, 1)

                for p in range(len(passes)):
                    b, d = passes[p]
                    if p:
                        act.wait_ge(product, p * NI)
                    for g in range(TILES // 4):
                        act.wait_ge(v_turned, p * (TILES // 4) + g + 1)
                        act.activation(turned_v[:, 4 * g:4 * g + 4, :].rearrange("p t c -> p (t c)"), ps_t[:, g % 2, :],
                                       ACT.Identity).then_inc(v_moved, 1)
                    for i in range(p * NI, (p + 1) * NI):
                        exp(i)
                        if i > p * NI:
                            move(i - 1)
                            if items[i - 1][2] == 0 and d == 0 and i - 1 > p * NI:
                                lines(i - 2)
                    move((p + 1) * NI - 1)
                    if d == 0:
                        lines((p + 1) * NI - 1)

            @block.gpsimd
            def _(pool):
                for i in range(len(items)):
                    pool.wait_ge(shifted, 5 * i + 5)
                    if i >= R:
                        pool.wait_ge(turned, i - R + 1)
                    pool.tensor_tensor(pr[:, i % R, :].rearrange("p (g k) -> p g k", k=SIDE),
                                       e[:, i % R, :].rearrange("p (g k) -> p g k", k=SIDE),
                                       sm[:, i % R, :].unsqueeze(2).to_broadcast([P, 8, SIDE]), ALU.mult).then_inc(probs, 1)

            @block.vector
            def _(dve):
                left = list(taps)
                count = [0]

                def local(k):
                    for _ in range(k):
                        if not left:
                            return
                        b, c, t = left.pop(0)
                        dy, dx = t // 5 - 2, t % 5 - 2
                        y0, y1 = max(c * ROWS, -dy), min((c + 1) * ROWS, SIDE - dy)
                        x0, x1 = max(0, -dx), min(SIDE, SIDE - dx)
                        out = padded(L[:, b, :], SIDE)[:, y0:y1, x0:x1]
                        src = padded(V_[:, b, :], SIDE)[:, y0 + dy:y1 + dy, x0 + dx:x1 + dx]
                        if t == LT // 2:
                            ins = dve.tensor_scalar(out, src, wl[:, b, t:t + 1], bl[:, b:b + 1], ALU.mult, ALU.add)
                        else:
                            dve.wait_ge(lepe, count[0])
                            ins = dve.scalar_tensor_tensor(out=out, in0=src, scalar=wl[:, b, t:t + 1], in1=out,
                                                           op0=ALU.mult, op1=ALU.add)
                        ins.then_inc(lepe, 1)
                        count[0] += 1

                def first(i):
                    p, u, j = items[i]
                    b, d = passes[p]
                    sv = s[:, i % R, :].rearrange("p (g k) -> p g k", k=SIDE)
                    dve.wait_ge(scored, i + 1)
                    if i >= R:
                        dve.wait_ge(exped, i - R + 1)
                    dve.tensor_tensor(sv, ps_s[:, j, :].rearrange("p (g k) -> p g k", k=SIDE),
                                      mask[:, d, b * HPB + j, :].unsqueeze(1).to_broadcast([P, 8, SIDE]), ALU.add).then_inc(shifted, 1)
                    dve.wait_ge(shifted, 5 * i + 1)
                    dve.reduce_max(mx[:, i % R, :], sv, AX.X).then_inc(shifted, 1)
                    dve.wait_ge(shifted, 5 * i + 2)
                    dve.tensor_tensor(sv, sv, mx[:, i % R, :].unsqueeze(2).to_broadcast([P, 8, SIDE]), ALU.subtract).then_inc(shifted, 1)

                def second(i):
                    dve.wait_ge(exped, i + 1)
                    if i >= R:
                        dve.wait_ge(probs, i - R + 1)
                    dve.reduce_sum(sm[:, i % R, :], e[:, i % R, :].rearrange("p (g k) -> p g k", k=SIDE), AX.X).then_inc(shifted, 1)
                    dve.wait_ge(shifted, 5 * i + 4)
                    dve.reciprocal(sm[:, i % R, :], sm[:, i % R, :]).then_inc(shifted, 1)

                def add_lines(i):
                    p, u, j = items[i]
                    b, d = passes[p]
                    while left and left[0][0] <= b:
                        local(1)
                    dve.wait_ge(lepe, count[0])
                    dve.wait_ge(product, i + 1)
                    for par in range(2):
                        dst = L[:, b, :].rearrange("p (y x) -> p x y", x=SIDE)[:, u * UNIT + par:(u + 1) * UNIT:2, :]
                        dve.tensor_tensor(dst, ps_v[:, par, :].rearrange("p (x y) -> p x y", y=SIDE), dst, ALU.add).then_inc(added, 1)

                dve.wait_ge(loaded, 64)
                for p in range(len(passes)):
                    b, d = passes[p]
                    for i in range(p * NI, (p + 1) * NI):
                        first(i)
                        local(per_item)
                        second(i)
                        if d == 1 and i - p * NI >= HPB and (i - p * NI) % HPB == 1:
                            add_lines(i - 2)
                    if d == 1:
                        add_lines((p + 1) * NI - 1)

def output(nc, w_dram, b_dram, x3_dram, out_dram, L):
    with ExitStack() as stack:
        n = Names(nc, stack, "out")
        w = n.sb("w", [P, CB, C])
        bias = n.sb("bias", [P, CB])
        x = n.sb("x", [P, CB, PX])
        y = n.sb("y", [P, CB, PX])
        ps = n.ps("ps", [P, 4, CH])
        loaded = n.sem("loaded")
        done = n.sem("product_done")
        ready = n.sem("ready")
        stored = n.sem("stored")
        work = [(c, ob) for c in range(NCH) for ob in range(CB)]
        with nc.Block() as block:

            @block.sync
            def _(sp):
                sp.dma_start(w[:, :, :], w_dram).then_inc(loaded, 16)
                sp.dma_start(bias[:, :], b_dram).then_inc(loaded, 16)
                sp.dma_start(x[:, :, :], x3_dram).then_inc(loaded, 16)
                for c in range(0, NCH, 2):
                    sp.wait_ge(ready, 2 * (c + 2))
                    sp.dma_start(out_dram.rearrange("(b p) n -> p b n", p=P)[:, :, c * CH:(c + 2) * CH],
                                 y[:, :, c * CH:(c + 2) * CH]).then_inc(stored, 16)
                sp.wait_ge(stored, 16 * (NCH // 2))

            @block.tensor
            def _(pe):
                pe.wait_ge(loaded, 48)
                for i, (c, ob) in enumerate(work):
                    if i >= 4:
                        pe.wait_ge(ready, i - 3)
                    for b in range(CB):
                        mm = pe.matmul(ps[:, i % 4, :], w[:, b, ob * P:(ob + 1) * P], L[:, b, c * CH:(c + 1) * CH],
                                       start=b == 0, stop=b == CB - 1)
                    mm.then_inc(done, 1)

            @block.vector
            def _(dve):
                dve.wait_ge(loaded, 48)
                for i, (c, ob) in enumerate(work):
                    dve.wait_ge(done, i + 1)
                    at = slice(c * CH, (c + 1) * CH)
                    dve.scalar_tensor_tensor(out=y[:, ob, at], in0=ps[:, i % 4, :], scalar=bias[:, ob:ob + 1],
                                             in1=x[:, ob, at], op0=ALU.add, op1=ALU.add).then_inc(ready, 1)

def conv_preact_kernel(nc, ins, out):
    dw = nc.dram_tensor("depthwise_out", (3 * CB, P, PX), F32, kind="Internal").ap()
    parts = nc.dram_tensor("unit_parts", (2, 2, C, PX), F16, kind="Internal").ap()
    vt = nc.dram_tensor("v_turned", (HEADS, P, MT, VW), F32, kind="Internal").ap()
    sums = nc.dram_tensor("attention_sums", (NG, VW, NB), F32, kind="Internal").ap()
    table = nc.dram_tensor("corner_table", (TAB * TAB, 4 * C), F32, kind="Internal").ap()
    x3 = nc.dram_tensor("image3", (P, CB, PX), F32, kind="Internal").ap()

    with ExitStack() as stack:
        n = Names(nc, stack, "padded")
        XH = n.sb("x_high", [P, CB, PAD5 * PAD5], F32R)
        XL = n.sb("x_low", [P, CB, PAD5 * PAD5], F32R)
        norm_and_split(nc, ins["x"], ins["group_mean"], XH, XL)
        conv_qkv(nc, [ins["w_q"], ins["w_k"], ins["w_v"]], ins["w_depthwise"], ins["head_sum"], dw, parts, XH, XL)
    transpose_v(nc, dw, vt, ins["identity"])
    attention(nc, parts, vt, ins["temperature"], sums)
    with ExitStack() as stack:
        n = Names(nc, stack, "image")
        X = n.sb("x", [P, CB, PX])
        project(nc, ins["x"], sums, ins["w_project"], X)
        covariance_gate(nc, ins["group_mean"], ins["eye"], ins["w_gate1"], ins["b_gate1"], ins["w_gate2"],
                        ins["b_gate2"], X)
        with ExitStack() as inner:
            n = Names(nc, inner, "corners")
            IDX = n.sb("index", [P, TILES * TAPS], I32)
            CW = n.sb("weight", [P, TILES * TAPS, 4])
            offsets_and_table(nc, ins["group_mean"], ins["identity"], ins["w_offset"], ins["b_offset"],
                              ins["positions"], table, X, IDX, CW)
            deform(nc, ins["identity"], ins["w_deform"], table, X, IDX, CW)
        with ExitStack() as inner:
            n = Names(nc, inner, "axial_in")
            Q = n.sb("q", [P, CB, PX])
            K = n.sb("k", [P, CB, PX])
            V = n.sb("v", [P, CB, PX])
            qkv_linear(nc, ins["group_mean"], ins["w_linear"], ins["b_linear"], x3, X, Q, K, V)
            axial_attention(nc, ins["identity"], ins["masks"], ins["w_local"], ins["b_local"], Q, K, V, X)
        output(nc, ins["w_out"], ins["b_out"], x3, out, X)

def _laid_out(a):
    def conv(w):
        taps = w.shape[2] * w.shape[3]
        return w.reshape(CB, P, CB, P, taps).transpose(0, 2, 3, 4, 1).reshape(CB, CB, P, taps * P)

    def linear(w):
        return w.reshape(CB, P, C).transpose(1, 0, 2)

    def channel(v):
        return v.reshape(CB, P).T

    tile, part, tap = np.meshgrid(np.arange(TILES), np.arange(P), np.arange(TAPS))
    positions = np.stack([2 * tile + part // SIDE + tap // 3, part % SIDE + tap % 3], 1)
    masks = np.stack([a["L3_conv_mask_w"], a["L3_conv_mask_h"]], 0).transpose(2, 0, 1, 3)
    ins = {
        "x": a["x"].reshape(PX, C).T,
        "group_mean": np.kron(np.eye(P // GROUP), np.full((GROUP, GROUP), 1.0 / GROUP)).astype(np.float32),
        "head_sum": np.kron(np.eye(HPB), np.ones((HD, HD))).astype(np.float32),
        "identity": np.eye(P, dtype=np.float32),
        "eye": linear(np.eye(C, dtype=np.float32)),
        "positions": positions.reshape(P, 2, TILES * TAPS).astype(np.float32),
        "w_q": conv(a["L0_conv_W1"]), "w_k": conv(a["L0_conv_W3"]), "w_v": conv(a["L0_conv_W5"]),
        "w_depthwise": a["L0_conv_Wdw"].reshape(3 * CB, P, 9).transpose(1, 0, 2),
        "temperature": np.broadcast_to(np.repeat(a["L0_conv_temperature"].reshape(HEADS), NNB)[None], (P, NG)),
        "w_project": linear(a["L0_conv_Wproj"][:, :, 0, 0].T),
        "w_gate1": linear(a["L1_conv_w1"][1, 1]), "b_gate1": channel(a["L1_conv_b1"]),
        "w_gate2": linear(a["L1_conv_w2"][1, 1]), "b_gate2": channel(a["L1_conv_b2"]),
        "w_offset": a["L2_conv_offset_w"].reshape(TAPS, CB, P, OM).transpose(2, 1, 0, 3).reshape(P, CB, TAPS * OM),
        "b_offset": a["L2_conv_offset_b"].reshape(OM, 1),
        "w_deform": a["L2_conv_dcn_weight"].reshape(C, CB, P, TAPS).transpose(2, 1, 3, 0),
        "w_linear": np.stack([linear(a["L3_conv_" + k].T) for k in ("Wq", "Wk", "Wv")], 1),
        "b_linear": np.stack([channel(a["L3_conv_" + k]) for k in ("bq", "bk", "bv")], 1),
        "masks": np.concatenate([masks, masks], 0),
        "w_local": a["L3_conv_Wlepe"].reshape(LT, CB, P).transpose(2, 1, 0), "b_local": channel(a["L3_conv_blepe"]),
        "w_out": linear(a["L3_conv_Wo"].T), "b_out": channel(a["L3_conv_bo"]),
    }
    return {k: np.ascontiguousarray(v) for k, v in ins.items()}

def kernel(**inputs):
    from concourse import bacc
    from concourse.bass_utils import run_bass_kernel_spmd

    nc = bacc.Bacc("TRN2", target_bir_lowering=False, num_devices=1)
    arrays = _laid_out({k: np.asarray(v) for k, v in inputs.items()})
    ins = {k: nc.dram_tensor(f"in_{k}", v.shape, mybir.dt.from_np(v.dtype), kind="ExternalInput").ap()
           for k, v in arrays.items()}
    out = nc.dram_tensor("out", (C, PX), F32, kind="ExternalOutput").ap()
    conv_preact_kernel(nc, ins, out)
    result = run_bass_kernel_spmd(nc, [{f"in_{k}": v for k, v in arrays.items()}], core_ids=[0])
    return result.results[0]["out"].T.reshape(1, SIDE, SIDE, C)
```

```python
import numpy as np
import concourse.bass as bass
from concourse import mybir
from contextlib import ExitStack

F32, F32R, F16 = mybir.dt.float32, mybir.dt.float32r, mybir.dt.float16
I32 = mybir.dt.int32
ALU = mybir.AluOpType
ACT = mybir.ActivationFunctionType
AX = mybir.AxisListType
ds = bass.ds

P = 128
SIDE = 64
PX = SIDE * SIDE
C = 256
CB = C // P
GROUP = 8
CH = 512
ROWS = CH // SIDE
NCH = PX // CH
HEADS, HD = 8, 32
HPB = P // HD
PAD5 = SIDE + 4
PAD3 = SIDE + 2

class Names:

    def __init__(self, nc, stack, stage):
        self.nc, self.stack, self.stage = nc, stack, stage

    def sb(self, name, shape, dt=F32):
        return self.stack.enter_context(self.nc.sbuf_tensor(f"{self.stage}_{name}", shape, dt))

    def ps(self, name, shape, dt=F32):
        return self.stack.enter_context(self.nc.psum_tensor(f"{self.stage}_{name}", shape, dt))

    def sem(self, name):
        return self.stack.enter_context(self.nc.semaphore(f"{self.stage}_{name}"))

class GroupNorm:

    def __init__(self, n, eps=1e-5):
        self.eps = eps
        self.stats = n.sb("gn_stats", [P, CB, NCH, 6])
        self.mv = n.sb("gn_mv", [P, CB, 2])
        self.m12 = n.sb("gn_m12", [P, CB, 2])
        self.g12 = n.sb("gn_g12", [P, CB, 2])
        self.var = n.sb("gn_var", [P, CB])
        self.std = n.sb("gn_std", [P, CB])
        self.scale = n.sb("gn_scale", [P, CB])
        self.shift = n.sb("gn_shift", [P, CB])
        self.step = n.sem("gn_step")
        self.moments = n.sem("gn_moments")
        self.joined = n.sem("gn_joined")
        self.var_ready = n.sem("gn_var_ready")
        self.std_ready = n.sem("gn_std_ready")
        self.ready = n.sem("gn_ready")

        self.steps = 0

    def up(self, ins):
        ins.then_inc(self.step, 1)
        self.steps += 1

    def chunk_stats(self, dve, x, b, c):
        self.up(dve.bn_stats(self.stats[:, b, c, :], x[:, b, c * CH:(c + 1) * CH]))

    def channel_moments(self, dve):
        dve.wait_ge(self.step, self.steps)
        for b in range(CB):
            self.up(dve.bn_aggr(self.mv[:, b, :], self.stats[:, b, :, :].rearrange("p c s -> p (c s)")))

    def moments_of_affine(self, dve, other, scale, shift):
        self.up(dve.tensor_tensor(self.mv[:, :, 0], other.mv[:, :, 0], scale, ALU.mult))
        self.up(dve.tensor_tensor(self.mv[:, :, 1], other.mv[:, :, 1], scale, ALU.mult))
        dve.wait_ge(self.step, self.steps)
        self.up(dve.tensor_tensor(self.mv[:, :, 0], self.mv[:, :, 0], shift, ALU.add))
        self.up(dve.tensor_tensor(self.mv[:, :, 1], self.mv[:, :, 1], scale, ALU.mult))

    def vector_moments(self, dve):
        dve.wait_ge(self.step, self.steps)
        dve.tensor_copy(self.m12[:, :, 0], self.mv[:, :, 0]).then_inc(self.moments, 1)
        self.up(dve.tensor_tensor(self.var[:, :], self.mv[:, :, 0], self.mv[:, :, 0], ALU.mult))
        dve.wait_ge(self.step, self.steps)
        dve.tensor_tensor(self.m12[:, :, 1], self.var[:, :], self.mv[:, :, 1], ALU.add).then_inc(self.moments, 1)

    def tensor_join(self, pe, ps, group_mean):
        pe.wait_ge(self.moments, 2)
        pe.matmul(ps, group_mean, self.m12[:, :, :].rearrange("p b s -> p (b s)"),
                  start=True, stop=True).then_inc(self.joined, 1)

    def vector_affine(self, dve, ps):
        dve.wait_ge(self.joined, 1)
        self.up(dve.tensor_copy(self.g12[:, :, :].rearrange("p b s -> p (b s)"), ps))
        dve.wait_ge(self.step, self.steps)
        self.up(dve.tensor_tensor(self.std[:, :], self.g12[:, :, 0], self.g12[:, :, 0], ALU.mult))
        dve.wait_ge(self.step, self.steps)
        self.up(dve.tensor_tensor(self.var[:, :], self.g12[:, :, 1], self.std[:, :], ALU.subtract))
        dve.wait_ge(self.step, self.steps)
        dve.tensor_scalar(self.var[:, :], self.var[:, :], self.eps, None, ALU.add).then_inc(self.var_ready, 1)
        dve.wait_ge(self.std_ready, 1)
        self.up(dve.reciprocal(self.scale[:, :], self.std[:, :]))
        dve.wait_ge(self.step, self.steps)
        dve.scalar_tensor_tensor(out=self.shift[:, :], in0=self.g12[:, :, 0], scalar=-1.0, in1=self.scale[:, :],
                                 op0=ALU.mult, op1=ALU.mult).then_inc(self.ready, 1)

    def scalar_std(self, act):
        act.wait_ge(self.var_ready, 1)
        act.activation(self.std[:, :], self.var[:, :], ACT.Sqrt).then_inc(self.std_ready, 1)

def apart(eng, sem):
    eng.wait_ge(sem, 1)

def padded(t, side):
    return t.rearrange("p (y x) -> p y x", x=side)

def norm_and_split(nc, x_dram, group_mean_dram, XH, XL):
    with ExitStack() as stack:
        n = Names(nc, stack, "norm0")
        x = n.sb("x", [P, CB, PX])
        gm = n.sb("group_mean", [P, P])
        xn = n.sb("xn", [P, 2, CH])
        ps = n.ps("ps", [P, CB * 2])
        gn = GroupNorm(n)
        loads = [n.sem(f"x_loaded{i}") for i in range(2 * CB)]
        gm_loaded = n.sem("gm_loaded")
        borders = n.sem("borders")
        whole = n.sem("whole_ready")
        high = n.sem("high_ready")
        low = n.sem("low_ready")
        half = PX // 2
        with nc.Block() as block:

            @block.sync
            def _(sp):
                sp.dma_start(gm[:, :], group_mean_dram).then_inc(gm_loaded, 16)
                for b in range(CB):
                    for h in range(2):
                        sp.dma_start(x[:, b, h * half:(h + 1) * half],
                                     x_dram[b * P:(b + 1) * P, h * half:(h + 1) * half]).then_inc(loads[2 * b + h], 16)

            @block.gpsimd
            def _(pool):
                for t in (XH, XL):
                    pool.memset(t[:, :, :].bitcast(F32), 0.0).then_inc(borders, 1)

            @block.vector
            def _(dve):
                for b in range(CB):
                    for c in range(NCH):
                        dve.wait_ge(loads[2 * b + c // (NCH // 2)], 16)
                        gn.chunk_stats(dve, x, b, c)
                gn.channel_moments(dve)
                gn.vector_moments(dve)
                gn.vector_affine(dve, ps[:, :])
                dve.wait_ge(borders, 2)
                pieces = [(b, c) for b in range(CB) for c in range(NCH)]

                def make_whole(i):
                    b, c = pieces[i]
                    if i >= 2:
                        dve.wait_ge(low, i - 1)
                    dve.tensor_scalar(xn[:, i % 2, :], x[:, b, c * CH:(c + 1) * CH], gn.scale[:, b:b + 1],
                                      gn.shift[:, b:b + 1], ALU.mult, ALU.add).then_inc(whole, 1)

                dve.wait_ge(gn.ready, 1)
                make_whole(0)
                for i, (b, c) in enumerate(pieces):
                    if i + 1 < len(pieces):
                        make_whole(i + 1)
                    dve.wait_ge(whole, i + 1)
                    dve.wait_ge(high, i + 1)
                    y = 2 + c * ROWS
                    dst = padded(XL[:, b, :], PAD5)[:, y:y + ROWS, 2:2 + SIDE]
                    hi = padded(XH[:, b, :], PAD5)[:, y:y + ROWS, 2:2 + SIDE]
                    dve.tensor_tensor(dst, xn[:, i % 2, :].rearrange("p (y x) -> p y x", x=SIDE),
                                      hi.bitcast(F32), ALU.subtract).then_inc(low, 1)

            @block.tensor
            def _(pe):
                pe.wait_ge(gm_loaded, 16)
                gn.tensor_join(pe, ps[:, :], gm[:, :])

            @block.scalar
            def _(act):
                gn.scalar_std(act)
                act.wait_ge(gn.ready, 1)
                act.wait_ge(borders, 2)
                for b in range(CB):
                    for c in range(NCH):
                        src = x[:, b, c * CH:(c + 1) * CH]
                        y = 2 + c * ROWS
                        dst = padded(XH[:, b, :], PAD5)[:, y:y + ROWS, 2:2 + SIDE]
                        act.activation(dst, src.rearrange("p (y x) -> p y x", x=SIDE), ACT.Identity,
                                       scale=gn.scale[:, b:b + 1], bias=gn.shift[:, b:b + 1]).then_inc(high, 1)

PIECE = 5
KERNELS = (1, 3, 5)
TC = CH // P
VW = 3 * HD
UNIT_SCALE = 64.0

def conv_qkv(nc, w_dram, wdw_dram, head_sum_dram, ident_dram, dw_dram, parts_dram, vt_dram, XH, XL):
    with ExitStack() as stack:
        n = Names(nc, stack, "conv")
        SLOTS = 3
        WH = n.sb("w_high", [P, SLOTS, 25 * P], F32R)
        WL = n.sb("w_low", [P, SLOTS, 25 * P], F32R)
        RAW = 3
        raw = n.sb("w_raw", [P, RAW, PIECE * P])
        co = n.sb("conv_out", [P, PAD3 * PAD3])
        cov = padded(co[:, :], PAD3)
        acc = n.sb("dw_out", [P, 2, CH])
        wdw = n.sb("wdw", [P, 6, 9])
        head_sum = n.sb("head_sum", [P, P])
        qd = n.sb("qk_in", [P, CB, CH])
        sq = n.sb("squares", [P, CB, CH])
        nrm = n.sb("norms", [P, CB, CH])
        unit = n.sb("unit", [P, CH])
        ident = n.sb("ident", [P, P])
        vt = n.sb("v_turned", [P, HPB, TC, VW], F32R)
        pt = n.ps("pt", [P, TC, P])
        half = n.sb("halves", [P, CB, 2, CH], F16)
        pc = n.ps("pc", [P, 2, CH])
        pn = n.ps("pn", [P, CB, CH])

        raw_loaded = [n.sem(f"raw_loaded{i}") for i in range(RAW)]
        consts = n.sem("consts_loaded")
        w_high = n.sem("w_high_ready")
        w_low = n.sem("w_low_ready")
        chunk_done = n.sem("conv_chunk_done")
        moved = n.sem("conv_chunk_moved")
        border = n.sem("border_zeroed")
        tap = n.sem("dw_tap")
        stored = [n.sem(f"dw_stored{i}") for i in range(2)]
        qk_loaded = [n.sem(f"qk_loaded{i}") for i in range(CB)]
        squared = n.sem("squared")
        summed = n.sem("summed")
        rooted = n.sem("rooted")
        nstep = n.sem("norm_step")
        half_stored = [n.sem(f"half_stored{i}") for i in range(CB)]
        STEPS = 5
        DW = 2 * 9
        v_turned = n.sem("v_turned")
        v_high = n.sem("v_high_ready")
        v_low = n.sem("v_low_ready")
        v_stored = n.sem("v_stored")

        blocks = [(0, 0), (1, 0), (1, 1), (0, 1), (2, 0), (2, 1)]
        units = [(blk, ib) for blk in range(len(blocks)) for ib in range(CB)]
        place = [(0, 18, None), (0, 19, None), (0, 0, None), (0, 9, None), (1, 0, None), (1, 9, None),
                 (1, 18, None), (1, 19, None), (2, 0, None), (0, 0, 1), (1, 0, 3), (2, 0, 4)]

        V0 = len(blocks) - CB

        def channel_block(blk):
            return blocks[blk][0] * CB + blocks[blk][1]

        def v_part(lo):
            return vt[:, :, :, lo * HD:(lo + 1) * HD].rearrange("p h m c -> p m h c")

        pieces = []
        for u, (blk, ib) in enumerate(units):
            taps = KERNELS[blocks[blk][0]] ** 2
            for t0 in range(0, taps, PIECE):
                pieces.append((u, t0, min(PIECE, taps - t0)))

        def steps(eng, step):
            step(0)
            step(1)
            with eng.Fori(0, NCH // 2 - 1) as i:
                for u in range(2):
                    step(i * 2 + (2 + u), u)

        with nc.Block() as block:

            @block.sync
            def _(sp):
                sp.dma_start(wdw[:, :, :], wdw_dram).then_inc(consts, 16)
                sp.dma_start(head_sum[:, :], head_sum_dram).then_inc(consts, 16)
                sp.dma_start(ident[:, :], ident_dram).then_inc(consts, 16)
                for i, (u, t0, nt) in enumerate(pieces):
                    blk, ib = units[u]
                    k, ob = blocks[blk]
                    if i >= RAW:
                        sp.wait_ge(w_low, i + 1 - RAW)
                    sp.dma_start(raw[:, i % RAW, 0:nt * P],
                                 w_dram[k][ob, ib, :, t0 * P:(t0 + nt) * P]).then_inc(raw_loaded[i % RAW], 16)

            @block.gpsimd
            def _(pool):
                for i, (u, t0, nt) in enumerate(pieces):
                    s, col, before = place[u]
                    if t0 == 0 and before is not None:
                        pool.wait_ge(chunk_done, NCH * (before + 1))
                    at = slice((col + t0) * P, (col + t0 + nt) * P)
                    pool.wait_ge(raw_loaded[i % RAW], 16 * (i // RAW + 1))
                    w = raw[:, i % RAW, 0:nt * P]
                    hi = WH[:, s, at]
                    pool.tensor_copy(hi, w).then_inc(w_high, 1)
                    pool.wait_ge(w_high, i + 1)
                    pool.tensor_tensor(WL[:, s, at], w, hi.bitcast(F32),
                                       ALU.subtract).then_inc(w_low, 1)

            @block.tensor
            def _(pe):
                def conv(blk, c, slot):
                    k, ob = blocks[blk]
                    side = KERNELS[k]
                    off = 2 - side // 2
                    if blk or not isinstance(c, int) or c >= 2:
                        pe.wait_ge(moved, c + (blk * NCH - 1))
                    first = True
                    for ib in range(CB):
                        s, col, _ = place[blk * CB + ib]
                        for t in range(side * side):
                            if isinstance(c, int) and c == 0 and t % PIECE == 0:
                                pe.wait_ge(w_low, pieces.index((blk * CB + ib, t, min(PIECE, side * side - t))) + 1)
                            y, x = off + t // side, off + t % side
                            for w, xs in ((WH, XH), (WH, XL), (WL, XH)):
                                last = ib == CB - 1 and t == side * side - 1 and w is WL
                                mm = pe.matmul(pc[:, slot, :], w[:, s, (col + t) * P:(col + t + 1) * P],
                                               padded(xs[:, ib, :], PAD5)[:, ds(c * ROWS + y, ROWS), x:x + SIDE],
                                               start=first, stop=last)
                                first = False
                        if k == 2 and ib == 0:
                            head_sums(ob, c)
                    mm.then_inc(chunk_done, 1)

                def head_sums(which, j):
                    for a in range(CB):
                        m = j * CB + (which * NCH * CB + a)
                        pe.wait_ge(squared, m + 1)
                        pe.matmul(pn[:, a, :], head_sum[:, :], sq[:, a, :], start=True, stop=True).then_inc(summed, 1)

                def turn_v(vi, slot):
                    pe.wait_ge(tap, (vi + (V0 * NCH + 1)) * DW)
                    pe.wait_ge(v_low, vi + 1)
                    for j in range(TC):
                        mm = pe.transpose(pt[:, j, :], acc[:, slot, j * P:(j + 1) * P], ident[:, :])
                    mm.then_inc(v_turned, 1)

                pe.wait_ge(consts, 48)
                for blk, (k, ob) in enumerate(blocks):
                    def step(c, u=None):
                        conv(blk, c, c if u is None else u)
                        if k == 2 and (ob or not isinstance(c, int)):
                            turn_v(c + (ob * NCH - 2), c if u is None else u)
                    steps(pe, step)
                for vi in range(CB * NCH - 2, CB * NCH):
                    turn_v(vi, vi % 2)

            @block.scalar
            def _(act):
                def move(blk, c, slot):
                    act.wait_ge(chunk_done, c + (blk * NCH + 1))
                    if blk:
                        act.wait_ge(tap, (c + ((blk - 1) * NCH + 2)) * DW)
                    apart(act, border)
                    act.activation(cov[:, ds(c * ROWS + 1, ROWS), 1:1 + SIDE],
                                   pc[:, slot, :].rearrange("p (y x) -> p y x", x=SIDE),
                                   ACT.Identity).then_inc(moved, 1)

                def store(blk, c, slot):
                    act.wait_ge(tap, (c + (blk * NCH + 1)) * DW)
                    act.dma_start(dw_dram[channel_block(blk), :, ds(c * CH, CH)], acc[:, slot, :]).then_inc(stored[slot], 16)

                def store_halves(which, j):
                    for a in range(CB):
                        m = j * CB + (which * NCH * CB + a)
                        act.wait_ge(nstep, (m + 1) * STEPS)
                        act.dma_start(parts_dram[1 - which, :, a * P:(a + 1) * P, ds(j * CH, CH)].rearrange("s p n -> p s n"),
                                      half[:, a, :, :]).then_inc(half_stored[a], 16)

                def split_v(ob, g, odd):
                    vi = g + ob * NCH
                    out = vt_dram.rearrange("(b h) p n -> b h p n", b=CB)
                    act.wait_ge(v_turned, vi + 1)
                    act.wait_ge(v_stored, (vi + 1) * 16)
                    src = pt[:, :, :].rearrange("p m (h c) -> p m h c", c=HD)
                    for j0, j1, plain in ((0, 2, False), (2, 3, True), (3, 4, False)) if odd else ((0, TC, False),):
                        dst = v_part(0)[:, j0:j1]
                        ins = act.activation(dst.bitcast(F32) if plain else dst, src[:, j0:j1], ACT.Identity)
                    ins.then_inc(v_high, 1)
                    act.wait_ge(v_low, vi + 2)
                    act.dma_start(out[ob, :, :, ds(g * (TC * VW), TC * VW)].rearrange("h p n -> p h n"),
                                  vt[:, :, :, :].bitcast(F32).rearrange("p h m c -> p h (m c)")).then_inc(v_stored, 16)

                def block_steps(blk, k, ob):
                    def step(c, u=None):
                        slot = c if u is None else u
                        if k == 2:
                            if not isinstance(c, int) or c:
                                store_halves(ob, c - 1)
                            elif ob:
                                store_halves(0, NCH - 1)
                            for a in range(CB):
                                m = c * CB + (ob * NCH * CB + a)
                                if not isinstance(m, int) or m >= CB:
                                    act.wait_ge(nstep, (m - CB + 1) * STEPS)
                                act.dma_start(qd[:, a, :], dw_dram[2 * (1 - ob) + a, :, ds(c * CH, CH)]).then_inc(qk_loaded[a], 16)
                            for a in range(CB):
                                act.wait_ge(qk_loaded[a], (c + (ob * NCH + 1)) * 16)
                                act.activation(sq[:, a, :], qd[:, a, :], ACT.Square).then_inc(squared, 1)
                            for a in range(CB):
                                act.wait_ge(summed, c * CB + (ob * NCH * CB + a + 1))
                                act.activation(nrm[:, a, :], pn[:, a, :], ACT.Sqrt).then_inc(rooted, 1)
                        move(blk, c, slot)
                        if k == 2:
                            if not isinstance(c, int) or c >= 2:
                                split_v(ob, c - 2, slot)
                            elif ob:
                                split_v(ob - 1, NCH - 2 + c, slot)
                        elif not isinstance(c, int) or c >= 2:
                            store(blk, c - 2, slot)
                    return step

                act.wait_ge(border, 1)
                for blk, (k, ob) in enumerate(blocks):
                    if k == 2:
                        for u in range(2):
                            act.wait_ge(stored[u], (V0 - 1 + ob) * (NCH // 2) * 16)
                    steps(act, block_steps(blk, k, ob))
                    if k < 2:
                        store(blk, NCH - 2, 0)
                        store(blk, NCH - 1, 1)
                store_halves(1, NCH - 1)
                split_v(CB - 1, NCH - 2, 0)
                split_v(CB - 1, NCH - 1, 1)
                act.wait_ge(v_stored, (CB * NCH + 1) * 16)
                for u in range(2):
                    act.wait_ge(stored[u], V0 * (NCH // 2) * 16)
                for a in range(CB):
                    act.wait_ge(half_stored[a], CB * NCH * 16)

            @block.vector
            def _(dve):
                def depthwise(blk, c, slot):
                    done = c + blk * NCH
                    last = isinstance(c, int) and c == NCH - 1
                    dve.wait_ge(moved, done + (1 if last else 2))
                    if blk > V0 or (blk == V0 and (not isinstance(c, int) or c >= 2)):
                        dve.wait_ge(v_turned, c + ((blk - V0) * NCH - 1))
                    elif blk or not isinstance(c, int) or c >= 2:
                        dve.wait_ge(stored[slot], (c - slot + blk * NCH) * 8)
                    out = acc[:, slot, :].rearrange("p (y x) -> p y x", x=SIDE)
                    HR = ROWS // 2
                    for t in range(9):
                        w = wdw[:, channel_block(blk), t:t + 1]
                        for h in range(2):
                            src = cov[:, ds(c * ROWS + (t // 3 + h * HR), HR), t % 3:t % 3 + SIDE]
                            half_out = out[:, h * HR:(h + 1) * HR, :]
                            if t == 0:
                                ins = dve.tensor_scalar(half_out, src, w, None, ALU.mult)
                            else:
                                dve.wait_ge(tap, done * DW + (2 * t - 1 + h))
                                ins = dve.scalar_tensor_tensor(out=half_out, in0=src, scalar=w, in1=half_out,
                                                               op0=ALU.mult, op1=ALU.add)
                            ins.then_inc(tap, 1)

                def unit_halves(which, j):
                    for a in range(CB):
                        m = j * CB + (which * NCH * CB + a)
                        dve.wait_ge(rooted, m + 1)
                        dve.tensor_scalar(nrm[:, a, :], nrm[:, a, :], 1e-12, None, ALU.max).then_inc(nstep, 1)
                        dve.wait_ge(nstep, m * STEPS + 1)
                        dve.reciprocal(nrm[:, a, :], nrm[:, a, :]).then_inc(nstep, 1)
                        dve.wait_ge(nstep, m * STEPS + 2)
                        dve.scalar_tensor_tensor(out=unit[:, :], in0=qd[:, a, :], scalar=UNIT_SCALE, in1=nrm[:, a, :],
                                                 op0=ALU.mult, op1=ALU.mult).then_inc(nstep, 1)
                        dve.wait_ge(nstep, m * STEPS + 3)
                        if which or not isinstance(j, int) or j:
                            dve.wait_ge(half_stored[a], (j + which * NCH) * 16)
                        dve.tensor_copy(half[:, a, 0, :], unit[:, :]).then_inc(nstep, 1)
                        dve.wait_ge(nstep, m * STEPS + 4)
                        dve.tensor_tensor(half[:, a, 1, :], unit[:, :], half[:, a, 0, :], ALU.subtract).then_inc(nstep, 1)

                def low_v(vi):
                    dve.wait_ge(v_high, vi + 1)
                    dve.tensor_tensor(v_part(1), pt[:, :, :].rearrange("p m (h c) -> p m h c", c=HD),
                                      v_part(0).bitcast(F32), ALU.subtract).then_inc(v_low, 1)

                dve.memset(co[:, :], 0.0).then_inc(border, 1)
                dve.memset(vt[:, :, :, 2 * HD:VW].bitcast(F32), 1.0).then_inc(v_stored, 16)
                dve.memset(nrm[:, 0, 0:1], 0.0).then_inc(v_low, 1)
                dve.wait_ge(consts, 48)
                for blk, (k, ob) in enumerate(blocks):
                    def step(c, u=None):
                        if k == 2:
                            unit_halves(ob, c)
                        if not isinstance(c, int) or c:
                            depthwise(blk, c - 1, (c - 1) % 2 if u is None else 1 - u)
                        if k == 2 and (ob or not isinstance(c, int)):
                            low_v(c + (ob * NCH - 2))
                    steps(dve, step)
                    depthwise(blk, NCH - 1, 1)
                for vi in range(CB * NCH - 2, CB * NCH):
                    low_v(vi)

NB = 1024
NNB = PX // NB
NG = HEADS * NNB
SCORE_RANGE = 60.0
MT = PX // P
PLAIN = (6, 14, 22, 30)
SPLIT = [m for m in range(MT) if m not in PLAIN]

def attention(nc, parts_dram, vt_dram, temp_dram, x_dram, o_dram, X):
    with ExitStack() as stack:
        n = Names(nc, stack, "att")
        R = 8
        LAG = 5
        qs = n.sb("q_stack", [P, 2, PX], F16)
        ks = n.sb("k_stack", [P, 2, PX], F16)
        vs = [n.sb(f"v_stack{i}", [P, MT, VW], F32R) for i in range(2)]
        e = n.sb("exp", [P, R, NB])
        eh = n.sb("exp_high", [P, R, NB], F32R)
        el = n.sb("exp_low", [P, R, NB], F32R)
        out = n.sb("out", [VW, 2, NB])
        temp = n.sb("temp", [P, HEADS * NNB])
        affine = n.sb("affine", [P, NG, 2])
        scale, shift = affine[:, :, 0], affine[:, :, 1]
        cur = n.sb("affine_now", [P, 2, 2])
        spare = n.sb("spare", [P, 2])
        sc = n.ps("scores", [P, 2, NB])
        pv = n.ps("pv", [P, 2, NB])

        temp_loaded = n.sem("temp_loaded")
        tstep = n.sem("temp_step")
        loaded = [n.sem(f"stack_loaded{i}") for i in range(2)]
        x_loaded = n.sem("x_loaded")
        v_loaded = [n.sem(f"v_loaded{i}") for i in range(2)]
        scored = n.sem("scored")
        exped = n.sem("exped")
        high_act = n.sem("exp_high_by_act")
        high_dve = n.sem("exp_high_by_dve")
        low = n.sem("exp_low_ready")
        summed = n.sem("pv_done")
        pv_free = n.sem("pv_free")
        tneg = n.sem("temp_neg")
        cur_ready = n.sem("affine_now_ready")
        stored = [n.sem(f"out_stored{i}") for i in range(2)]
        LOADS = 8
        ON_ACT = SPLIT[1::3]
        ON_DVE = [m for m in SPLIT if m not in ON_ACT]

        def upto(tiles, g, mt):
            return g * len(tiles) + sum(m <= mt for m in tiles)

        with nc.Block() as block:

            @block.sync
            def _(sp):
                sp.dma_start(temp[:, :], temp_dram).then_inc(temp_loaded, 16)

                def load(head, s):
                    at = head * HD
                    for i, (a, b) in enumerate(((0, 0), (0, 1), (1, 0), (1, 1))):
                        rows = slice(i * HD, (i + 1) * HD)
                        sp.dma_start(qs[rows, s, :], parts_dram[0, a, ds(at, HD), :]).then_inc(loaded[s], 16)
                        sp.dma_start(ks[rows, s, :], parts_dram[1, b, ds(at, HD), :]).then_inc(loaded[s], 16)
                    sp.dma_start(vs[s][:, :, :].bitcast(F32).rearrange("p m c -> p (m c)"),
                                 vt_dram[ds(head, 1), :, :].rearrange("h p n -> (h p) n")).then_inc(v_loaded[s], 16)

                load(0, 0)
                load(1, 1)
                for b in range(CB):
                    sp.dma_start(X[:, b, :], x_dram[b * P:(b + 1) * P, :]).then_inc(x_loaded, 16)
                with sp.Fori(0, HEADS // 2 - 1) as hp:
                    for s in range(2):
                        sp.wait_ge(summed, (hp * 2 + (s + 1)) * (NNB * MT))
                        load(hp * 2 + (2 + s), s)
                sp.wait_ge(summed, (HEADS - 1) * NNB * MT)
                load(0, 0)
                sp.wait_ge(loaded[0], 16 * LOADS * (HEADS // 2 + 1))
                sp.wait_ge(v_loaded[0], 16 * (HEADS // 2 + 1))
                sp.wait_ge(x_loaded, 16 * CB)

            @block.tensor
            def _(pe):
                def scores(s, n0, mt):
                    for c in range(2):
                        mm = pe.matmul(sc[:, mt % 2, c * CH:(c + 1) * CH], ks[:, s, mt * P:(mt + 1) * P],
                                       qs[:, s, n0 + c * CH:n0 + (c + 1) * CH], start=True, stop=True)
                    mm.then_inc(scored, 1)

                def tiles(g, s, nb, s_next, nb_next, next_loaded=None):
                    slot = nb % 2
                    for mt in range(MT):
                        ahead = mt + LAG
                        if ahead == MT and next_loaded is not None:
                            pe.wait_ge(loaded[s_next], next_loaded)
                        pe.wait_ge(exped, g * MT + (ahead - 1))
                        if ahead < MT:
                            scores(s, nb * NB, ahead)
                        else:
                            scores(s_next, nb_next * NB, ahead - MT)
                        if mt in PLAIN:
                            pe.wait_ge(exped, g * MT + (mt + 1))
                            for c in range(2):
                                mm = pe.matmul(pv[0:VW, slot, c * CH:(c + 1) * CH], vs[s][:, mt, :].bitcast(F32),
                                               e[:, mt % R, c * CH:(c + 1) * CH], start=False, stop=False)
                            mm.then_inc(summed, 1)
                            continue
                        if mt in ON_ACT:
                            pe.wait_ge(high_act, upto(ON_ACT, g, mt))
                        else:
                            pe.wait_ge(high_dve, upto(ON_DVE, g, mt))
                        for part in (eh, el):
                            if part is el:
                                pe.wait_ge(low, upto(SPLIT, g, mt))
                            for c in range(2):
                                mm = pe.matmul(pv[0:VW, slot, c * CH:(c + 1) * CH], vs[s][:, mt, :],
                                               part[:, mt % R, c * CH:(c + 1) * CH],
                                               start=mt == 0 and part is eh, stop=mt == MT - 1 and part is el)
                        mm.then_inc(summed, 1)

                pe.wait_ge(loaded[0], 16 * LOADS)
                for mt in range(LAG):
                    if mt >= 2:
                        pe.wait_ge(exped, mt - 1)
                    scores(0, 0, mt)
                with pe.Fori(0, HEADS // 2) as hp:
                    for s in range(2):
                        for nb in range(NNB):
                            g = hp * (2 * NNB) + (s * NNB + nb)
                            pe.wait_ge(pv_free, g + 1)
                            if nb == 0:
                                pe.wait_ge(v_loaded[s], hp * 16 + 16)
                            if nb < NNB - 1:
                                tiles(g, s, nb, s, nb + 1)
                            else:
                                tiles(g, s, nb, 1 - s, 0, (hp + (1 + s)) * (16 * LOADS))

            @block.scalar
            def _(act):
                def move(g, slot):
                    act.wait_ge(summed, (g + 1) * MT)
                    if not isinstance(g, int) or g >= 2:
                        act.wait_ge(stored[slot], (g - slot) * 8)
                    act.activation(out[:, slot, :], pv[0:VW, slot, :], ACT.Identity).then_inc(pv_free, 1)

                def store(g, slot):
                    act.wait_ge(pv_free, g + 3)
                    act.dma_start(o_dram[ds(g, 1), :, :].rearrange("g c n -> (g c) n"), out[:, slot, :]).then_inc(stored[slot], 16)

                def body(g, slot):
                    act.activation(cur[:, slot, :], affine[:, ds(g, 1), :].rearrange("p g a -> p (g a)"),
                                   ACT.Identity).then_inc(cur_ready, 1)
                    act.wait_ge(cur_ready, g + 1)
                    for mt in range(MT):
                        act.wait_ge(scored, g * MT + (mt + 1))
                        if not isinstance(g, int) or g * MT + mt >= R:
                            if (mt - R) % MT in PLAIN:
                                act.wait_ge(summed, g * MT + (mt + 1 - R))
                            else:
                                act.wait_ge(low, g * len(SPLIT) + (sum(m <= (mt - R) % MT for m in SPLIT) - len(SPLIT) * (mt < R)))
                        act.activation(e[:, mt % R, :], sc[:, mt % 2, :], ACT.Exp, scale=cur[:, slot, 0:1],
                                       bias=cur[:, slot, 1:2]).then_inc(exped, 1)
                        if mt - 1 in ON_ACT:
                            if not isinstance(g, int) or g * MT + mt - 1 >= R:
                                act.wait_ge(summed, g * MT + (mt - R))
                            act.wait_ge(exped, g * MT + mt)
                            act.activation(eh[:, (mt - 1) % R, :], e[:, (mt - 1) % R, :], ACT.Identity).then_inc(high_act, 1)
                        if not isinstance(g, int) or g:
                            if mt == LAG + 2:
                                move(g - 1, 1 - slot)
                            if mt == LAG + 4:
                                store(g - 1, 1 - slot)

                act.wait_ge(tstep, 4)
                body(0, 0)
                body(1, 1)
                with act.Fori(0, NG // 2 - 1) as i:
                    for s in range(2):
                        body(i * 2 + (2 + s), s)
                for mt in range(LAG - 2):
                    act.wait_ge(scored, NG * MT + mt + 1)
                    act.wait_ge(low, upto(SPLIT, NG - 1, MT - R + mt))
                    act.activation(e[:, mt, :], sc[:, mt % 2, :], ACT.Exp, scale=cur[:, 0, 0:1],
                                   bias=cur[:, 0, 1:2]).then_inc(exped, 1)
                move(NG - 1, 1)
                store(NG - 1, 1)
                for s in range(2):
                    act.wait_ge(stored[s], 16 * (NG // 2))

            @block.vector
            def _(dve):
                dve.wait_ge(temp_loaded, 16)
                dve.tensor_scalar(scale, temp[:, :], 1.0 / (UNIT_SCALE * UNIT_SCALE), None, ALU.mult).then_inc(tstep, 1)
                dve.tensor_scalar(shift, temp[:, :], -1.0, None, ALU.mult).then_inc(tstep, 1)
                dve.wait_ge(tstep, 2)
                dve.tensor_tensor(shift, shift, temp[:, :], ALU.max).then_inc(tstep, 1)
                dve.wait_ge(tstep, 3)
                dve.tensor_scalar(temp[:, :], shift, -1.0, SCORE_RANGE, ALU.mult, ALU.add).then_inc(tneg, 1)
                dve.wait_ge(tneg, 1)
                dve.tensor_scalar(shift, temp[:, :], 0.0, None, ALU.min).then_inc(tstep, 1)
                dve.memset(spare[:, 0:1], 0.0).then_inc(pv_free, 1)
                dve.memset(spare[:, 1:2], 0.0).then_inc(pv_free, 1)

                def body(g):
                    for mt in SPLIT:
                        if not isinstance(g, int) or g * MT + mt >= R:
                            dve.wait_ge(summed, g * MT + (mt + 1 - R))
                        if mt in ON_ACT:
                            dve.wait_ge(high_act, upto(ON_ACT, g, mt))
                        else:
                            dve.wait_ge(exped, g * MT + (mt + 1))
                            dve.tensor_copy(eh[:, mt % R, :], e[:, mt % R, :]).then_inc(high_dve, 1)
                            dve.wait_ge(high_dve, upto(ON_DVE, g, mt))
                        dve.tensor_tensor(el[:, mt % R, :], e[:, mt % R, :], eh[:, mt % R, :].bitcast(F32),
                                          ALU.subtract).then_inc(low, 1)

                body(0)
                with dve.Fori(0, NG - 1) as i:
                    body(i + 1)

CROP = 48
M1 = CROP * CROP
SEG = M1 // C
NEWTON = 5

def project(nc, o_dram, w_dram, spread_dram, X, gn):
    with ExitStack() as stack:
        n = Names(nc, stack, "proj")
        SLOTS = 4
        w = n.sb("w", [P, CB, C])
        spread = n.sb("spread", [NG, NNB * CB, P])
        inverse = n.sb("inverse", [NG, NB])
        sums = n.sb("sums", [P, SLOTS, 2, NB])
        o = n.sb("o", [P, 2, CB, NB])
        ps = n.ps("ps", [P, 2, CB, CH])
        ps_i = n.ps("ps_i", [P, 2, NB])
        w_loaded = n.sem("w_loaded")
        total_loaded = n.sem("total_loaded")
        sums_loaded = [n.sem(f"sums_loaded{i}") for i in range(SLOTS)]
        inverted = n.sem("inverted")
        spread_done = n.sem("spread_done")
        step = n.sem("step")
        projected = n.sem("projected")
        added = n.sem("added")
        UNITS0 = CB * NNB
        with nc.Block() as block:

            @block.sync
            def _(sp):
                sp.dma_start(inverse[:, :], o_dram[:, 2 * HD, :]).then_inc(total_loaded, 16)
                sp.dma_start(spread[:, :, :], spread_dram).then_inc(w_loaded, 16)
                sp.dma_start(w[:, :, :], w_dram).then_inc(w_loaded, 16)
                for i in range(UNITS0):
                    nb, b = divmod(i, CB)
                    if i >= SLOTS:
                        sp.wait_ge(step, 2 * (i - SLOTS + 1))
                    for h in range(HPB):
                        g = (b * HPB + h) * NNB + nb
                        sp.dma_start(sums[h * HD:(h + 1) * HD, i % SLOTS, :, :],
                                     o_dram[g, 0:2 * HD, :].rearrange("(k c) n -> c k n", c=HD)).then_inc(sums_loaded[i % SLOTS], 16)

            @block.vector
            def _(dve):
                def add(c):
                    dve.wait_ge(projected, c + 1)
                    for ob in range(CB):
                        xs = X[:, ob, c * CH:(c + 1) * CH]
                        dve.tensor_tensor(xs, ps[:, c % 2, ob, :], xs, ALU.add).then_inc(added, 1)
                    dve.wait_ge(added, CB * (c + 1))
                    for ob in range(CB):
                        gn.chunk_stats(dve, X, ob, c)

                dve.wait_ge(total_loaded, 16)
                for q in range(2):
                    at = slice(q * CH, (q + 1) * CH)
                    dve.reciprocal(inverse[:, at], inverse[:, at]).then_inc(inverted, 1)
                for i in range(UNITS0):
                    nb, b = divmod(i, CB)
                    s = sums[:, i % SLOTS]
                    dve.wait_ge(sums_loaded[i % SLOTS], 16 * HPB * (i // SLOTS + 1))
                    dve.tensor_tensor(s[:, 0, :], s[:, 0, :], s[:, 1, :], ALU.add).then_inc(step, 1)
                    dve.wait_ge(step, 2 * i + 1)
                    dve.wait_ge(spread_done, i + 1)
                    if nb >= 2:
                        dve.wait_ge(projected, 2 * (nb - 1))
                    dve.tensor_tensor(o[:, nb % 2, b, :], s[:, 0, :], ps_i[:, i % 2, :], ALU.mult).then_inc(step, 1)
                    if b == 1 and nb:
                        add(2 * nb - 2)
                        add(2 * nb - 1)
                add(NCH - 2)
                add(NCH - 1)
                gn.channel_moments(dve)
                gn.vector_moments(dve)

            @block.tensor
            def _(pe):
                def spread_unit(i):
                    if i >= 2:
                        pe.wait_ge(step, 2 * (i - 1))
                    for h in range(2):
                        if i == 0:
                            pe.wait_ge(inverted, h + 1)
                        mm = pe.matmul(ps_i[:, i % 2, h * CH:(h + 1) * CH], spread[:, i, :],
                                       inverse[:, h * CH:(h + 1) * CH], start=True, stop=True)
                    mm.then_inc(spread_done, 1)

                pe.wait_ge(w_loaded, 32)
                spread_unit(0)
                spread_unit(1)
                for c in range(NCH):
                    nb, h = divmod(c, 2)
                    if h == 0:
                        for b in range(CB):
                            if 2 * (nb + 1) + b < UNITS0:
                                spread_unit(2 * (nb + 1) + b)
                    pe.wait_ge(step, 2 * CB * (nb + 1))
                    if c >= 2:
                        pe.wait_ge(added, 2 * (c - 1))
                    for ob in range(CB):
                        for ib in range(CB):
                            mm = pe.matmul(ps[:, c % 2, ob, :], w[:, ib, ob * P:(ob + 1) * P],
                                           o[:, nb % 2, ib, h * CH:(h + 1) * CH], start=ib == 0, stop=ib == CB - 1)
                    mm.then_inc(projected, 1)

class Count:

    def __init__(self, n, name):
        self.sem, self.value = n.sem(name), 0

    def up(self, ins):
        ins.then_inc(self.sem, 1)
        self.value += 1
        return self.value

def covariance_gate(nc, gm_dram, eye_dram, w1_dram, b1_dram, w2_dram, b2_dram, X, gn, gn_after):
    with ExitStack() as stack:
        n = Names(nc, stack, "cov")
        gm = n.sb("group_mean", [P, P])
        eye = n.sb("eye", [P, CB, C])
        ones = n.sb("ones", [P, P])
        w = n.sb("w", [P, 2, CB, C])
        bias = n.sb("bias", [P, 2, CB])
        new = n.sb("new", [P, 2, CB])
        xc = n.sb("xc", [P, CB, M1])
        rows = n.sb("row_sums", [1, 2, C])
        mats = {k: n.sb(k, [P, CB, C]) for k in ("cov", "A", "Y", "Y2", "Z", "Z2", "ZY", "diag")}
        small = n.sb("small", [P, 16])
        ps_gn = n.ps("ps_gn", [P, CB * 2])
        ps_g = n.ps("ps_g", [P, CB, C])
        ps_r = n.ps("ps_r", [P, C])
        ps_y = n.ps("ps_y", [P, CB, C])
        ps_z = n.ps("ps_z", [P, CB, C])
        ps_s = n.ps("ps_s", [P, 8])
        loaded = n.sem("loaded")
        ones_set = n.sem("ones_set")
        crop = n.sem("crop_ready")
        new_ready = n.sem("new_ready")
        x_ready = n.sem("x_ready")
        T = Count(n, "tensor_done")
        V = Count(n, "vector_done")
        A = Count(n, "scalar_done")
        at = {}

        nt = nv = na = 0
        for name in ("sums", "gram", "trace", "Y0") + tuple(f"{m}{i}" for i in range(1, NEWTON - 1) for m in "TYZ") + (
                "TF", "YF", "FC1", "FC2"):
            nt += 1
            at["t", name] = nt
        with nc.Block() as block:

            @block.sync
            def _(sp):
                for t, d in ((gm[:, :], gm_dram), (eye[:, :, :], eye_dram), (w[:, 0], w1_dram), (w[:, 1], w2_dram),
                             (bias[:, 0], b1_dram), (bias[:, 1], b2_dram)):
                    sp.dma_start(t, d).then_inc(loaded, 16)

            @block.gpsimd
            def _(pool):
                pool.memset(ones[:, :], 1.0).then_inc(ones_set, 1)

            @block.vector
            def _(dve):
                gn.vector_affine(dve, ps_gn[:, :])
                v = dict()

                def made(name, ins):
                    v[name] = at["v", name] = V.up(ins)

                def after(name):
                    dve.wait_ge(V.sem, v[name])

                dve.wait_ge(loaded, 96)
                dve.wait_ge(T.sem, at["t", "sums"])
                made("row", dve.tensor_copy(rows[0:1, 0, :], ps_r[0:1, :]))
                made("nrow", dve.tensor_scalar(rows[0:1, 1, :], ps_r[0:1, :], -1.0 / M1, None, ALU.mult))
                dve.wait_ge(T.sem, at["t", "gram"])
                made("cov", dve.tensor_scalar(mats["cov"][:, :, :], ps_g[:, :, :], 1.0 / M1, None, ALU.mult))
                after("cov")
                made("diag", dve.tensor_tensor(mats["diag"][:, :, :], mats["cov"][:, :, :], eye[:, :, :], ALU.mult))
                after("diag")
                made("diag_sum", dve.reduce_sum(small[:, 0:1], mats["diag"][:, :, :].rearrange("p b c -> p (b c)"), AX.X))
                dve.wait_ge(T.sem, at["t", "trace"])
                made("trace", dve.tensor_copy(small[:, 1:2], ps_s[:, 0:1]))
                after("trace")
                made("inv", dve.reciprocal(small[:, 2:3], small[:, 1:2]))
                after("inv")
                made("A", dve.tensor_scalar(mats["A"][:, :, :], mats["cov"][:, :, :], small[:, 2:3], None, ALU.mult))
                made("eye15", dve.tensor_scalar(mats["diag"][:, :, :], eye[:, :, :], 1.5, None, ALU.mult))
                after("eye15")
                e15 = mats["diag"]
                made("Z0", dve.scalar_tensor_tensor(out=mats["Z"][:, :, :], in0=mats["A"][:, :, :], scalar=-0.5,
                                                    in1=e15[:, :, :], op0=ALU.mult, op1=ALU.add))
                dve.wait_ge(T.sem, at["t", "Y0"])
                made("Y0", dve.tensor_copy(mats["Y"][:, :, :], ps_y[:, :, :]))
                for i in range(1, NEWTON):
                    dve.wait_ge(T.sem, at["t", f"T{i}" if i < NEWTON - 1 else "TF"])
                    made(f"ZY{i}", dve.scalar_tensor_tensor(out=mats["ZY"][:, :, :], in0=ps_y[:, :, :], scalar=-0.5,
                                                            in1=e15[:, :, :], op0=ALU.mult, op1=ALU.add))
                    if i == NEWTON - 1:
                        break
                    dve.wait_ge(T.sem, at["t", f"Y{i}"])
                    made(f"Y{i}", dve.tensor_copy(mats["Y"][:, :, :], ps_z[:, :, :]))
                    dve.wait_ge(T.sem, at["t", f"Z{i}"])
                    made(f"Z{i}", dve.tensor_copy(mats["Z"][:, :, :], ps_g[:, :, :]))
                dve.wait_ge(T.sem, at["t", "YF"])
                made("mean", dve.reduce_sum(small[:, 4:6], ps_z[:, :, :], AX.X))
                after("mean")
                dve.wait_ge(A.sem, 1)
                made("y", dve.tensor_scalar(small[:, 6:8], small[:, 4:6], small[:, 3:4], 1.0 / C, ALU.mult, ALU.mult))
                dve.wait_ge(T.sem, at["t", "FC1"])
                made("h0", dve.tensor_tensor(small[:, 8:10], ps_s[:, 2:4], bias[:, 0, :], ALU.add))
                after("h0")
                made("h", dve.tensor_scalar(small[:, 8:10], small[:, 8:10], 0.0, None, ALU.max))
                dve.wait_ge(T.sem, at["t", "FC2"])
                made("g0", dve.tensor_tensor(small[:, 10:12], ps_s[:, 4:6], bias[:, 1, :], ALU.add))
                dve.wait_ge(A.sem, 2)
                gate = small[:, 12:14]
                made("gscale", dve.tensor_tensor(new[:, 0, :], gate, gn.scale[:, :], ALU.mult))
                after("gscale")
                dve.tensor_scalar(new[:, 0, :], new[:, 0, :], 1.0, None, ALU.add).then_inc(new_ready, 1)
                dve.tensor_tensor(new[:, 1, :], gate, gn.shift[:, :], ALU.mult).then_inc(new_ready, 1)
                dve.wait_ge(new_ready, 2)
                gn_after.moments_of_affine(dve, gn, new[:, 0, :], new[:, 1, :])
                gn_after.vector_moments(dve)
                dve.wait_ge(crop, CB)
                dve.tensor_scalar(X[:, 1, :], X[:, 1, :], new[:, 0, 1:2], new[:, 1, 1:2], ALU.mult, ALU.add).then_inc(x_ready, 1)

            @block.tensor
            def _(pe):
                def product(name, out, left, right):
                    for m in range(CB):
                        for k in range(CB):
                            mm = pe.matmul(out[:, m, :], left[:, k, m * P:(m + 1) * P], right[:, k, :],
                                           start=k == 0, stop=k == CB - 1)
                    assert T.up(mm) == at["t", name]

                def after(name):
                    pe.wait_ge(V.sem, at["v", name])

                pe.wait_ge(loaded, 96)
                gn.tensor_join(pe, ps_gn[:, :], gm[:, :])
                pe.wait_ge(ones_set, 1)
                pe.wait_ge(crop, CB)
                tiles = [xc[:, b, j::SEG] for b in range(CB) for j in range(SEG)]
                for i, t in enumerate(tiles):
                    mm = pe.matmul(ps_r[0:1, :], ones[:, 0:1], t, start=i == 0, stop=i == len(tiles) - 1)
                T.up(mm)
                for m in range(CB):
                    for i, t in enumerate(tiles):
                        pe.matmul(ps_g[:, m, :], t[:, m * P:(m + 1) * P], t, start=i == 0, stop=False)
                    if m == 0:
                        after("nrow")
                    mm = pe.matmul(ps_g[:, m, :], rows[0:1, 0, m * P:(m + 1) * P], rows[0:1, 1, :], start=False, stop=True)
                T.up(mm)
                after("diag_sum")
                T.up(pe.matmul(ps_s[:, 0:1], ones[:, :], small[:, 0:1], start=True, stop=True))
                after("Z0")
                product("Y0", ps_y, mats["A"], mats["Z"])
                after("Y0")
                for i in range(1, NEWTON - 1):
                    product(f"T{i}", ps_y, mats["Z"], mats["Y"])
                    after(f"ZY{i}")
                    product(f"Y{i}", ps_z, mats["Y"], mats["ZY"])
                    product(f"Z{i}", ps_g, mats["ZY"], mats["Z"])
                    after(f"Z{i}")
                product("TF", ps_y, mats["Z"], mats["Y"])
                after(f"ZY{NEWTON - 1}")
                product("YF", ps_z, mats["Y"], mats["ZY"])
                for layer, (name, src, col) in enumerate((("y", 6, 2), ("h", 8, 4))):
                    after(name)
                    for ob in range(CB):
                        for ib in range(CB):
                            mm = pe.matmul(ps_s[:, col + ob:col + ob + 1], w[:, layer, ib, ob * P:(ob + 1) * P],
                                           small[:, src + ib:src + ib + 1], start=ib == 0, stop=ib == CB - 1)
                    T.up(mm)

            @block.scalar
            def _(act):
                gn.scalar_std(act)
                act.wait_ge(gn.ready, 1)
                lo = (SIDE - CROP) // 2
                for b in range(CB):
                    act.activation(xc[:, b, :].rearrange("p (y x) -> p y x", x=CROP),
                                   padded(X[:, b, :], SIDE)[:, lo:lo + CROP, lo:lo + CROP], ACT.Identity,
                                   scale=gn.scale[:, b:b + 1], bias=gn.shift[:, b:b + 1]).then_inc(crop, 1)
                act.wait_ge(V.sem, at["v", "trace"])
                A.up(act.activation(small[:, 3:4], small[:, 1:2], ACT.Sqrt))
                act.wait_ge(V.sem, at["v", "g0"])
                A.up(act.activation(small[:, 12:14], small[:, 10:12], ACT.Sigmoid))
                act.wait_ge(new_ready, 2)
                act.wait_ge(crop, CB)
                act.activation(X[:, 0, :], X[:, 0, :], ACT.Identity, scale=new[:, 0, 0:1],
                               bias=new[:, 1, 0:1]).then_inc(x_ready, 1)

TAPS = 9
TAB = SIDE + 2
TILES = PX // P
OM = 3 * TAPS

def offsets_and_table(nc, gm_dram, ident_dram, ow_dram, ob_dram, base_dram, table_dram, X, IDX, CW, gn):
    with ExitStack() as stack:
        n = Names(nc, stack, "off")
        gm = n.sb("group_mean", [P, P])
        ident = n.sb("ident", [P, P])
        xp = n.sb("x_padded", [P, CB, PAD3 * PAD3])
        xn = n.sb("xn", [P, CB, PX])
        ow = n.sb("offset_w", [P, CB, TAPS * OM])
        obias = n.sb("offset_b", [OM, 1])
        base = n.sb("base", [P, 2, TILES * TAPS])
        om = n.sb("om", [OM, PX])
        omt = n.sb("om_t", [P, TILES, OM])
        zero = n.sb("zero", [P, C])
        xt = n.sb("x_turned", [P, 2, C])
        F = {k: n.sb(k, [P, TILES, TAPS]) for k in ("py", "px", "fy", "fx", "ly", "lx", "hy", "hx", "gy", "gx", "mask")}
        whole = n.sb("whole", [P, 2, TILES * TAPS], I32)
        ps_gn = n.ps("ps_gn", [P, CB * 2])
        ps_o = n.ps("ps_o", [P, 2, CH])
        ps_t = n.ps("ps_t", [P, 2, CH])
        ps_m = n.ps("ps_m", [P, 2, CH])
        loaded = n.sem("loaded")
        border = n.sem("border")
        zero_set = n.sem("zero_set")
        normed = n.sem("normed")
        conv = n.sem("om_conv")
        om_ready = n.sem("om_ready")
        om_turned = n.sem("om_turned")
        turned = n.sem("turned")
        xt_ready = n.sem("xt_ready")
        kept = [n.sem(f"kept{i}") for i in range(2)]
        zeroed = n.sem("table_zeroed")
        masked = n.sem("masked")
        V = Count(n, "vector_done")
        corner = table_dram.rearrange("(y x) (q c) -> q y x c", x=TAB, c=C)
        HB = TILES // 2

        with nc.Block() as block:

            @block.sync
            def _(sp):
                for t, d in ((gm[:, :], gm_dram), (ident[:, :], ident_dram), (ow[:, :, :], ow_dram),
                             (obias[:, :], ob_dram), (base[:, :, :], base_dram)):
                    sp.dma_start(t, d).then_inc(loaded, 16)
                with sp.Fori(0, TILES // 2) as i:
                    for u in range(2):
                        sp.wait_ge(xt_ready, i * 2 + (u + 1))
                        for q in range(4):
                            dy, dx = divmod(q, 2)
                            for r in range(2):
                                sp.dma_start(corner[q, ds(i * 4 + (2 * u + r + 1 - dy), 1), 1 - dx:1 - dx + SIDE, :].rearrange("y x c -> (y x) c"),
                                             xt[r * SIDE:(r + 1) * SIDE, u, :]).then_inc(kept[u], 16)
                for u in range(2):
                    sp.wait_ge(kept[u], 16 * 8 * TILES // 2)

            @block.gpsimd
            def _(pool):
                pool.memset(xp[:, :, :], 0.0).then_inc(border, 1)
                pool.memset(zero[:, :], 0.0).then_inc(zero_set, 1)
                pool.wait_ge(zero_set, 1)
                done = 0
                for q in range(4):
                    dy, dx = divmod(q, 2)
                    for line in ({0, TAB - 1} if not dy else {TAB - 2, TAB - 1}):
                        pool.dma_start(corner[q, line, :, :], zero[0:TAB, :]).then_inc(zeroed, 16)
                        done += 16
                    rows = slice(1 - dy, 1 - dy + SIDE)
                    for line in ({0, TAB - 1} if not dx else {TAB - 2, TAB - 1}):
                        pool.dma_start(corner[q, rows, line, :], zero[0:SIDE, :]).then_inc(zeroed, 16)
                        done += 16
                pool.wait_ge(zeroed, done)

            @block.scalar
            def _(act):
                gn.scalar_std(act)
                act.wait_ge(gn.ready, 1)
                act.wait_ge(border, 1)
                for b in range(CB):
                    act.activation(xn[:, b, :], X[:, b, :], ACT.Identity, scale=gn.scale[:, b:b + 1],
                                   bias=gn.shift[:, b:b + 1]).then_inc(normed, 1)
                    act.activation(padded(xp[:, b, :], PAD3)[:, 1:1 + SIDE, 1:1 + SIDE], padded(X[:, b, :], SIDE),
                                   ACT.Identity, scale=gn.scale[:, b:b + 1], bias=gn.shift[:, b:b + 1]).then_inc(normed, 1)
                for t in range(TILES):
                    act.wait_ge(turned, t + 1)
                    if t >= 2:
                        act.wait_ge(kept[t % 2], 16 * 8 * (t // 2))
                    act.activation(xt[:, t % 2, :], ps_t[:, t % 2, 0:C], ACT.Identity).then_inc(xt_ready, 1)
                act.wait_ge(V.sem, 1)
                act.activation(F["mask"][:, :, :], omt[:, :, 2 * TAPS:], ACT.Sigmoid).then_inc(masked, 1)

            @block.tensor
            def _(pe):
                pe.wait_ge(loaded, 16 * 5)
                gn.tensor_join(pe, ps_gn[:, :], gm[:, :])
                pe.wait_ge(normed, 2 * CB)

                def turn(t):
                    if t >= 2:
                        pe.wait_ge(xt_ready, t - 1)
                    for b in range(CB):
                        mm = pe.transpose(ps_t[:, t % 2, b * P:(b + 1) * P],
                                          xn[:, b, t * P:(t + 1) * P], ident[:, :])
                    mm.then_inc(turned, 1)

                for c in range(NCH):
                    if c >= 2:
                        pe.wait_ge(om_ready, c - 1)
                    for b in range(CB):
                        for t in range(TAPS):
                            mm = pe.matmul(ps_o[0:OM, c % 2, :], ow[:, b, t * OM:(t + 1) * OM],
                                           padded(xp[:, b, :], PAD3)[:, c * ROWS + t // 3:c * ROWS + t // 3 + ROWS, t % 3:t % 3 + SIDE],
                                           start=b == 0 and t == 0, stop=b == CB - 1 and t == TAPS - 1)
                    mm.then_inc(conv, 1)
                    for t in range(4 * c, 4 * c + 4):
                        turn(t)
                pe.wait_ge(om_ready, NCH)
                for t in range(TILES):
                    h, i = divmod(t, HB)
                    mm = pe.transpose(ps_m[:, h, i * OM:(i + 1) * OM], om[:, t * P:(t + 1) * P], ident[0:OM, 0:OM])
                mm.then_inc(om_turned, 1)

            @block.vector
            def _(dve):
                gn.vector_affine(dve, ps_gn[:, :])
                dve.wait_ge(loaded, 16 * 5)
                for c in range(NCH):
                    dve.wait_ge(conv, c + 1)
                    dve.tensor_scalar(om[:, c * CH:(c + 1) * CH], ps_o[0:OM, c % 2, :], obias[:, 0:1], None,
                                      ALU.add).then_inc(om_ready, 1)
                dve.wait_ge(om_turned, 1)

                def made(ins):
                    V.up(ins)
                    dve.wait_ge(V.sem, V.value)

                made(dve.tensor_copy(omt[:, :, :].rearrange("p (h t) m -> p h (t m)", h=2), ps_m[:, :, 0:HB * OM]))
                for k, (pos, frac, hi, fl, gap) in enumerate((("py", "ly", "hy", "fy", "gy"), ("px", "lx", "hx", "fx", "gx"))):
                    bs = base[:, k, :].rearrange("p (t a) -> p t a", a=TAPS)
                    wh = whole[:, k, :].rearrange("p (t a) -> p t a", a=TAPS)
                    made(dve.tensor_tensor(F[pos][:, :, :], omt[:, :, k:2 * TAPS:2], bs, ALU.add))
                    made(dve.tensor_scalar(F[pos][:, :, :], F[pos][:, :, :], 0.0, float(SIDE + 1), ALU.max, ALU.min))
                    made(dve.tensor_copy(wh, F[pos][:, :, :]))
                    made(dve.tensor_copy(F[fl][:, :, :], wh))
                    made(dve.tensor_tensor(F[gap][:, :, :], F[fl][:, :, :], F[pos][:, :, :], ALU.is_gt))
                    made(dve.tensor_tensor(F[fl][:, :, :], F[fl][:, :, :], F[gap][:, :, :], ALU.subtract))
                    made(dve.tensor_tensor(F[frac][:, :, :], F[pos][:, :, :], F[fl][:, :, :], ALU.subtract))
                    made(dve.tensor_scalar(F[hi][:, :, :], F[frac][:, :, :], -1.0, 1.0, ALU.mult, ALU.add))
                made(dve.scalar_tensor_tensor(out=F["gy"][:, :, :], in0=F["fy"][:, :, :], scalar=float(TAB),
                                              in1=F["fx"][:, :, :], op0=ALU.mult, op1=ALU.add))
                made(dve.tensor_copy(IDX[:, :].rearrange("p (t a) -> p t a", a=TAPS), F["gy"][:, :, :]))
                dve.wait_ge(masked, 1)
                for q, (a, b) in enumerate((("hy", "hx"), ("hy", "lx"), ("ly", "hx"), ("ly", "lx"))):
                    made(dve.tensor_tensor(F["gx"][:, :, :], F[a][:, :, :], F[b][:, :, :], ALU.mult))
                    made(dve.tensor_tensor(CW[:, :, q].rearrange("p (t a) -> p t a", a=TAPS), F["gx"][:, :, :],
                                           F["mask"][:, :, :], ALU.mult))

def deform(nc, ident_dram, dw_dram, table_dram, X, IDX, CW, gn):
    with ExitStack() as stack:
        n = Names(nc, stack, "dcn")
        GT = 4
        NGR = TILES // GT
        GS = 9
        BATCH = 3
        VS = 6
        TS = 3
        BEHIND = 2
        ident = n.sb("ident", [P, P])
        w = n.sb("w", [P, CB, TAPS, C])
        cur_idx = n.sb("cur_idx", [P, 2, TAPS], I32)
        g = n.sb("gathered", [P, GS, 4 * C])
        tick = n.sb("tick", [P, 2])
        tick_set = n.sem("tick_set")
        ticked = n.sem("ticked")
        val = n.sb("val", [P, VS, C])
        vt = n.sb("val_turned", [P, 2, TAPS, CB, GT * P])
        ps_t = n.ps("ps_t", [P, TS, 2 * CB, P])
        ps_o = n.ps("ps_o", [P, 2, CB, CH])
        loaded = n.sem("loaded")
        idx_ready = n.sem("idx_ready")
        got = [n.sem(f"gathered{i}") for i in range(GS)]
        first = n.sem("first_product")
        step = n.sem("step")
        turned = n.sem("turned")
        kept = n.sem("turned_moved")
        product = n.sem("product")
        added = n.sem("added")

        def groups(eng, body):
            body(0, 0)
            body(1, 1)
            with eng.Fori(0, NGR // 2 - 2) as i:
                for u in range(2):
                    body(i * 2 + (2 + u), u)
            body(NGR - 2, 0)
            body(NGR - 1, 1)

        def static(v):
            return isinstance(v, int)

        with nc.Block() as block:

            @block.sync
            def _(sp):
                sp.dma_start(ident[:, :], ident_dram).then_inc(loaded, 16)
                sp.dma_start(w[:, :, :, :], dw_dram).then_inc(loaded, 16)

            @block.gpsimd
            def _(pool):
                pool.memset(tick[:, :], 0.0).then_inc(tick_set, 1)
                pool.wait_ge(tick_set, 1)
                pool.tensor_tensor(tick[:, 1:2], tick[:, 0:1], tick[:, 0:1], ALU.add).then_inc(ticked, 1)

                TICKS = 2 + 2 * TAPS // BATCH

                def passed(t2, k, sem, value):
                    if not static(t2):
                        pool.wait_ge(ticked, (t2 - 1) * TICKS + (k + 1))
                        pool.wait_ge(sem, value)
                        pool.tensor_tensor(tick[:, 1:2], tick[:, 0:1], tick[:, 0:1], ALU.add).then_inc(ticked, 1)
                    else:
                        pool.wait_ge(sem, value)

                def gathers(t2):
                    for u in range(2):
                        passed(t2, u * (TICKS // 2), idx_ready, t2 * 2 + (u + 1))
                        for k in range(TAPS):
                            i = u * TAPS + k
                            if i % BATCH == 0 and (not static(t2) or i >= GS):
                                passed(t2, u * (TICKS // 2) + 1 + k // BATCH, step, (t2 * (2 * TAPS) + (i + BATCH - GS)) * 3)
                            pool.indirect_dma_start(g[:, i % GS, :], None, table_dram,
                                                    bass.IndirectOffsetOnAxis(ap=cur_idx[:, u, k:k + 1], axis=0)).then_inc(
                                                        got[i % GS], 16)
                gathers(0)
                with pool.Fori(0, TILES // 2 - 1) as t:
                    gathers(t + 1)

            def gather_count(t2, i):
                return (t2 * (2 * TAPS // GS) + (i // GS + 1)) * 16

            @block.scalar
            def _(act):
                def pair(t2, gt, gslot):
                    for u in range(2):
                        for k in range(TAPS):
                            i = u * TAPS + k
                            m = t2 * (2 * TAPS) + i
                            act.wait_ge(got[i % GS], gather_count(t2, i))
                            if not static(t2) or t2 * 2 * TAPS + i >= VS:
                                act.wait_ge(turned, m - (VS - 1))
                            if not static(t2):
                                apart(act, turned)
                            act.activation(val[:, i % VS, :], g[:, i % GS, 0:C], ACT.Identity,
                                           scale=CW[:, ds(m, 1), 0]).then_inc(first, 1)
                            if i >= BEHIND:
                                move(t2, i - BEHIND, gt, gslot)
                    for i in range(2 * TAPS - BEHIND, 2 * TAPS):
                        move(t2, i, gt, gslot)

                def move(t2, i, gt, gslot):
                    u, k = divmod(i, TAPS)
                    act.wait_ge(turned, t2 * (2 * TAPS) + (i + 1))
                    at = (gt + u) * P
                    act.activation(vt[:, gslot, k, :, at:at + P], ps_t[:, i % TS, 0:CB, :], ACT.Identity).then_inc(kept, 1)

                def group(gr, slot):
                    if not static(gr) or gr >= 2:
                        act.wait_ge(product, gr - 1)
                    for h in range(GT // 2):
                        pair(gr * (GT // 2) + h, 2 * h, slot)

                groups(act, group)

            @block.vector
            def _(dve):
                def put(t2, u):
                    if not static(t2) or t2:
                        dve.wait_ge(got[(u * TAPS + TAPS - 1) % GS],
                                    ((t2 - 1) * (2 * TAPS // GS) + ((u * TAPS + TAPS - 1) // GS + 1)) * 16)
                    dve.tensor_copy(cur_idx[:, u, :], IDX[:, ds(t2 * (2 * TAPS) + u * TAPS, TAPS)]).then_inc(idx_ready, 1)

                waiting = [(b, c) for c in range(NCH - 2) for b in range(CB)]

                def stats(b, c):
                    dve.wait_ge(added, CB * (c + 1))
                    gn.chunk_stats(dve, X, b, c)

                def pair(t2, last=False):
                    for i in range(2 * TAPS):
                        if i % TAPS == 0 and i and not last:
                            put(t2 + 1, 0)
                        if static(t2) and waiting and i % 4 == 3 and waiting[0][1] + 2 <= t2 // (GT // 2) >= NGR - 2:
                            stats(*waiting.pop(0))
                        m = t2 * (2 * TAPS) + i
                        s = i % GS
                        dve.wait_ge(first, m + 1)
                        for q in range(1, 4):
                            if q > 1:
                                dve.wait_ge(step, m * 3 + (q - 1))
                            dve.scalar_tensor_tensor(out=val[:, i % VS, :], in0=g[:, s, q * C:(q + 1) * C],
                                                     scalar=CW[:, ds(m, 1), q], in1=val[:, i % VS, :],
                                                     op0=ALU.mult, op1=ALU.add).then_inc(step, 1)
                    if not last:
                        put(t2 + 1, 1)

                def add(gr, slot):
                    for ob in range(CB):
                        dve.wait_ge(product, gr + 1)
                        xs = X[:, ob, ds(gr * CH, CH)]
                        dve.tensor_tensor(xs, ps_o[:, slot, ob, :], xs, ALU.add).then_inc(added, 1)

                def group(gr, slot):
                    for h in range(GT // 2):
                        t2 = gr * (GT // 2) + h
                        pair(t2, static(gr) and gr == NGR - 1 and h == 1)
                    if not static(gr) or gr:
                        add(gr - 1, 1 - slot)

                for u in range(2):
                    put(0, u)
                groups(dve, group)
                for b, c in waiting + [(b, NCH - 2) for b in range(CB)]:
                    stats(b, c)
                add(NGR - 1, 1)
                for b in range(CB):
                    stats(b, NCH - 1)
                gn.channel_moments(dve)
                gn.vector_moments(dve)

            @block.tensor
            def _(pe):
                def turn(gr, gt, k):
                    i = (gt % 2) * TAPS + k
                    m = gr * (GT * TAPS) + (gt * TAPS + k)
                    pe.wait_ge(step, (m + 1) * 3)
                    if not static(m) or m >= TS:
                        pe.wait_ge(kept, m - (TS - 1))
                    for b in range(CB):
                        mm = pe.transpose(ps_t[:, i % TS, b, :], val[:, i % VS, b * P:(b + 1) * P], ident[:, :])
                    mm.then_inc(turned, 1)

                def product_part(gr, slot, part, k):
                    ob, b = divmod(part, CB)
                    if part == 0 and k == 0:
                        pe.wait_ge(kept, (gr + 1) * (GT * TAPS))
                        if not static(gr) or gr >= 2:
                            pe.wait_ge(added, (gr - 1) * CB)
                    mm = pe.matmul(ps_o[:, slot, ob, :], w[:, b, k, ob * P:(ob + 1) * P], vt[:, slot, k, b, :],
                                   start=b == 0 and k == 0, stop=b == CB - 1 and k == TAPS - 1)
                    if part == GT - 1 and k == TAPS - 1:
                        mm.then_inc(product, 1)

                def last_products(gt):
                    pe.wait_ge(kept, ((NGR - 1) * GT + gt + 1) * TAPS)
                    if gt == 0:
                        pe.wait_ge(added, (NGR - 2) * CB)
                    at = slice(gt * P, (gt + 1) * P)
                    for ob in range(CB):
                        for b in range(CB):
                            for k in range(TAPS):
                                mm = pe.matmul(ps_o[:, 1, ob, at], w[:, b, k, ob * P:(ob + 1) * P], vt[:, 1, k, b, at],
                                               start=b == 0 and k == 0, stop=b == CB - 1 and k == TAPS - 1)
                    if gt == GT - 1:
                        mm.then_inc(product, 1)

                def group(gr, slot):
                    for gt in range(GT):
                        for k in range(TAPS):
                            turn(gr, gt, k)
                            if not static(gr) or gr:
                                product_part(gr - 1, 1 - slot, gt, k)
                            if static(gr) and gr == NGR - 1 and gt and k == BEHIND + 1:
                                last_products(gt - 1)

                pe.wait_ge(loaded, 32)
                groups(pe, group)
                last_products(GT - 1)

LT = 25
UNIT = 16
UNITS = SIDE // UNIT
LOCAL_BESIDE_LINEAR = 4
KEY_SCALE = float(HD) ** -0.5

class LocalConv:

    def __init__(self, n, V_, L):
        self.V_, self.L = V_, L
        self.w = n.sb("w_local", [P, CB, LT])
        self.bias = n.sb("b_local", [P, CB])
        self.done = n.sem("local_tap")
        self.count = 0
        chunks = [(b, c) for b in range(CB) for c in range(NCH)]
        self.left = [(b, c, LT // 2) for b, c in chunks]
        for i in range(0, len(chunks), 2):
            self.left += [(b, c, t) for t in range(LT) if t != LT // 2 for b, c in chunks[i:i + 2]]

    def centres_left(self):
        return sum(t == LT // 2 for _, _, t in self.left)

    def steps(self, dve, k):
        for b, c, t in self.left[:k]:
            dy, dx = t // 5 - 2, t % 5 - 2
            y0, y1 = max(c * ROWS, -dy), min((c + 1) * ROWS, SIDE - dy)
            x0, x1 = max(0, -dx), min(SIDE, SIDE - dx)
            out = padded(self.L[:, b, :], SIDE)[:, y0:y1, x0:x1]
            src = padded(self.V_[:, b, :], SIDE)[:, y0 + dy:y1 + dy, x0 + dx:x1 + dx]
            if t == LT // 2:
                ins = dve.tensor_scalar(out, src, self.w[:, b, t:t + 1], self.bias[:, b:b + 1], ALU.mult, ALU.add)
            else:
                dve.wait_ge(self.done, self.count - 1)
                ins = dve.scalar_tensor_tensor(out=out, in0=src, scalar=self.w[:, b, t:t + 1], in1=out,
                                               op0=ALU.mult, op1=ALU.add)
            ins.then_inc(self.done, 1)
            self.count += 1
        del self.left[:k]

def qkv_linear(nc, gm_dram, w_dram, b_dram, wl_dram, bl_dram, x3_dram, X, Q, K, V_, local, gn):
    with ExitStack() as stack:
        n = Names(nc, stack, "lin")
        gm = n.sb("group_mean", [P, P])
        w = n.sb("w", [P, 3, CB, C])
        bias = n.sb("bias", [P, 3, CB])
        xn = n.sb("xn", [P, CB, PX])
        ps_gn = n.ps("ps_gn", [P, CB * 2])
        ps = n.ps("ps", [P, 4, CH])
        loaded = n.sem("loaded")
        aside = n.sem("x_aside")
        normed = n.sem("normed")
        done = n.sem("product_done")
        moved = n.sem("moved")
        moved_act = n.sem("moved_by_act")
        work = [(c, 2, ob) for c in range(NCH) for ob in range(CB)]
        work += [(c, m, ob) for c in range(NCH) for ob in range(CB) for m in (0, 1)]
        by_act = [i for i, (c, m, ob) in enumerate(work) if m == 0 or (m == 2 and ob == 0)]
        by_dve = [i for i in range(len(work)) if i not in by_act]

        def wait_moved(eng, i):
            if i in by_act:
                eng.wait_ge(moved_act, by_act.index(i) + 1)
            else:
                eng.wait_ge(moved, by_dve.index(i) + 1)
        with nc.Block() as block:

            @block.sync
            def _(sp):
                for t, d in ((gm[:, :], gm_dram), (w[:, :, :, :], w_dram), (bias[:, :, :], b_dram),
                             (local.w[:, :, :], wl_dram), (local.bias[:, :], bl_dram)):
                    sp.dma_start(t, d).then_inc(loaded, 16)
                for b in range(CB):
                    sp.dma_start(x3_dram[:, b, :], X[:, b, :]).then_inc(aside, 16)
                sp.wait_ge(aside, 16 * CB)

            @block.scalar
            def _(act):
                gn.scalar_std(act)
                act.wait_ge(gn.ready, 1)
                for c in range(NCH):
                    for b in range(CB):
                        act.activation(xn[:, b, c * CH:(c + 1) * CH], X[:, b, c * CH:(c + 1) * CH], ACT.Identity,
                                       scale=gn.scale[:, b:b + 1], bias=gn.shift[:, b:b + 1]).then_inc(normed, 1)
                act.wait_ge(loaded, 16 * 5)
                for i in by_act:
                    c, m, ob = work[i]
                    act.wait_ge(done, i + 1)
                    act.activation((Q, K, V_)[m][:, ob, c * CH:(c + 1) * CH], ps[:, i % 4, :], ACT.Identity,
                                   bias=bias[:, m, ob:ob + 1]).then_inc(moved_act, 1)

            @block.tensor
            def _(pe):
                pe.wait_ge(loaded, 16 * 5)
                gn.tensor_join(pe, ps_gn[:, :], gm[:, :])
                for i, (c, m, ob) in enumerate(work):
                    pe.wait_ge(normed, CB * (c + 1))
                    if i >= 4:
                        wait_moved(pe, i - 4)
                    for b in range(CB):
                        mm = pe.matmul(ps[:, i % 4, :], w[:, m, b, ob * P:(ob + 1) * P], xn[:, b, c * CH:(c + 1) * CH],
                                       start=b == 0, stop=b == CB - 1)
                    mm.then_inc(done, 1)

            @block.vector
            def _(dve):
                gn.vector_affine(dve, ps_gn[:, :])
                dve.wait_ge(loaded, 16 * 5)
                for i in by_dve:
                    c, m, ob = work[i]
                    dve.wait_ge(done, i + 1)
                    out = (Q, K, V_)[m][:, ob, c * CH:(c + 1) * CH]
                    dve.tensor_scalar(out, ps[:, i % 4, :], bias[:, m, ob:ob + 1], KEY_SCALE if m == 1 else 1.0,
                                      ALU.add, ALU.mult).then_inc(moved, 1)
                    if m == 1:
                        if c == 0 and ob == 0:
                            dve.wait_ge(moved_act, by_act.index(CB * NCH - 2) + 1)
                            dve.wait_ge(moved, by_dve.index(CB * NCH - 1) + 1)
                            dve.wait_ge(aside, 16 * CB)
                            dve.wait_ge(normed, CB * NCH)
                        local.steps(dve, LOCAL_BESIDE_LINEAR)

def axial_attention(nc, ident_dram, mask_dram, x3_dram, Q, K, V_, L, local):
    with ExitStack() as stack:
        n = Names(nc, stack, "axial")
        R = 2
        ident = n.sb("ident", [P, P])
        mask = n.sb("mask", [P, 2, HEADS, SIDE])
        turned_v = n.sb("turned_v", [P, TILES, P])
        v1 = n.sb("v1", [P, PX])
        s = n.sb("s", [P, R, CH])
        e = n.sb("e", [P, R, CH])
        pr = n.sb("prob", [P, R, CH])
        pt = n.sb("prob_turned", [P, R, CH])
        mx = n.sb("max", [P, R, 8])
        sm = n.sb("sum", [P, R, 8])
        ps_s = n.ps("ps_s", [P, HPB, CH])
        ps_t = n.ps("ps_t", [P, 2, CH])
        ps_v = n.ps("ps_v", [P, 2, CH])

        loaded = n.sem("loaded")
        scored = n.sem("scored")
        shifted = n.sem("dve_softmax")
        exped = n.sem("exped")
        probs = n.sem("probs")
        turned = n.sem("turned")
        moved = n.sem("moved")
        v_turned = n.sem("v_turned")
        v_moved = n.sem("v_moved")
        product = n.sem("product")
        line = n.sem("lines_moved")
        added = n.sem("lines_added")

        passes = [(b, d) for b in range(CB) for d in range(2)]
        items = [(p, u, j) for p in range(len(passes)) for u in range(UNITS) for j in range(HPB)]
        NI = UNITS * HPB

        def group_line(u, g, r):
            return u * UNIT + 4 * (g // 2) + 2 * r + g % 2

        per_item = 5
        at_pass = 14

        with nc.Block() as block:

            @block.sync
            def _(sp):
                for t, d in ((ident[:, :], ident_dram), (mask[:, :, :, :], mask_dram)):
                    sp.dma_start(t, d).then_inc(loaded, 16)
                sp.wait_ge(scored, len(items))
                sp.dma_start(K[:, :, :], x3_dram).then_inc(loaded, 16)
                sp.wait_ge(loaded, 48)

            @block.tensor
            def _(pe):
                def scores(i):
                    p, u, j = items[i]
                    b, d = passes[p]
                    if i >= HPB:
                        pe.wait_ge(shifted, 5 * (i - HPB) + 1)
                    hd = slice(j * HD, (j + 1) * HD)
                    for g in range(8):
                        for r in range(2):
                            at = group_line(u, g, r)
                            px = slice(at * SIDE, (at + 1) * SIDE) if d == 0 else slice(at, PX, SIDE)
                            mm = pe.matmul(ps_s[r * SIDE:(r + 1) * SIDE, j, g * SIDE:(g + 1) * SIDE],
                                           Q[hd, b, px], K[hd, b, px], start=True, stop=True)
                    mm.then_inc(scored, 1)

                def turn_v(p):
                    b, d = passes[p]
                    src = V_[:, b, :] if d == 0 else v1[:, :]
                    if d == 1:
                        pe.wait_ge(line, 2 * UNITS * (b + 1))
                    for g in range(TILES // 4):
                        k = p * (TILES // 4) + g
                        pe.wait_ge(moved, p * NI) if g == 0 and p else None
                        if g >= 2:
                            pe.wait_ge(v_moved, k - 1)
                        for t in range(4):
                            mm = pe.transpose(ps_t[:, g % 2, t * P:(t + 1) * P],
                                              src[:, (4 * g + t) * P:(4 * g + t + 1) * P], ident[:, :])
                        mm.then_inc(v_turned, 1)
                    pe.wait_ge(v_moved, (p + 1) * (TILES // 4))

                def turn(i):
                    pe.wait_ge(probs, i + 1)
                    if i >= 2:
                        pe.wait_ge(moved, i - 1)
                    for t in range(4):
                        mm = pe.transpose(ps_t[:, i % 2, t * P:(t + 1) * P], pr[:, i % R, t * P:(t + 1) * P], ident[:, :])
                    mm.then_inc(turned, 1)

                def values(i):
                    p, u, j = items[i]
                    b, d = passes[p]
                    pe.wait_ge(moved, i + 1)
                    if j == 0:
                        units = p * UNITS + u
                        rows = sum(1 for q in range(units) if passes[q // UNITS][1] == 0)
                        if rows:
                            pe.wait_ge(line, 2 * rows)
                        if units - rows:
                            pe.wait_ge(added, 2 * (units - rows))
                    for g in range(8):
                        for r in range(2):
                            at = group_line(u, g, r)
                            k = slice((at % 2) * SIDE, (at % 2 + 1) * SIDE)
                            slot = (at % UNIT) // 2
                            mm = pe.matmul(ps_v[j * HD:(j + 1) * HD, at % 2, slot * SIDE:(slot + 1) * SIDE],
                                           turned_v[k, at // 2, j * HD:(j + 1) * HD],
                                           pt[k, i % R, (g // 2) * P + r * SIDE:(g // 2) * P + (r + 1) * SIDE],
                                           start=True, stop=True)
                    mm.then_inc(product, 1)

                pe.wait_ge(loaded, 32)
                for p in range(len(passes)):
                    if passes[p][1]:
                        turn_v(p)
                        scores(p * NI)
                        scores(p * NI + 1)
                    else:
                        scores(p * NI)
                        scores(p * NI + 1)
                        turn_v(p)
                    for i in range(p * NI, (p + 1) * NI):
                        if i + 2 < (p + 1) * NI:
                            scores(i + 2)
                        turn(i)
                        if i > p * NI:
                            values(i - 1)
                    values((p + 1) * NI - 1)

            @block.scalar
            def _(act):
                def exp(i):
                    act.wait_ge(shifted, 5 * i + 3)
                    if i >= R:
                        act.wait_ge(probs, i - R + 1)
                    act.activation(e[:, i % R, :], s[:, i % R, :], ACT.Exp).then_inc(exped, 1)

                def move(i):
                    act.wait_ge(turned, i + 1)
                    if i >= R:
                        act.wait_ge(product, i - R + 1)
                    act.activation(pt[:, i % R, :], ps_t[:, i % 2, :], ACT.Identity).then_inc(moved, 1)

                def lines(i):
                    p, u, j = items[i]
                    act.wait_ge(product, i + 1)
                    for par in range(2):
                        dst = v1[:, :].rearrange("p (x y) -> p y x", y=SIDE)[:, u * UNIT + par:(u + 1) * UNIT:2, :]
                        act.activation(dst, ps_v[:, par, :].rearrange("p (y x) -> p y x", x=SIDE), ACT.Identity).then_inc(line, 1)

                for p in range(len(passes)):
                    b, d = passes[p]
                    if p:
                        act.wait_ge(product, p * NI)
                    for g in range(TILES // 4):
                        act.wait_ge(v_turned, p * (TILES // 4) + g + 1)
                        act.activation(turned_v[:, 4 * g:4 * g + 4, :].rearrange("p t c -> p (t c)"), ps_t[:, g % 2, :],
                                       ACT.Identity).then_inc(v_moved, 1)
                    for i in range(p * NI, (p + 1) * NI):
                        exp(i)
                        if i > p * NI:
                            move(i - 1)
                            if items[i - 1][2] == 0 and d == 0 and i - 1 > p * NI:
                                lines(i - 2)
                    move((p + 1) * NI - 1)
                    if d == 0:
                        lines((p + 1) * NI - 1)

            @block.gpsimd
            def _(pool):
                for i in range(len(items)):
                    pool.wait_ge(shifted, 5 * i + 5)
                    if i >= R:
                        pool.wait_ge(turned, i - R + 1)
                    pool.tensor_tensor(pr[:, i % R, :].rearrange("p (g k) -> p g k", k=SIDE),
                                       e[:, i % R, :].rearrange("p (g k) -> p g k", k=SIDE),
                                       sm[:, i % R, :].unsqueeze(2).to_broadcast([P, 8, SIDE]), ALU.mult).then_inc(probs, 1)

            @block.vector
            def _(dve):
                def first(i):
                    p, u, j = items[i]
                    b, d = passes[p]
                    sv = s[:, i % R, :].rearrange("p (g k) -> p g k", k=SIDE)
                    dve.wait_ge(scored, i + 1)
                    if i >= R:
                        dve.wait_ge(exped, i - R + 1)
                    dve.tensor_tensor(sv, ps_s[:, j, :].rearrange("p (g k) -> p g k", k=SIDE),
                                      mask[:, d, b * HPB + j, :].unsqueeze(1).to_broadcast([P, 8, SIDE]), ALU.add).then_inc(shifted, 1)
                    local.steps(dve, 1)
                    dve.wait_ge(shifted, 5 * i + 1)
                    dve.reduce_max(mx[:, i % R, :], sv, AX.X).then_inc(shifted, 1)
                    local.steps(dve, 1)
                    dve.wait_ge(shifted, 5 * i + 2)
                    dve.tensor_tensor(sv, sv, mx[:, i % R, :].unsqueeze(2).to_broadcast([P, 8, SIDE]), ALU.subtract).then_inc(shifted, 1)

                def second(i):
                    dve.wait_ge(exped, i + 1)
                    if i >= R:
                        dve.wait_ge(probs, i - R + 1)
                    dve.reduce_sum(sm[:, i % R, :], e[:, i % R, :].rearrange("p (g k) -> p g k", k=SIDE), AX.X).then_inc(shifted, 1)
                    local.steps(dve, 1)
                    dve.wait_ge(shifted, 5 * i + 4)
                    dve.reciprocal(sm[:, i % R, :], sm[:, i % R, :]).then_inc(shifted, 1)

                def add_lines(i):
                    p, u, j = items[i]
                    b, d = passes[p]
                    local.steps(dve, local.centres_left())
                    dve.wait_ge(local.done, local.count)
                    dve.wait_ge(product, i + 1)
                    for par in range(2):
                        dst = L[:, b, :].rearrange("p (y x) -> p x y", x=SIDE)[:, u * UNIT + par:(u + 1) * UNIT:2, :]
                        dve.tensor_tensor(dst, ps_v[:, par, :].rearrange("p (x y) -> p x y", y=SIDE), dst, ALU.add).then_inc(added, 1)
                    dve.wait_ge(added, 2 * (b * UNITS + u + 1))

                dve.wait_ge(loaded, 32)
                for p in range(len(passes)):
                    b, d = passes[p]
                    for i in range(p * NI, (p + 1) * NI):
                        if i == p * NI:
                            local.steps(dve, at_pass)
                        first(i)
                        local.steps(dve, per_item - 3)
                        second(i)
                        if d == 1 and i - p * NI >= HPB and (i - p * NI) % HPB == 1:
                            add_lines(i - 2)
                    if d == 1:
                        add_lines((p + 1) * NI - 1)
                local.steps(dve, len(local.left))

def output(nc, w_dram, b_dram, out_dram, L, x, y):
    with ExitStack() as stack:
        n = Names(nc, stack, "out")
        w = n.sb("w", [P, CB, C])
        bias = n.sb("bias", [P, CB])
        ps = n.ps("ps", [P, 4, CH])
        loaded = n.sem("loaded")
        done = n.sem("product_done")
        ready = n.sem("ready")
        stored = n.sem("stored")
        work = [(c, ob) for c in range(NCH) for ob in range(CB)]
        with nc.Block() as block:

            @block.sync
            def _(sp):
                sp.dma_start(w[:, :, :], w_dram).then_inc(loaded, 16)
                sp.dma_start(bias[:, :], b_dram).then_inc(loaded, 16)
                for c in range(0, NCH, 2):
                    sp.wait_ge(ready, 2 * (c + 2))
                    sp.dma_start(out_dram.rearrange("(b p) n -> p b n", p=P)[:, :, c * CH:(c + 2) * CH],
                                 y[:, :, c * CH:(c + 2) * CH]).then_inc(stored, 16)
                sp.wait_ge(stored, 16 * (NCH // 2))

            @block.tensor
            def _(pe):
                pe.wait_ge(loaded, 32)
                for i, (c, ob) in enumerate(work):
                    if i >= 4:
                        pe.wait_ge(ready, i - 3)
                    for b in range(CB):
                        mm = pe.matmul(ps[:, i % 4, :], w[:, b, ob * P:(ob + 1) * P], L[:, b, c * CH:(c + 1) * CH],
                                       start=b == 0, stop=b == CB - 1)
                    mm.then_inc(done, 1)

            @block.vector
            def _(dve):
                dve.wait_ge(loaded, 32)
                for i, (c, ob) in enumerate(work):
                    dve.wait_ge(done, i + 1)
                    at = slice(c * CH, (c + 1) * CH)
                    dve.scalar_tensor_tensor(out=y[:, ob, at], in0=ps[:, i % 4, :], scalar=bias[:, ob:ob + 1],
                                             in1=x[:, ob, at], op0=ALU.add, op1=ALU.add).then_inc(ready, 1)

def conv_preact_kernel(nc, ins, out):
    dw = nc.dram_tensor("depthwise_out", (2 * CB, P, PX), F32, kind="Internal").ap()
    parts = nc.dram_tensor("unit_parts", (2, 2, C, PX), F16, kind="Internal").ap()
    vt = nc.dram_tensor("v_turned", (HEADS, P, MT * VW), F32, kind="Internal").ap()
    sums = nc.dram_tensor("attention_sums", (NG, VW, NB), F32, kind="Internal").ap()
    table = nc.dram_tensor("corner_table", (TAB * TAB, 4 * C), F32, kind="Internal").ap()
    x3 = nc.dram_tensor("image3", (P, CB, PX), F32, kind="Internal").ap()

    with ExitStack() as stack:
        n = Names(nc, stack, "padded")
        XH = n.sb("x_high", [P, CB, PAD5 * PAD5], F32R)
        XL = n.sb("x_low", [P, CB, PAD5 * PAD5], F32R)
        norm_and_split(nc, ins["x"], ins["group_mean"], XH, XL)
        conv_qkv(nc, [ins["w_q"], ins["w_k"], ins["w_v"]], ins["w_depthwise"], ins["head_sum"],
                 ins["identity"], dw, parts, vt, XH, XL)
    with ExitStack() as stack:
        n = Names(nc, stack, "image")
        X = n.sb("x", [P, CB, PX])
        attention(nc, parts, vt, ins["temperature"], ins["x"], sums, X)
        gn = [GroupNorm(Names(nc, stack, f"layer{i}")) for i in (1, 2, 3)]
        project(nc, sums, ins["w_project"], ins["spread"], X, gn[0])
        covariance_gate(nc, ins["group_mean"], ins["eye"], ins["w_gate1"], ins["b_gate1"], ins["w_gate2"],
                        ins["b_gate2"], X, gn[0], gn[1])
        with ExitStack() as inner:
            n = Names(nc, inner, "corners")
            IDX = n.sb("index", [P, TILES * TAPS], I32)
            CW = n.sb("weight", [P, TILES * TAPS, 4])
            offsets_and_table(nc, ins["group_mean"], ins["identity"], ins["w_offset"], ins["b_offset"],
                              ins["positions"], table, X, IDX, CW, gn[1])
            deform(nc, ins["identity"], ins["w_deform"], table, X, IDX, CW, gn[2])
        with ExitStack() as inner:
            n = Names(nc, inner, "axial_in")
            Q = n.sb("q", [P, CB, PX])
            K = n.sb("k", [P, CB, PX])
            V = n.sb("v", [P, CB, PX])
            local = LocalConv(n, V, X)
            qkv_linear(nc, ins["group_mean"], ins["w_linear"], ins["b_linear"], ins["w_local"], ins["b_local"],
                       x3, X, Q, K, V, local, gn[2])
            axial_attention(nc, ins["identity"], ins["masks"], x3, Q, K, V, X, local)
            output(nc, ins["w_out"], ins["b_out"], out, X, K, Q)

def _laid_out(a):
    def conv(w):
        taps = w.shape[2] * w.shape[3]
        return w.reshape(CB, P, CB, P, taps).transpose(0, 2, 3, 4, 1).reshape(CB, CB, P, taps * P)

    def linear(w):
        return w.reshape(CB, P, C).transpose(1, 0, 2)

    def channel(v):
        return v.reshape(CB, P).T

    tile, part, tap = np.meshgrid(np.arange(TILES), np.arange(P), np.arange(TAPS))
    positions = np.stack([2 * tile + part // SIDE + tap // 3, part % SIDE + tap % 3], 1)
    masks = np.stack([a["L3_conv_mask_w"], a["L3_conv_mask_h"]], 0).transpose(2, 0, 1, 3)
    spread = np.zeros((NG, NNB * CB, P), np.float32)
    for g in range(NG):
        head, nb = divmod(g, NNB)
        spread[g, nb * CB + head // HPB, head % HPB * HD:(head % HPB + 1) * HD] = 1.0
    ins = {
        "spread": spread,
        "x": a["x"].reshape(PX, C).T,
        "group_mean": np.kron(np.eye(P // GROUP), np.full((GROUP, GROUP), 1.0 / GROUP)).astype(np.float32),
        "head_sum": np.kron(np.eye(HPB), np.ones((HD, HD))).astype(np.float32),
        "identity": np.eye(P, dtype=np.float32),
        "eye": linear(np.eye(C, dtype=np.float32)),
        "positions": positions.reshape(P, 2, TILES * TAPS).astype(np.float32),
        "w_q": conv(a["L0_conv_W1"]), "w_k": conv(a["L0_conv_W3"]), "w_v": conv(a["L0_conv_W5"]),
        "w_depthwise": a["L0_conv_Wdw"].reshape(3 * CB, P, 9).transpose(1, 0, 2),
        "temperature": np.broadcast_to(np.repeat(a["L0_conv_temperature"].reshape(HEADS), NNB)[None], (P, NG)),
        "w_project": linear(a["L0_conv_Wproj"][:, :, 0, 0].T),
        "w_gate1": linear(a["L1_conv_w1"][1, 1]), "b_gate1": channel(a["L1_conv_b1"]),
        "w_gate2": linear(a["L1_conv_w2"][1, 1]), "b_gate2": channel(a["L1_conv_b2"]),
        "w_offset": a["L2_conv_offset_w"].reshape(TAPS, CB, P, OM).transpose(2, 1, 0, 3).reshape(P, CB, TAPS * OM),
        "b_offset": a["L2_conv_offset_b"].reshape(OM, 1),
        "w_deform": a["L2_conv_dcn_weight"].reshape(C, CB, P, TAPS).transpose(2, 1, 3, 0),
        "w_linear": np.stack([linear(a["L3_conv_" + k].T) for k in ("Wq", "Wk", "Wv")], 1),
        "b_linear": np.stack([channel(a["L3_conv_" + k]) for k in ("bq", "bk", "bv")], 1),
        "masks": np.concatenate([masks, masks], 0),
        "w_local": a["L3_conv_Wlepe"].reshape(LT, CB, P).transpose(2, 1, 0), "b_local": channel(a["L3_conv_blepe"]),
        "w_out": linear(a["L3_conv_Wo"].T), "b_out": channel(a["L3_conv_bo"]),
    }
    return {k: np.ascontiguousarray(v) for k, v in ins.items()}

def kernel(**inputs):
    from concourse import bacc
    from concourse.bass_utils import run_bass_kernel_spmd

    nc = bacc.Bacc("TRN2", target_bir_lowering=False, num_devices=1)
    arrays = _laid_out({k: np.asarray(v) for k, v in inputs.items()})
    ins = {k: nc.dram_tensor(f"in_{k}", v.shape, mybir.dt.from_np(v.dtype), kind="ExternalInput").ap()
           for k, v in arrays.items()}
    out = nc.dram_tensor("out", (C, PX), F32, kind="ExternalOutput").ap()
    conv_preact_kernel(nc, ins, out)
    result = run_bass_kernel_spmd(nc, [{f"in_{k}": v for k, v in arrays.items()}], core_ids=[0])
    return result.results[0]["out"].T.reshape(1, SIDE, SIDE, C)
```

```python
import numpy as np
import concourse.bass as bass
from concourse import mybir
from contextlib import ExitStack

F32, F32R, F16 = mybir.dt.float32, mybir.dt.float32r, mybir.dt.float16
I32 = mybir.dt.int32
ALU = mybir.AluOpType
ACT = mybir.ActivationFunctionType
AX = mybir.AxisListType
ds = bass.ds

P = 128
SIDE = 64
PX = SIDE * SIDE
C = 256
CB = C // P
GROUP = 8
CH = 512
ROWS = CH // SIDE
NCH = PX // CH
HEADS, HD = 8, 32
HPB = P // HD
PAD5 = SIDE + 4
PAD3 = SIDE + 2

class Names:

    def __init__(self, nc, stack, stage):
        self.nc, self.stack, self.stage = nc, stack, stage

    def sb(self, name, shape, dt=F32):
        return self.stack.enter_context(self.nc.sbuf_tensor(f"{self.stage}_{name}", shape, dt))

    def ps(self, name, shape, dt=F32):
        return self.stack.enter_context(self.nc.psum_tensor(f"{self.stage}_{name}", shape, dt))

    def sem(self, name):
        return self.stack.enter_context(self.nc.semaphore(f"{self.stage}_{name}"))

def load_ahead(sp, pairs, sem):
    for tile, dram in pairs:
        sp.dma_start(tile, dram).then_inc(sem, 16)

class GroupNorm:

    def __init__(self, n, eps=1e-5):
        self.eps = eps
        self.stats = n.sb("gn_stats", [P, CB, NCH, 6])
        self.mv = n.sb("gn_mv", [P, CB, 2])
        self.m12 = n.sb("gn_m12", [P, CB, 2])
        self.g12 = n.sb("gn_g12", [P, CB, 2])
        self.var = n.sb("gn_var", [P, CB])
        self.std = n.sb("gn_std", [P, CB])
        self.scale = n.sb("gn_scale", [P, CB])
        self.shift = n.sb("gn_shift", [P, CB])
        self.step = n.sem("gn_step")
        self.moments = n.sem("gn_moments")
        self.joined = n.sem("gn_joined")
        self.var_ready = n.sem("gn_var_ready")
        self.std_ready = n.sem("gn_std_ready")
        self.ready = n.sem("gn_ready")

        self.steps = 0

    def up(self, ins):
        ins.then_inc(self.step, 1)
        self.steps += 1

    def chunk_stats(self, dve, x, b, c):
        self.up(dve.bn_stats(self.stats[:, b, c, :], x[:, b, c * CH:(c + 1) * CH]))

    def channel_moments(self, dve):
        dve.wait_ge(self.step, self.steps)
        for b in range(CB):
            self.up(dve.bn_aggr(self.mv[:, b, :], self.stats[:, b, :, :].rearrange("p c s -> p (c s)")))

    def moments_of_affine(self, dve, other, scale, shift):
        self.up(dve.tensor_tensor(self.mv[:, :, 0], other.mv[:, :, 0], scale, ALU.mult))
        self.up(dve.tensor_tensor(self.mv[:, :, 1], other.mv[:, :, 1], scale, ALU.mult))
        dve.wait_ge(self.step, self.steps)
        self.up(dve.tensor_tensor(self.mv[:, :, 0], self.mv[:, :, 0], shift, ALU.add))
        self.up(dve.tensor_tensor(self.mv[:, :, 1], self.mv[:, :, 1], scale, ALU.mult))

    def vector_moments(self, dve):
        dve.wait_ge(self.step, self.steps)
        dve.tensor_copy(self.m12[:, :, 0], self.mv[:, :, 0]).then_inc(self.moments, 1)
        self.up(dve.tensor_tensor(self.var[:, :], self.mv[:, :, 0], self.mv[:, :, 0], ALU.mult))
        dve.wait_ge(self.step, self.steps)
        dve.tensor_tensor(self.m12[:, :, 1], self.var[:, :], self.mv[:, :, 1], ALU.add).then_inc(self.moments, 1)

    def tensor_join(self, pe, ps, group_mean):
        pe.wait_ge(self.moments, 2)
        pe.matmul(ps, group_mean, self.m12[:, :, :].rearrange("p b s -> p (b s)"),
                  start=True, stop=True).then_inc(self.joined, 1)

    def vector_affine(self, dve, ps):
        dve.wait_ge(self.joined, 1)
        self.up(dve.tensor_copy(self.g12[:, :, :].rearrange("p b s -> p (b s)"), ps))
        dve.wait_ge(self.step, self.steps)
        self.up(dve.tensor_tensor(self.std[:, :], self.g12[:, :, 0], self.g12[:, :, 0], ALU.mult))
        dve.wait_ge(self.step, self.steps)
        self.up(dve.tensor_tensor(self.var[:, :], self.g12[:, :, 1], self.std[:, :], ALU.subtract))
        dve.wait_ge(self.step, self.steps)
        dve.tensor_scalar(self.var[:, :], self.var[:, :], self.eps, None, ALU.add).then_inc(self.var_ready, 1)
        dve.wait_ge(self.std_ready, 1)
        self.up(dve.reciprocal(self.scale[:, :], self.std[:, :]))
        dve.wait_ge(self.step, self.steps)
        dve.scalar_tensor_tensor(out=self.shift[:, :], in0=self.g12[:, :, 0], scalar=-1.0, in1=self.scale[:, :],
                                 op0=ALU.mult, op1=ALU.mult).then_inc(self.ready, 1)

    def scalar_std(self, act):
        act.wait_ge(self.var_ready, 1)
        act.activation(self.std[:, :], self.var[:, :], ACT.Sqrt).then_inc(self.std_ready, 1)

def apart(eng, sem):
    eng.wait_ge(sem, 1)

def padded(t, side):
    return t.rearrange("p (y x) -> p y x", x=side)

PIECE = 5
KERNELS = (1, 3, 5)
BLOCKS = ((0, 0), (1, 0), (1, 1), (0, 1), (2, 0), (2, 1))

class ConvWeights:
    RAW = 3

    def __init__(self, n, w_dram):
        self.w_dram = w_dram
        self.high = n.sb("w_high", [P, 3, 25 * P], F32R)
        self.low = n.sb("w_low", [P, 3, 25 * P], F32R)
        self.raw = n.sb("w_raw", [P, self.RAW, PIECE * P])
        self.raw_loaded = [n.sem(f"raw_loaded{i}") for i in range(self.RAW)]
        self.high_ready = n.sem("w_high_ready")
        self.low_ready = n.sem("w_low_ready")
        self.units = [(blk, ib) for blk in range(len(BLOCKS)) for ib in range(CB)]
        self.place = [(0, 18, None), (0, 19, None), (0, 0, None), (0, 9, None), (1, 0, None), (1, 9, None),
                      (1, 18, None), (1, 19, None), (2, 0, None), (0, 0, 1), (1, 0, 3), (2, 0, 4)]
        self.pieces = []
        for u, (blk, ib) in enumerate(self.units):
            taps = KERNELS[BLOCKS[blk][0]] ** 2
            for t0 in range(0, taps, PIECE):
                self.pieces.append((u, t0, min(PIECE, taps - t0)))
        self.early = sum(u < 2 * CB for u, _, _ in self.pieces)

    def pieces_upto(self, blk, ib, t):
        return [(u, t0) for u, t0, _ in self.pieces].index((blk * CB + ib, t)) + 1

    def load(self, sp, first, end):
        for i in range(first, end):
            u, t0, nt = self.pieces[i]
            blk, ib = self.units[u]
            k, ob = BLOCKS[blk]
            if i >= self.RAW:
                sp.wait_ge(self.low_ready, i + 1 - self.RAW)
            sp.dma_start(self.raw[:, i % self.RAW, 0:nt * P],
                         self.w_dram[k][ob, ib, :, t0 * P:(t0 + nt) * P]).then_inc(self.raw_loaded[i % self.RAW], 16)

    def split(self, pool, first, end, chunk_done=None):
        for i in range(first, end):
            u, t0, nt = self.pieces[i]
            s, col, before = self.place[u]
            if t0 == 0 and before is not None:
                pool.wait_ge(chunk_done, NCH * (before + 1))
            at = slice((col + t0) * P, (col + t0 + nt) * P)
            pool.wait_ge(self.raw_loaded[i % self.RAW], 16 * (i // self.RAW + 1))
            w = self.raw[:, i % self.RAW, 0:nt * P]
            pool.tensor_copy(self.high[:, s, at], w).then_inc(self.high_ready, 1)
            pool.wait_ge(self.high_ready, i + 1)
            pool.tensor_tensor(self.low[:, s, at], w, self.high[:, s, at].bitcast(F32),
                               ALU.subtract).then_inc(self.low_ready, 1)

def norm_and_split(nc, x_dram, group_mean_dram, XH, XL, weights):
    with ExitStack() as stack:
        n = Names(nc, stack, "norm0")
        x = n.sb("x", [P, CB, PX])
        gm = n.sb("group_mean", [P, P])
        xn = n.sb("xn", [P, 2, CH])
        ps = n.ps("ps", [P, CB * 2])
        gn = GroupNorm(n)
        loads = [n.sem(f"x_loaded{i}") for i in range(2 * CB)]
        gm_loaded = n.sem("gm_loaded")
        borders = n.sem("borders")
        whole = n.sem("whole_ready")
        high = n.sem("high_ready")
        low = n.sem("low_ready")
        half = PX // 2
        with nc.Block() as block:

            @block.sync
            def _(sp):
                sp.dma_start(gm[:, :], group_mean_dram).then_inc(gm_loaded, 16)
                for b in range(CB):
                    for h in range(2):
                        sp.dma_start(x[:, b, h * half:(h + 1) * half],
                                     x_dram[b * P:(b + 1) * P, h * half:(h + 1) * half]).then_inc(loads[2 * b + h], 16)
                weights.load(sp, 0, weights.early)

            @block.gpsimd
            def _(pool):
                for t in (XH, XL):
                    pool.memset(t[:, :, :].bitcast(F32), 0.0).then_inc(borders, 1)
                weights.split(pool, 0, weights.early)

            @block.vector
            def _(dve):
                for b in range(CB):
                    for c in range(NCH):
                        dve.wait_ge(loads[2 * b + c // (NCH // 2)], 16)
                        gn.chunk_stats(dve, x, b, c)
                gn.channel_moments(dve)
                gn.vector_moments(dve)
                gn.vector_affine(dve, ps[:, :])
                dve.wait_ge(borders, 2)
                pieces = [(b, c) for b in range(CB) for c in range(NCH)]

                def make_whole(i):
                    b, c = pieces[i]
                    if i >= 2:
                        dve.wait_ge(low, i - 1)
                    dve.tensor_scalar(xn[:, i % 2, :], x[:, b, c * CH:(c + 1) * CH], gn.scale[:, b:b + 1],
                                      gn.shift[:, b:b + 1], ALU.mult, ALU.add).then_inc(whole, 1)

                dve.wait_ge(gn.ready, 1)
                make_whole(0)
                for i, (b, c) in enumerate(pieces):
                    if i + 1 < len(pieces):
                        make_whole(i + 1)
                    dve.wait_ge(whole, i + 1)
                    dve.wait_ge(high, i + 1)
                    y = 2 + c * ROWS
                    dst = padded(XL[:, b, :], PAD5)[:, y:y + ROWS, 2:2 + SIDE]
                    hi = padded(XH[:, b, :], PAD5)[:, y:y + ROWS, 2:2 + SIDE]
                    dve.tensor_tensor(dst, xn[:, i % 2, :].rearrange("p (y x) -> p y x", x=SIDE),
                                      hi.bitcast(F32), ALU.subtract).then_inc(low, 1)

            @block.tensor
            def _(pe):
                pe.wait_ge(gm_loaded, 16)
                gn.tensor_join(pe, ps[:, :], gm[:, :])

            @block.scalar
            def _(act):
                gn.scalar_std(act)
                act.wait_ge(gn.ready, 1)
                act.wait_ge(borders, 2)
                for b in range(CB):
                    for c in range(NCH):
                        src = x[:, b, c * CH:(c + 1) * CH]
                        y = 2 + c * ROWS
                        dst = padded(XH[:, b, :], PAD5)[:, y:y + ROWS, 2:2 + SIDE]
                        act.activation(dst, src.rearrange("p (y x) -> p y x", x=SIDE), ACT.Identity,
                                       scale=gn.scale[:, b:b + 1], bias=gn.shift[:, b:b + 1]).then_inc(high, 1)

TC = CH // P
VW = 3 * HD
UNIT_SCALE = 64.0

def conv_qkv(nc, weights, wdw_dram, head_sum_dram, ident_dram, dw_dram, parts_dram, vt_dram, XH, XL):
    with ExitStack() as stack:
        n = Names(nc, stack, "conv")
        co = n.sb("conv_out", [P, PAD3 * PAD3])
        cov = padded(co[:, :], PAD3)
        acc = n.sb("dw_out", [P, 2, CH])
        wdw = n.sb("wdw", [P, 6, 9])
        head_sum_raw = n.sb("head_sum_raw", [P, P])
        head_sum = n.sb("head_sum", [P, P], F32R)
        qd = n.sb("qk_in", [P, CB, CH])
        sqh = n.sb("squares_high", [P, CB, CH], F32R)
        sql = n.sb("squares_low", [P, CB, CH], F32R)
        nrm = n.sb("norms", [P, CB, CH])
        unit = n.sb("unit", [P, CH])
        ident = n.sb("ident", [P, P])
        vt = n.sb("v_turned", [P, HPB, TC, VW], F32R)
        pt = n.ps("pt", [P, TC, P])
        half = n.sb("halves", [P, CB, 2, CH], F16)
        pc = n.ps("pc", [P, 2, CH])
        pn = n.ps("pn", [P, CB, CH])

        consts = n.sem("consts_loaded")
        chunk_done = n.sem("conv_chunk_done")
        moved = n.sem("conv_chunk_moved")
        border = n.sem("border_zeroed")
        tap = n.sem("dw_tap")
        stored = [n.sem(f"dw_stored{i}") for i in range(2)]
        qk_loaded = [n.sem(f"qk_loaded{i}") for i in range(CB)]
        squared = n.sem("squared")
        square_low = n.sem("square_low_ready")
        summed = n.sem("summed")
        rooted = n.sem("rooted")
        nstep = n.sem("norm_step")
        half_stored = [n.sem(f"half_stored{i}") for i in range(CB)]
        STEPS = 5
        DW = 2 * 9
        v_turned = n.sem("v_turned")
        v_high = n.sem("v_high_ready")
        v_low = n.sem("v_low_ready")
        v_stored = n.sem("v_stored")

        blocks = BLOCKS
        V0 = len(blocks) - CB

        def channel_block(blk):
            return blocks[blk][0] * CB + blocks[blk][1]

        def v_part(lo):
            return vt[:, :, :, lo * HD:(lo + 1) * HD].rearrange("p h m c -> p m h c")

        def steps(eng, step):
            step(0)
            step(1)
            with eng.Fori(0, NCH // 2 - 1) as i:
                for u in range(2):
                    step(i * 2 + (2 + u), u)

        with nc.Block() as block:

            @block.sync
            def _(sp):
                sp.dma_start(wdw[:, :, :], wdw_dram).then_inc(consts, 16)
                sp.dma_start(head_sum_raw[:, :], head_sum_dram).then_inc(consts, 16)
                sp.dma_start(ident[:, :], ident_dram).then_inc(consts, 16)
                weights.load(sp, weights.early, len(weights.pieces))

            @block.gpsimd
            def _(pool):
                weights.split(pool, weights.early, len(weights.pieces), chunk_done)

            @block.tensor
            def _(pe):
                def conv(blk, c, slot):
                    k, ob = blocks[blk]
                    side = KERNELS[k]
                    off = 2 - side // 2
                    if blk or not isinstance(c, int) or c >= 2:
                        pe.wait_ge(moved, c + (blk * NCH - 1))
                    first = True
                    for ib in range(CB):
                        s, col, _ = weights.place[blk * CB + ib]
                        for t in range(side * side):
                            if isinstance(c, int) and c == 0 and t % PIECE == 0:
                                pe.wait_ge(weights.low_ready, weights.pieces_upto(blk, ib, t))
                            y, x = off + t // side, off + t % side
                            for w, xs in ((weights.high, XH), (weights.high, XL), (weights.low, XH)):
                                last = ib == CB - 1 and t == side * side - 1 and w is weights.low
                                mm = pe.matmul(pc[:, slot, :], w[:, s, (col + t) * P:(col + t + 1) * P],
                                               padded(xs[:, ib, :], PAD5)[:, ds(c * ROWS + y, ROWS), x:x + SIDE],
                                               start=first, stop=last)
                                first = False
                        if k == 2 and ib == (1 if blk == V0 and isinstance(c, int) and c == 0 else 0):
                            head_sums(ob, c)
                    mm.then_inc(chunk_done, 1)

                def head_sums(which, j):
                    for a in range(CB):
                        m = j * CB + (which * NCH * CB + a)
                        pe.wait_ge(square_low, m + 1)
                        pe.matmul(pn[:, a, :], head_sum[:, :], sqh[:, a, :], start=True, stop=False)
                        pe.matmul(pn[:, a, :], head_sum[:, :], sql[:, a, :], start=False, stop=True).then_inc(summed, 1)

                def turn_v(vi, slot):
                    pe.wait_ge(tap, (vi + (V0 * NCH + 1)) * DW)
                    pe.wait_ge(v_low, vi + 1)
                    for j in range(TC):
                        mm = pe.transpose(pt[:, j, :], acc[:, slot, j * P:(j + 1) * P], ident[:, :])
                    mm.then_inc(v_turned, 1)

                for blk, (k, ob) in enumerate(blocks):
                    if blk == V0:
                        pe.wait_ge(consts, 48)
                        pe.wait_ge(border, 2)

                    def step(c, u=None):
                        conv(blk, c, c if u is None else u)
                        if k == 2 and (ob or not isinstance(c, int)):
                            turn_v(c + (ob * NCH - 2), c if u is None else u)
                    steps(pe, step)
                for vi in range(CB * NCH - 2, CB * NCH):
                    turn_v(vi, vi % 2)

            @block.scalar
            def _(act):
                def move(blk, c, slot):
                    act.wait_ge(chunk_done, c + (blk * NCH + 1))
                    if blk:
                        act.wait_ge(tap, (c + ((blk - 1) * NCH + 2)) * DW)
                    apart(act, border)
                    act.activation(cov[:, ds(c * ROWS + 1, ROWS), 1:1 + SIDE],
                                   pc[:, slot, :].rearrange("p (y x) -> p y x", x=SIDE),
                                   ACT.Identity).then_inc(moved, 1)

                def store(blk, c, slot):
                    act.wait_ge(tap, (c + (blk * NCH + 1)) * DW)
                    act.dma_start(dw_dram[channel_block(blk), :, ds(c * CH, CH)], acc[:, slot, :]).then_inc(stored[slot], 16)

                def store_halves(which, j):
                    for a in range(CB):
                        m = j * CB + (which * NCH * CB + a)
                        act.wait_ge(nstep, (m + 1) * STEPS)
                        act.dma_start(parts_dram[1 - which, :, a * P:(a + 1) * P, ds(j * CH, CH)].rearrange("s p n -> p s n"),
                                      half[:, a, :, :]).then_inc(half_stored[a], 16)

                def split_v(ob, g, odd):
                    vi = g + ob * NCH
                    out = vt_dram.rearrange("(b h) p n -> b h p n", b=CB)
                    act.wait_ge(v_turned, vi + 1)
                    act.wait_ge(v_stored, (vi + 1) * 16)
                    src = pt[:, :, :].rearrange("p m (h c) -> p m h c", c=HD)
                    for j0, j1, plain in ((0, 2, False), (2, 3, True), (3, 4, False)) if odd else ((0, TC, False),):
                        dst = v_part(0)[:, j0:j1]
                        ins = act.activation(dst.bitcast(F32) if plain else dst, src[:, j0:j1], ACT.Identity)
                    ins.then_inc(v_high, 1)
                    act.wait_ge(v_low, vi + 2)
                    act.dma_start(out[ob, :, :, ds(g * (TC * VW), TC * VW)].rearrange("h p n -> p h n"),
                                  vt[:, :, :, :].bitcast(F32).rearrange("p h m c -> p h (m c)")).then_inc(v_stored, 16)

                def block_steps(blk, k, ob):
                    def step(c, u=None):
                        slot = c if u is None else u
                        if k == 2:
                            if not isinstance(c, int) or c:
                                store_halves(ob, c - 1)
                            elif ob:
                                store_halves(0, NCH - 1)
                            for a in range(CB):
                                m = c * CB + (ob * NCH * CB + a)
                                if not isinstance(m, int) or m >= CB:
                                    act.wait_ge(nstep, (m - CB + 1) * STEPS)
                                act.dma_start(qd[:, a, :], dw_dram[2 * (1 - ob) + a, :, ds(c * CH, CH)]).then_inc(qk_loaded[a], 16)
                            for a in range(CB):
                                act.wait_ge(qk_loaded[a], (c + (ob * NCH + 1)) * 16)
                                act.activation(nrm[:, a, :], qd[:, a, :], ACT.Square).then_inc(squared, 1)
                            for a in range(CB):
                                act.wait_ge(squared, c * (2 * CB) + (ob * NCH * 2 * CB + a + 1))
                                act.activation(sqh[:, a, :], nrm[:, a, :], ACT.Identity).then_inc(squared, 1)
                            for a in range(CB):
                                act.wait_ge(summed, c * CB + (ob * NCH * CB + a + 1))
                                act.activation(nrm[:, a, :], pn[:, a, :], ACT.Sqrt).then_inc(rooted, 1)
                        move(blk, c, slot)
                        if k == 2:
                            if not isinstance(c, int) or c >= 2:
                                split_v(ob, c - 2, slot)
                            elif ob:
                                split_v(ob - 1, NCH - 2 + c, slot)
                        elif not isinstance(c, int) or c >= 2:
                            store(blk, c - 2, slot)
                    return step

                act.wait_ge(border, 1)
                for blk, (k, ob) in enumerate(blocks):
                    if k == 2:
                        for u in range(2):
                            act.wait_ge(stored[u], (V0 - 1 + ob) * (NCH // 2) * 16)
                    if blk == V0 - 1:
                        for c in range(NCH):
                            move(blk, c, c % 2)
                        for c in range(NCH - 2):
                            store(blk, c, c % 2)
                    else:
                        steps(act, block_steps(blk, k, ob))
                    if k < 2:
                        store(blk, NCH - 2, 0)
                        store(blk, NCH - 1, 1)
                store_halves(1, NCH - 1)
                split_v(CB - 1, NCH - 2, 0)
                split_v(CB - 1, NCH - 1, 1)
                act.wait_ge(v_stored, (CB * NCH + 1) * 16)
                for u in range(2):
                    act.wait_ge(stored[u], V0 * (NCH // 2) * 16)
                for a in range(CB):
                    act.wait_ge(half_stored[a], CB * NCH * 16)

            @block.vector
            def _(dve):
                def depthwise(blk, c, slot):
                    done = c + blk * NCH
                    last = isinstance(c, int) and c == NCH - 1
                    dve.wait_ge(moved, done + (1 if last else 2))
                    if blk > V0 or (blk == V0 and (not isinstance(c, int) or c >= 2)):
                        dve.wait_ge(v_turned, c + ((blk - V0) * NCH - 1))
                    elif blk or not isinstance(c, int) or c >= 2:
                        dve.wait_ge(stored[slot], (c - slot + blk * NCH) * 8)
                    out = acc[:, slot, :].rearrange("p (y x) -> p y x", x=SIDE)
                    HR = ROWS // 2
                    for t in range(9):
                        w = wdw[:, channel_block(blk), t:t + 1]
                        for h in range(2):
                            src = cov[:, ds(c * ROWS + (t // 3 + h * HR), HR), t % 3:t % 3 + SIDE]
                            half_out = out[:, h * HR:(h + 1) * HR, :]
                            if t == 0:
                                ins = dve.tensor_scalar(half_out, src, w, None, ALU.mult)
                            else:
                                dve.wait_ge(tap, done * DW + (2 * t - 1 + h))
                                ins = dve.scalar_tensor_tensor(out=half_out, in0=src, scalar=w, in1=half_out,
                                                               op0=ALU.mult, op1=ALU.add)
                            ins.then_inc(tap, 1)

                def unit_halves(which, j):
                    for a in range(CB):
                        m = j * CB + (which * NCH * CB + a)
                        dve.wait_ge(squared, j * (2 * CB) + (which * NCH * 2 * CB + CB + a + 1))
                        if which or not isinstance(j, int) or j:
                            dve.wait_ge(summed, m - 1)
                        dve.tensor_tensor(sql[:, a, :], nrm[:, a, :], sqh[:, a, :].bitcast(F32),
                                          ALU.subtract).then_inc(square_low, 1)
                    for a in range(CB):
                        m = j * CB + (which * NCH * CB + a)
                        dve.wait_ge(rooted, m + 1)
                        dve.tensor_scalar(nrm[:, a, :], nrm[:, a, :], 1e-12, None, ALU.max).then_inc(nstep, 1)
                        dve.wait_ge(nstep, m * STEPS + 1)
                        dve.reciprocal(nrm[:, a, :], nrm[:, a, :]).then_inc(nstep, 1)
                        dve.wait_ge(nstep, m * STEPS + 2)
                        dve.scalar_tensor_tensor(out=unit[:, :], in0=qd[:, a, :], scalar=UNIT_SCALE, in1=nrm[:, a, :],
                                                 op0=ALU.mult, op1=ALU.mult).then_inc(nstep, 1)
                        dve.wait_ge(nstep, m * STEPS + 3)
                        if which or not isinstance(j, int) or j:
                            dve.wait_ge(half_stored[a], (j + which * NCH) * 16)
                        dve.tensor_copy(half[:, a, 0, :], unit[:, :]).then_inc(nstep, 1)
                        dve.wait_ge(nstep, m * STEPS + 4)
                        dve.tensor_tensor(half[:, a, 1, :], unit[:, :], half[:, a, 0, :], ALU.subtract).then_inc(nstep, 1)

                def low_v(vi):
                    dve.wait_ge(v_high, vi + 1)
                    dve.tensor_tensor(v_part(1), pt[:, :, :].rearrange("p m (h c) -> p m h c", c=HD),
                                      v_part(0).bitcast(F32), ALU.subtract).then_inc(v_low, 1)

                dve.memset(co[:, :], 0.0).then_inc(border, 1)
                dve.memset(vt[:, :, :, 2 * HD:VW].bitcast(F32), 1.0).then_inc(v_stored, 16)
                dve.memset(nrm[:, 0, 0:1], 0.0).then_inc(v_low, 1)
                dve.wait_ge(consts, 48)
                dve.tensor_copy(head_sum[:, :], head_sum_raw[:, :]).then_inc(border, 1)
                for blk, (k, ob) in enumerate(blocks):
                    def step(c, u=None):
                        if k == 2:
                            unit_halves(ob, c)
                        if not isinstance(c, int) or c:
                            depthwise(blk, c - 1, (c - 1) % 2 if u is None else 1 - u)
                        if k == 2 and (ob or not isinstance(c, int)):
                            low_v(c + (ob * NCH - 2))
                    steps(dve, step)
                    depthwise(blk, NCH - 1, 1)
                for vi in range(CB * NCH - 2, CB * NCH):
                    low_v(vi)

NB = 1024
NNB = PX // NB
NG = HEADS * NNB
SCORE_RANGE = 60.0
MT = PX // P
PLAIN = (6, 14, 22, 30)
SPLIT = [m for m in range(MT) if m not in PLAIN]

def attention(nc, parts_dram, vt_dram, temp_dram, o_dram, ahead):
    with ExitStack() as stack:
        n = Names(nc, stack, "att")
        R = 8
        LAG = 5
        qs = n.sb("q_stack", [P, 2, PX], F16)
        ks = n.sb("k_stack", [P, 2, PX], F16)
        vs = [n.sb(f"v_stack{i}", [P, MT, VW], F32R) for i in range(2)]
        e = n.sb("exp", [P, R, NB])
        eh = n.sb("exp_high", [P, R, NB], F32R)
        el = n.sb("exp_low", [P, R, NB], F32R)
        out = n.sb("out", [VW, 2, NB])
        temp = n.sb("temp", [P, HEADS * NNB])
        affine = n.sb("affine", [P, NG, 2])
        scale, shift = affine[:, :, 0], affine[:, :, 1]
        cur = n.sb("affine_now", [P, 2, 2])
        spare = n.sb("spare", [P, 2])
        sc = n.ps("scores", [P, 2, NB])
        pv = n.ps("pv", [P, 2, NB])

        temp_loaded = n.sem("temp_loaded")
        tstep = n.sem("temp_step")
        loaded = [n.sem(f"stack_loaded{i}") for i in range(2)]
        ahead_loaded = n.sem("ahead_loaded")
        v_loaded = [n.sem(f"v_loaded{i}") for i in range(2)]
        scored = n.sem("scored")
        exped = n.sem("exped")
        high_act = n.sem("exp_high_by_act")
        high_dve = n.sem("exp_high_by_dve")
        low = n.sem("exp_low_ready")
        summed = n.sem("pv_done")
        pv_free = n.sem("pv_free")
        tneg = n.sem("temp_neg")
        cur_ready = n.sem("affine_now_ready")
        stored = [n.sem(f"out_stored{i}") for i in range(2)]
        LOADS = 8
        ON_ACT = SPLIT[1::3]
        ON_DVE = [m for m in SPLIT if m not in ON_ACT]

        def upto(tiles, g, mt):
            return g * len(tiles) + sum(m <= mt for m in tiles)

        with nc.Block() as block:

            @block.sync
            def _(sp):
                sp.dma_start(temp[:, :], temp_dram).then_inc(temp_loaded, 16)

                def load(head, s):
                    at = head * HD
                    for i, (a, b) in enumerate(((0, 0), (0, 1), (1, 0), (1, 1))):
                        rows = slice(i * HD, (i + 1) * HD)
                        sp.dma_start(qs[rows, s, :], parts_dram[0, a, ds(at, HD), :]).then_inc(loaded[s], 16)
                        sp.dma_start(ks[rows, s, :], parts_dram[1, b, ds(at, HD), :]).then_inc(loaded[s], 16)
                    sp.dma_start(vs[s][:, :, :].bitcast(F32).rearrange("p m c -> p (m c)"),
                                 vt_dram[ds(head, 1), :, :].rearrange("h p n -> (h p) n")).then_inc(v_loaded[s], 16)

                load(0, 0)
                load(1, 1)
                load_ahead(sp, ahead, ahead_loaded)
                with sp.Fori(0, HEADS // 2 - 1) as hp:
                    for s in range(2):
                        sp.wait_ge(summed, (hp * 2 + (s + 1)) * (NNB * MT))
                        load(hp * 2 + (2 + s), s)
                sp.wait_ge(summed, (HEADS - 1) * NNB * MT)
                load(0, 0)
                sp.wait_ge(loaded[0], 16 * LOADS * (HEADS // 2 + 1))
                sp.wait_ge(v_loaded[0], 16 * (HEADS // 2 + 1))
                sp.wait_ge(ahead_loaded, 16 * len(ahead))

            @block.tensor
            def _(pe):
                def scores(s, n0, mt):
                    for c in range(2):
                        mm = pe.matmul(sc[:, mt % 2, c * CH:(c + 1) * CH], ks[:, s, mt * P:(mt + 1) * P],
                                       qs[:, s, n0 + c * CH:n0 + (c + 1) * CH], start=True, stop=True)
                    mm.then_inc(scored, 1)

                def tiles(g, s, nb, s_next, nb_next, next_loaded=None):
                    slot = nb % 2
                    for mt in range(MT):
                        ahead = mt + LAG
                        if ahead == MT and next_loaded is not None:
                            pe.wait_ge(loaded[s_next], next_loaded)
                        pe.wait_ge(exped, g * MT + (ahead - 1))
                        if ahead < MT:
                            scores(s, nb * NB, ahead)
                        else:
                            scores(s_next, nb_next * NB, ahead - MT)
                        if mt in PLAIN:
                            pe.wait_ge(exped, g * MT + (mt + 1))
                            for c in range(2):
                                mm = pe.matmul(pv[0:VW, slot, c * CH:(c + 1) * CH], vs[s][:, mt, :].bitcast(F32),
                                               e[:, mt % R, c * CH:(c + 1) * CH], start=False, stop=False)
                            mm.then_inc(summed, 1)
                            continue
                        if mt in ON_ACT:
                            pe.wait_ge(high_act, upto(ON_ACT, g, mt))
                        else:
                            pe.wait_ge(high_dve, upto(ON_DVE, g, mt))
                        for part in (eh, el):
                            if part is el:
                                pe.wait_ge(low, upto(SPLIT, g, mt))
                            for c in range(2):
                                mm = pe.matmul(pv[0:VW, slot, c * CH:(c + 1) * CH], vs[s][:, mt, :],
                                               part[:, mt % R, c * CH:(c + 1) * CH],
                                               start=mt == 0 and part is eh, stop=mt == MT - 1 and part is el)
                        mm.then_inc(summed, 1)

                pe.wait_ge(loaded[0], 16 * LOADS)
                for mt in range(LAG):
                    if mt >= 2:
                        pe.wait_ge(exped, mt - 1)
                    scores(0, 0, mt)
                with pe.Fori(0, HEADS // 2) as hp:
                    for s in range(2):
                        for nb in range(NNB):
                            g = hp * (2 * NNB) + (s * NNB + nb)
                            pe.wait_ge(pv_free, g + 1)
                            if nb == 0:
                                pe.wait_ge(v_loaded[s], hp * 16 + 16)
                            if nb < NNB - 1:
                                tiles(g, s, nb, s, nb + 1)
                            else:
                                tiles(g, s, nb, 1 - s, 0, (hp + (1 + s)) * (16 * LOADS))

            @block.scalar
            def _(act):
                def move(g, slot):
                    act.wait_ge(summed, (g + 1) * MT)
                    if not isinstance(g, int) or g >= 2:
                        act.wait_ge(stored[slot], (g - slot) * 8)
                    act.activation(out[:, slot, :], pv[0:VW, slot, :], ACT.Identity).then_inc(pv_free, 1)

                def store(g, slot):
                    act.wait_ge(pv_free, g + 3)
                    act.dma_start(o_dram[ds(g, 1), :, :].rearrange("g c n -> (g c) n"), out[:, slot, :]).then_inc(stored[slot], 16)

                def body(g, slot):
                    act.activation(cur[:, slot, :], affine[:, ds(g, 1), :].rearrange("p g a -> p (g a)"),
                                   ACT.Identity).then_inc(cur_ready, 1)
                    act.wait_ge(cur_ready, g + 1)
                    for mt in range(MT):
                        act.wait_ge(scored, g * MT + (mt + 1))
                        if not isinstance(g, int) or g * MT + mt >= R:
                            if (mt - R) % MT in PLAIN:
                                act.wait_ge(summed, g * MT + (mt + 1 - R))
                            else:
                                act.wait_ge(low, g * len(SPLIT) + (sum(m <= (mt - R) % MT for m in SPLIT) - len(SPLIT) * (mt < R)))
                        act.activation(e[:, mt % R, :], sc[:, mt % 2, :], ACT.Exp, scale=cur[:, slot, 0:1],
                                       bias=cur[:, slot, 1:2]).then_inc(exped, 1)
                        if mt - 1 in ON_ACT:
                            if not isinstance(g, int) or g * MT + mt - 1 >= R:
                                act.wait_ge(summed, g * MT + (mt - R))
                            act.wait_ge(exped, g * MT + mt)
                            act.activation(eh[:, (mt - 1) % R, :], e[:, (mt - 1) % R, :], ACT.Identity).then_inc(high_act, 1)
                        if not isinstance(g, int) or g:
                            if mt == LAG + 2:
                                move(g - 1, 1 - slot)
                            if mt == LAG + 4:
                                store(g - 1, 1 - slot)

                act.wait_ge(tstep, 4)
                body(0, 0)
                body(1, 1)
                with act.Fori(0, NG // 2 - 1) as i:
                    for s in range(2):
                        body(i * 2 + (2 + s), s)
                for mt in range(LAG - 2):
                    act.wait_ge(scored, NG * MT + mt + 1)
                    act.wait_ge(low, upto(SPLIT, NG - 1, MT - R + mt))
                    act.activation(e[:, mt, :], sc[:, mt % 2, :], ACT.Exp, scale=cur[:, 0, 0:1],
                                   bias=cur[:, 0, 1:2]).then_inc(exped, 1)
                move(NG - 1, 1)
                store(NG - 1, 1)
                for s in range(2):
                    act.wait_ge(stored[s], 16 * (NG // 2))

            @block.vector
            def _(dve):
                dve.wait_ge(temp_loaded, 16)
                dve.tensor_scalar(scale, temp[:, :], 1.0 / (UNIT_SCALE * UNIT_SCALE), None, ALU.mult).then_inc(tstep, 1)
                dve.tensor_scalar(shift, temp[:, :], -1.0, None, ALU.mult).then_inc(tstep, 1)
                dve.wait_ge(tstep, 2)
                dve.tensor_tensor(shift, shift, temp[:, :], ALU.max).then_inc(tstep, 1)
                dve.wait_ge(tstep, 3)
                dve.tensor_scalar(temp[:, :], shift, -1.0, SCORE_RANGE, ALU.mult, ALU.add).then_inc(tneg, 1)
                dve.wait_ge(tneg, 1)
                dve.tensor_scalar(shift, temp[:, :], 0.0, None, ALU.min).then_inc(tstep, 1)
                dve.memset(spare[:, 0:1], 0.0).then_inc(pv_free, 1)
                dve.memset(spare[:, 1:2], 0.0).then_inc(pv_free, 1)

                def body(g):
                    for mt in SPLIT:
                        if not isinstance(g, int) or g * MT + mt >= R:
                            dve.wait_ge(summed, g * MT + (mt + 1 - R))
                        if mt in ON_ACT:
                            dve.wait_ge(high_act, upto(ON_ACT, g, mt))
                        else:
                            dve.wait_ge(exped, g * MT + (mt + 1))
                            dve.tensor_copy(eh[:, mt % R, :], e[:, mt % R, :]).then_inc(high_dve, 1)
                            dve.wait_ge(high_dve, upto(ON_DVE, g, mt))
                        dve.tensor_tensor(el[:, mt % R, :], e[:, mt % R, :], eh[:, mt % R, :].bitcast(F32),
                                          ALU.subtract).then_inc(low, 1)

                body(0)
                with dve.Fori(0, NG - 1) as i:
                    body(i + 1)

CROP = 48
M1 = CROP * CROP
SEG = M1 // C
NEWTON = 5

def project(nc, o_dram, w_dram, spread_dram, X, gn):
    with ExitStack() as stack:
        n = Names(nc, stack, "proj")
        SLOTS = 4
        w = n.sb("w", [P, CB, C])
        spread_raw = n.sb("spread_raw", [NG, NNB * CB, P])
        spread = n.sb("spread", [NG, NNB * CB, P], F32R)
        inverse = n.sb("inverse", [NG, NB])
        inverse_high = n.sb("inverse_high", [NG, NB], F32R)
        inverse_low = n.sb("inverse_low", [NG, NB], F32R)
        sums = n.sb("sums", [P, SLOTS, 2, NB])
        o = n.sb("o", [P, 2, CB, NB])
        ps = n.ps("ps", [P, 2, CB, CH])
        ps_i = n.ps("ps_i", [P, 2, NB])
        w_loaded = n.sem("w_loaded")
        total_loaded = n.sem("total_loaded")
        sums_loaded = [n.sem(f"sums_loaded{i}") for i in range(SLOTS)]
        inverted = n.sem("inverted")
        spread_done = n.sem("spread_done")
        step = n.sem("step")
        projected = n.sem("projected")
        added = n.sem("added")
        UNITS0 = CB * NNB
        with nc.Block() as block:

            @block.sync
            def _(sp):
                sp.dma_start(inverse[:, :], o_dram[:, 2 * HD, :]).then_inc(total_loaded, 16)
                sp.dma_start(spread_raw[:, :, :], spread_dram).then_inc(w_loaded, 16)
                sp.dma_start(w[:, :, :], w_dram).then_inc(w_loaded, 16)
                for i in range(UNITS0):
                    nb, b = divmod(i, CB)
                    if i >= SLOTS:
                        sp.wait_ge(step, 2 * (i - SLOTS + 1))
                    for h in range(HPB):
                        g = (b * HPB + h) * NNB + nb
                        sp.dma_start(sums[h * HD:(h + 1) * HD, i % SLOTS, :, :],
                                     o_dram[g, 0:2 * HD, :].rearrange("(k c) n -> c k n", c=HD)).then_inc(sums_loaded[i % SLOTS], 16)

            @block.vector
            def _(dve):
                def add(c):
                    dve.wait_ge(projected, c + 1)
                    for ob in range(CB):
                        xs = X[:, ob, c * CH:(c + 1) * CH]
                        dve.tensor_tensor(xs, ps[:, c % 2, ob, :], xs, ALU.add).then_inc(added, 1)
                    dve.wait_ge(added, CB * (c + 1))
                    for ob in range(CB):
                        gn.chunk_stats(dve, X, ob, c)

                dve.wait_ge(w_loaded, 32)
                dve.tensor_copy(spread[:, :, :], spread_raw[:, :, :]).then_inc(inverted, 1)
                dve.wait_ge(total_loaded, 16)
                for q in range(2):
                    at = slice(q * CH, (q + 1) * CH)
                    dve.reciprocal(inverse[:, at], inverse[:, at]).then_inc(inverted, 1)
                    dve.wait_ge(inverted, 3 * q + 2)
                    dve.tensor_copy(inverse_high[:, at], inverse[:, at]).then_inc(inverted, 1)
                    dve.wait_ge(inverted, 3 * q + 3)
                    dve.tensor_tensor(inverse_low[:, at], inverse[:, at], inverse_high[:, at].bitcast(F32),
                                      ALU.subtract).then_inc(inverted, 1)
                for i in range(UNITS0):
                    nb, b = divmod(i, CB)
                    s = sums[:, i % SLOTS]
                    dve.wait_ge(sums_loaded[i % SLOTS], 16 * HPB * (i // SLOTS + 1))
                    dve.tensor_tensor(s[:, 0, :], s[:, 0, :], s[:, 1, :], ALU.add).then_inc(step, 1)
                    dve.wait_ge(step, 2 * i + 1)
                    dve.wait_ge(spread_done, i + 1)
                    if nb >= 2:
                        dve.wait_ge(projected, 2 * (nb - 1))
                    dve.tensor_tensor(o[:, nb % 2, b, :], s[:, 0, :], ps_i[:, i % 2, :], ALU.mult).then_inc(step, 1)
                    if b == 1 and nb:
                        add(2 * nb - 2)
                        add(2 * nb - 1)
                add(NCH - 2)
                add(NCH - 1)
                gn.channel_moments(dve)
                gn.vector_moments(dve)

            @block.tensor
            def _(pe):
                def spread_unit(i):
                    if i >= 2:
                        pe.wait_ge(step, 2 * (i - 1))
                    for h in range(2):
                        if i == 0:
                            pe.wait_ge(inverted, 3 * (h + 1) + 1)
                        for part in (inverse_high, inverse_low):
                            mm = pe.matmul(ps_i[:, i % 2, h * CH:(h + 1) * CH], spread[:, i, :],
                                           part[:, h * CH:(h + 1) * CH], start=part is inverse_high, stop=part is inverse_low)
                    mm.then_inc(spread_done, 1)

                pe.wait_ge(w_loaded, 32)
                spread_unit(0)
                spread_unit(1)
                for c in range(NCH):
                    nb, h = divmod(c, 2)
                    if h == 0:
                        for b in range(CB):
                            if 2 * (nb + 1) + b < UNITS0:
                                spread_unit(2 * (nb + 1) + b)
                    pe.wait_ge(step, 2 * CB * (nb + 1))
                    if c >= 2:
                        pe.wait_ge(added, 2 * (c - 1))
                    for ob in range(CB):
                        for ib in range(CB):
                            mm = pe.matmul(ps[:, c % 2, ob, :], w[:, ib, ob * P:(ob + 1) * P],
                                           o[:, nb % 2, ib, h * CH:(h + 1) * CH], start=ib == 0, stop=ib == CB - 1)
                    mm.then_inc(projected, 1)

class Count:

    def __init__(self, n, name):
        self.sem, self.value = n.sem(name), 0

    def up(self, ins):
        ins.then_inc(self.sem, 1)
        self.value += 1
        return self.value

def covariance_gate(nc, gm, eye_dram, w1_dram, b1_dram, w2_dram, b2_dram, X, gn, gn_after):
    with ExitStack() as stack:
        n = Names(nc, stack, "cov")
        eye = n.sb("eye", [P, CB, C])
        ones = n.sb("ones", [P, P])
        w = n.sb("w", [P, 2, CB, C])
        bias = n.sb("bias", [P, 2, CB])
        new = n.sb("new", [P, 2, CB])
        xc = n.sb("xc", [P, CB, M1])
        part_sums = n.sb("part_sums", [P, CB, C])
        rows = n.sb("row_sums", [1, 2, C])
        mats = {k: n.sb(k, [P, CB, C]) for k in ("cov", "A", "Y", "Y2", "Z", "Z2", "ZY", "diag")}
        small = n.sb("small", [P, 16])
        ps_gn = n.ps("ps_gn", [P, CB * 2])
        ps_g = n.ps("ps_g", [P, CB, C])
        ps_r = n.ps("ps_r", [P, C])
        ps_y = n.ps("ps_y", [P, CB, C])
        ps_z = n.ps("ps_z", [P, CB, C])
        ps_s = n.ps("ps_s", [P, 8])
        loaded = n.sem("loaded")
        ones_set = n.sem("ones_set")
        crop = n.sem("crop_ready")
        new_ready = n.sem("new_ready")
        x_ready = n.sem("x_ready")
        T = Count(n, "tensor_done")
        V = Count(n, "vector_done")
        A = Count(n, "scalar_done")
        at = {}

        nt = nv = na = 0
        for name in ("sums", "gram", "trace", "Y0") + tuple(f"{m}{i}" for i in range(1, NEWTON - 1) for m in "TYZ") + (
                "TF", "YF", "FC1", "FC2"):
            nt += 1
            at["t", name] = nt
        with nc.Block() as block:

            @block.sync
            def _(sp):
                for t, d in ((eye[:, :, :], eye_dram), (w[:, 0], w1_dram), (w[:, 1], w2_dram),
                             (bias[:, 0], b1_dram), (bias[:, 1], b2_dram)):
                    sp.dma_start(t, d).then_inc(loaded, 16)

            @block.gpsimd
            def _(pool):
                pool.memset(ones[:, :], 1.0).then_inc(ones_set, 1)

            @block.vector
            def _(dve):
                gn.vector_affine(dve, ps_gn[:, :])
                v = dict()

                def made(name, ins):
                    v[name] = at["v", name] = V.up(ins)

                def after(name):
                    dve.wait_ge(V.sem, v[name])

                dve.wait_ge(loaded, 80)
                for b in range(CB):
                    dve.wait_ge(crop, b + 1)
                    made(f"part{b}", dve.reduce_sum(part_sums[:, b, :], xc[:, b, :].rearrange("p (c j) -> p c j", j=SEG), AX.X))
                dve.wait_ge(T.sem, at["t", "sums"])
                made("row", dve.tensor_copy(rows[0:1, 0, :], ps_r[0:1, :]))
                made("nrow", dve.tensor_scalar(rows[0:1, 1, :], ps_r[0:1, :], -1.0 / M1, None, ALU.mult))
                dve.wait_ge(T.sem, at["t", "gram"])
                made("cov", dve.tensor_scalar(mats["cov"][:, :, :], ps_g[:, :, :], 1.0 / M1, None, ALU.mult))
                after("cov")
                made("diag", dve.tensor_tensor(mats["diag"][:, :, :], mats["cov"][:, :, :], eye[:, :, :], ALU.mult))
                after("diag")
                made("diag_sum", dve.reduce_sum(small[:, 0:1], mats["diag"][:, :, :].rearrange("p b c -> p (b c)"), AX.X))
                dve.wait_ge(T.sem, at["t", "trace"])
                made("trace", dve.tensor_copy(small[:, 1:2], ps_s[:, 0:1]))
                after("trace")
                made("inv", dve.reciprocal(small[:, 2:3], small[:, 1:2]))
                after("inv")
                made("A", dve.tensor_scalar(mats["A"][:, :, :], mats["cov"][:, :, :], small[:, 2:3], None, ALU.mult))
                made("eye15", dve.tensor_scalar(mats["diag"][:, :, :], eye[:, :, :], 1.5, None, ALU.mult))
                after("eye15")
                e15 = mats["diag"]
                made("Z0", dve.scalar_tensor_tensor(out=mats["Z"][:, :, :], in0=mats["A"][:, :, :], scalar=-0.5,
                                                    in1=e15[:, :, :], op0=ALU.mult, op1=ALU.add))
                dve.wait_ge(T.sem, at["t", "Y0"])
                made("Y0", dve.tensor_copy(mats["Y"][:, :, :], ps_y[:, :, :]))
                for i in range(1, NEWTON):
                    dve.wait_ge(T.sem, at["t", f"T{i}" if i < NEWTON - 1 else "TF"])
                    made(f"ZY{i}", dve.scalar_tensor_tensor(out=mats["ZY"][:, :, :], in0=ps_y[:, :, :], scalar=-0.5,
                                                            in1=e15[:, :, :], op0=ALU.mult, op1=ALU.add))
                    if i == NEWTON - 1:
                        break
                    dve.wait_ge(T.sem, at["t", f"Y{i}"])
                    made(f"Y{i}", dve.tensor_copy(mats["Y"][:, :, :], ps_z[:, :, :]))
                    dve.wait_ge(T.sem, at["t", f"Z{i}"])
                    made(f"Z{i}", dve.tensor_copy(mats["Z"][:, :, :], ps_g[:, :, :]))
                dve.wait_ge(T.sem, at["t", "YF"])
                made("mean", dve.reduce_sum(small[:, 4:6], ps_z[:, :, :], AX.X))
                after("mean")
                dve.wait_ge(A.sem, 1)
                made("y", dve.tensor_scalar(small[:, 6:8], small[:, 4:6], small[:, 3:4], 1.0 / C, ALU.mult, ALU.mult))
                dve.wait_ge(T.sem, at["t", "FC1"])
                made("h0", dve.tensor_tensor(small[:, 8:10], ps_s[:, 2:4], bias[:, 0, :], ALU.add))
                after("h0")
                made("h", dve.tensor_scalar(small[:, 8:10], small[:, 8:10], 0.0, None, ALU.max))
                dve.wait_ge(T.sem, at["t", "FC2"])
                made("g0", dve.tensor_tensor(small[:, 10:12], ps_s[:, 4:6], bias[:, 1, :], ALU.add))
                dve.wait_ge(A.sem, 2)
                gate = small[:, 12:14]
                made("gscale", dve.tensor_tensor(new[:, 0, :], gate, gn.scale[:, :], ALU.mult))
                after("gscale")
                dve.tensor_scalar(new[:, 0, :], new[:, 0, :], 1.0, None, ALU.add).then_inc(new_ready, 1)
                dve.tensor_tensor(new[:, 1, :], gate, gn.shift[:, :], ALU.mult).then_inc(new_ready, 1)
                dve.wait_ge(new_ready, 2)
                gn_after.moments_of_affine(dve, gn, new[:, 0, :], new[:, 1, :])
                gn_after.vector_moments(dve)
                dve.wait_ge(crop, CB)
                dve.tensor_scalar(X[:, 1, :], X[:, 1, :], new[:, 0, 1:2], new[:, 1, 1:2], ALU.mult, ALU.add).then_inc(x_ready, 1)

            @block.tensor
            def _(pe):
                def product(name, out, left, right):
                    for m in range(CB):
                        for k in range(CB):
                            mm = pe.matmul(out[:, m, :], left[:, k, m * P:(m + 1) * P], right[:, k, :],
                                           start=k == 0, stop=k == CB - 1)
                    assert T.up(mm) == at["t", name]

                def after(name):
                    pe.wait_ge(V.sem, at["v", name])

                gn.tensor_join(pe, ps_gn[:, :], gm[:, :])
                pe.wait_ge(ones_set, 1)
                pe.wait_ge(crop, CB)
                tiles = [xc[:, b, j::SEG] for b in range(CB) for j in range(SEG)]
                for m in range(CB):
                    for i, t in enumerate(tiles):
                        pe.matmul(ps_g[:, m, :], t[:, m * P:(m + 1) * P], t, start=i == 0, stop=False)
                    if m == 0:
                        after("part1")
                        for b in range(CB):
                            mm = pe.matmul(ps_r[0:1, :], ones[:, 0:1], part_sums[:, b, :], start=b == 0, stop=b == CB - 1)
                        T.up(mm)
                        after("nrow")
                    mm = pe.matmul(ps_g[:, m, :], rows[0:1, 0, m * P:(m + 1) * P], rows[0:1, 1, :], start=False, stop=True)
                T.up(mm)
                after("diag_sum")
                T.up(pe.matmul(ps_s[:, 0:1], ones[:, :], small[:, 0:1], start=True, stop=True))
                after("Z0")
                product("Y0", ps_y, mats["A"], mats["Z"])
                after("Y0")
                for i in range(1, NEWTON - 1):
                    product(f"T{i}", ps_y, mats["Z"], mats["Y"])
                    after(f"ZY{i}")
                    product(f"Y{i}", ps_z, mats["Y"], mats["ZY"])
                    product(f"Z{i}", ps_g, mats["ZY"], mats["Z"])
                    after(f"Z{i}")
                product("TF", ps_y, mats["Z"], mats["Y"])
                after(f"ZY{NEWTON - 1}")
                product("YF", ps_z, mats["Y"], mats["ZY"])
                pe.wait_ge(loaded, 80)
                for layer, (name, src, col) in enumerate((("y", 6, 2), ("h", 8, 4))):
                    after(name)
                    for ob in range(CB):
                        for ib in range(CB):
                            mm = pe.matmul(ps_s[:, col + ob:col + ob + 1], w[:, layer, ib, ob * P:(ob + 1) * P],
                                           small[:, src + ib:src + ib + 1], start=ib == 0, stop=ib == CB - 1)
                    T.up(mm)

            @block.scalar
            def _(act):
                gn.scalar_std(act)
                act.wait_ge(gn.ready, 1)
                lo = (SIDE - CROP) // 2
                for b in range(CB):
                    act.activation(xc[:, b, :].rearrange("p (y x) -> p y x", x=CROP),
                                   padded(X[:, b, :], SIDE)[:, lo:lo + CROP, lo:lo + CROP], ACT.Identity,
                                   scale=gn.scale[:, b:b + 1], bias=gn.shift[:, b:b + 1]).then_inc(crop, 1)
                act.wait_ge(V.sem, at["v", "trace"])
                A.up(act.activation(small[:, 3:4], small[:, 1:2], ACT.Sqrt))
                act.wait_ge(V.sem, at["v", "g0"])
                A.up(act.activation(small[:, 12:14], small[:, 10:12], ACT.Sigmoid))
                act.wait_ge(new_ready, 2)
                act.wait_ge(crop, CB)
                act.activation(X[:, 0, :], X[:, 0, :], ACT.Identity, scale=new[:, 0, 0:1],
                               bias=new[:, 1, 0:1]).then_inc(x_ready, 1)

TAPS = 9
TAB = SIDE + 2
TILES = PX // P
OM = 3 * TAPS

def offsets_and_table(nc, gm, ident, ow_dram, ob_dram, base_dram, table_dram, X, IDX, CW, gn, ahead):
    with ExitStack() as stack:
        n = Names(nc, stack, "off")
        xh = n.sb("x_high", [P, CB, PAD3 * PAD3], F32R)
        xl = n.sb("x_low", [P, CB, PAD3 * PAD3], F32R)
        owh = n.sb("offset_w_high", [P, CB, TAPS * OM], F32R)
        owl = n.sb("offset_w_low", [P, CB, TAPS * OM], F32R)
        xn = n.sb("xn", [P, CB, PX])
        ow = n.sb("offset_w", [P, CB, TAPS * OM])
        obias = n.sb("offset_b", [OM, 1])
        base = n.sb("base", [P, 2, TILES * TAPS])
        om = n.sb("om", [OM, 2, CH])
        omt = n.sb("om_t", [P, TILES, OM])
        zero = n.sb("zero", [P, C])
        xt = n.sb("x_turned", [P, 2, ROWS // 2, C])
        pos, floor, over = (n.sb(k, [P, 2, TILES, TAPS]) for k in ("position", "floor", "over"))
        frac = n.sb("fraction", [P, 2, 2, TILES, TAPS])
        mask = n.sb("mask", [P, TILES, TAPS])
        rows_w = over
        row_index = n.sb("row_index", [P, TILES, TAPS])
        whole = n.sb("whole", [P, 2, TILES, TAPS], I32)
        ps_gn = n.ps("ps_gn", [P, CB * 2])
        ps_o = n.ps("ps_o", [P, 2, CH])
        ps_t = n.ps("ps_t", [P, 2, CH])
        ps_m = n.ps("ps_m", [P, 2, CH])
        loaded = n.sem("loaded")
        border = n.sem("border")
        ahead_loaded = n.sem("ahead_loaded")
        zero_set = n.sem("zero_set")
        normed = n.sem("normed")
        high = n.sem("high_ready")
        low = n.sem("low_ready")
        w_split = n.sem("offset_w_split")
        omt_ready = n.sem("om_t_ready")
        conv = n.sem("om_conv")
        om_ready = n.sem("om_ready")
        om_turned = n.sem("om_turned")
        turned = n.sem("turned")
        xt_ready = n.sem("xt_ready")
        kept = [n.sem(f"kept{i}") for i in range(2)]
        zeroed = n.sem("table_zeroed")
        masked = n.sem("masked")
        V = Count(n, "vector_done")
        corner = table_dram.rearrange("(y x) (q c) -> q y x c", x=TAB, c=C)
        HB = TILES // 2

        def half(h):
            return slice(h * HB, (h + 1) * HB)

        def inside(part, b, c):
            return padded(part[:, b, :], PAD3)[:, 1 + c * ROWS:1 + (c + 1) * ROWS, 1:1 + SIDE]

        with nc.Block() as block:

            @block.sync
            def _(sp):
                for t, d in ((ow[:, :, :], ow_dram),
                             (obias[:, :], ob_dram), (base[:, :, :], base_dram)):
                    sp.dma_start(t, d).then_inc(loaded, 16)
                load_ahead(sp, ahead, ahead_loaded)
                with sp.Fori(0, NCH // 2) as i:
                    for u in range(2):
                        sp.wait_ge(xt_ready, i * 4 + 2 * (u + 1))
                        for q in range(4):
                            dy, dx = divmod(q, 2)
                            for r in range(2):
                                lines = corner[q, ds(i * (2 * ROWS) + (u * ROWS + r + 1 - dy), ROWS // 2, 2), 1 - dx:1 - dx + SIDE, :]
                                sp.dma_start(lines.rearrange("y x c -> x y c"),
                                             xt[r * SIDE:(r + 1) * SIDE, u, :, :]).then_inc(kept[u], 16)
                for u in range(2):
                    sp.wait_ge(kept[u], 16 * 8 * NCH // 2)
                sp.wait_ge(ahead_loaded, 16 * len(ahead))

            @block.gpsimd
            def _(pool):
                for part in (xh, xl):
                    for b in range(CB):
                        frame = padded(part[:, b, :], PAD3).bitcast(F32)
                        pool.memset(frame[:, 0:PAD3:PAD3 - 1, :], 0.0).then_inc(border, 1)
                        pool.memset(frame[:, 1:1 + SIDE, 0:PAD3:PAD3 - 1], 0.0).then_inc(border, 1)
                pool.memset(zero[:, :], 0.0).then_inc(zero_set, 1)
                pool.wait_ge(zero_set, 1)
                done = 0
                for q in range(4):
                    dy, dx = divmod(q, 2)
                    for line in ({0, TAB - 1} if not dy else {TAB - 2, TAB - 1}):
                        pool.dma_start(corner[q, line, :, :], zero[0:TAB, :]).then_inc(zeroed, 16)
                        done += 16
                    rows = slice(1 - dy, 1 - dy + SIDE)
                    for line in ({0, TAB - 1} if not dx else {TAB - 2, TAB - 1}):
                        pool.dma_start(corner[q, rows, line, :], zero[0:SIDE, :]).then_inc(zeroed, 16)
                        done += 16
                pool.wait_ge(zeroed, done)

            @block.scalar
            def _(act):
                gn.scalar_std(act)
                act.wait_ge(gn.ready, 1)
                for c in range(NCH):
                    for b in range(CB):
                        at = slice(c * CH, (c + 1) * CH)
                        act.activation(xn[:, b, at], X[:, b, at], ACT.Identity, scale=gn.scale[:, b:b + 1],
                                       bias=gn.shift[:, b:b + 1]).then_inc(normed, 1)
                        act.activation(inside(xh, b, c), padded(X[:, b, at], SIDE), ACT.Identity,
                                       scale=gn.scale[:, b:b + 1], bias=gn.shift[:, b:b + 1]).then_inc(high, 1)
                for t in range(2 * NCH):
                    act.wait_ge(turned, t + 1)
                    c, j = divmod(t, 2)
                    if c >= 2:
                        act.wait_ge(kept[c % 2], 16 * 8 * (c // 2))
                    act.activation(xt[:, c % 2, 2 * j:2 * j + 2, :].rearrange("p t c -> p (t c)"), ps_t[:, t % 2, :],
                                   ACT.Identity).then_inc(xt_ready, 1)
                    if t in (NCH + 3, 2 * NCH - 1):
                        h = 0 if t == NCH + 3 else 1
                        act.wait_ge(omt_ready, h + 1)
                        act.activation(mask[:, half(h), :], omt[:, half(h), 2 * TAPS:], ACT.Sigmoid).then_inc(masked, 1)

            @block.tensor
            def _(pe):
                gn.tensor_join(pe, ps_gn[:, :], gm[:, :])
                pe.wait_ge(w_split, 2)
                pe.wait_ge(border, 4 * CB)

                def turn(t):
                    if t >= 2:
                        pe.wait_ge(xt_ready, t - 1)
                    for j in range(2):
                        for b in range(CB):
                            mm = pe.transpose(ps_t[:, t % 2, (j * CB + b) * P:(j * CB + b + 1) * P],
                                              xn[:, b, (2 * t + j) * P:(2 * t + j + 1) * P], ident[:, :])
                    mm.then_inc(turned, 1)

                def turn_om(c):
                    pe.wait_ge(om_ready, c + 1)
                    for t in range(4 * c, 4 * c + 4):
                        h, i = divmod(t, HB)
                        mm = pe.transpose(ps_m[:, h, i * OM:(i + 1) * OM], om[:, c % 2, (t - 4 * c) * P:(t - 4 * c + 1) * P],
                                          ident[0:OM, 0:OM])
                    mm.then_inc(om_turned, 1)

                for c in range(NCH):
                    if c >= 2:
                        pe.wait_ge(om_ready, c - 1)
                    pe.wait_ge(low, CB * min(c + 2, NCH))
                    for b in range(CB):
                        for t in range(TAPS):
                            for w, xs in ((owh, xh), (owh, xl), (owl, xh)):
                                mm = pe.matmul(ps_o[0:OM, c % 2, :], w[:, b, t * OM:(t + 1) * OM],
                                               padded(xs[:, b, :], PAD3)[:, c * ROWS + t // 3:c * ROWS + t // 3 + ROWS, t % 3:t % 3 + SIDE],
                                               start=b == 0 and t == 0 and xs is xh and w is owh,
                                               stop=b == CB - 1 and t == TAPS - 1 and w is owl)
                    mm.then_inc(conv, 1)
                    if c:
                        turn_om(c - 1)
                    for t in range(2 * c, 2 * c + 2):
                        turn(t)
                turn_om(NCH - 1)

            @block.vector
            def _(dve):
                gn.vector_affine(dve, ps_gn[:, :])
                dve.wait_ge(loaded, 16 * 3)
                for i, (part, src) in enumerate(((owh, ow), (owl, ow))):
                    if part is owh:
                        dve.tensor_copy(owh[:, :, :], ow[:, :, :]).then_inc(w_split, 1)
                    else:
                        dve.wait_ge(w_split, 1)
                        dve.tensor_tensor(owl[:, :, :], ow[:, :, :], owh[:, :, :].bitcast(F32), ALU.subtract).then_inc(w_split, 1)
                for c in range(NCH):
                    for b in range(CB):
                        dve.wait_ge(high, c * CB + b + 1)
                        dve.tensor_tensor(inside(xl, b, c), padded(xn[:, b, c * CH:(c + 1) * CH], SIDE),
                                          inside(xh, b, c).bitcast(F32), ALU.subtract).then_inc(low, 1)

                def made(ins):
                    V.up(ins)
                    dve.wait_ge(V.sem, V.value)

                def positions(h):
                    t = half(h)
                    dve.wait_ge(om_turned, NCH // 2 * (h + 1))
                    dve.tensor_copy(omt[:, t, :].rearrange("p t m -> p (t m)"), ps_m[:, h, 0:HB * OM]).then_inc(omt_ready, 1)
                    dve.wait_ge(omt_ready, h + 1)
                    made(dve.tensor_tensor(pos[:, :, t, :], omt[:, t, 0:2 * TAPS].rearrange("p t (a k) -> p k t a", k=2),
                                           base[:, :, :].rearrange("p k (t a) -> p k t a", a=TAPS)[:, :, t, :], ALU.add))
                    made(dve.tensor_scalar(pos[:, :, t, :], pos[:, :, t, :], 0.0, float(SIDE + 1), ALU.max, ALU.min))
                    made(dve.tensor_copy(whole[:, :, t, :], pos[:, :, t, :]))
                    made(dve.tensor_copy(floor[:, :, t, :], whole[:, :, t, :]))
                    made(dve.tensor_tensor(over[:, :, t, :], floor[:, :, t, :], pos[:, :, t, :], ALU.is_gt))
                    made(dve.tensor_tensor(floor[:, :, t, :], floor[:, :, t, :], over[:, :, t, :], ALU.subtract))
                    V.up(dve.tensor_tensor(frac[:, 1, :, t, :], pos[:, :, t, :], floor[:, :, t, :], ALU.subtract))
                    made(dve.scalar_tensor_tensor(out=row_index[:, t, :], in0=floor[:, 0, t, :], scalar=float(TAB),
                                                  in1=floor[:, 1, t, :], op0=ALU.mult, op1=ALU.add))
                    V.up(dve.tensor_copy(IDX[:, :].rearrange("p (t a) -> p t a", a=TAPS)[:, t, :], row_index[:, t, :]))
                    made(dve.tensor_scalar(frac[:, 0, :, t, :], frac[:, 1, :, t, :], -1.0, 1.0, ALU.mult, ALU.add))

                def weights(h):
                    t = half(h)
                    dve.wait_ge(masked, h + 1)
                    for k in range(2):
                        V.up(dve.tensor_tensor(rows_w[:, k, t, :], frac[:, k, 0, t, :], mask[:, t, :], ALU.mult))
                    dve.wait_ge(V.sem, V.value)
                    for q in range(4):
                        V.up(dve.tensor_tensor(CW[:, :, q].rearrange("p (t a) -> p t a", a=TAPS)[:, t, :],
                                               rows_w[:, q // 2, t, :], frac[:, q % 2, 1, t, :], ALU.mult))

                for c in range(NCH):
                    dve.wait_ge(conv, c + 1)
                    if c >= 2:
                        dve.wait_ge(om_turned, c - 1)
                    dve.tensor_scalar(om[:, c % 2, :], ps_o[0:OM, c % 2, :], obias[:, 0:1], None,
                                      ALU.add).then_inc(om_ready, 1)
                    if c == NCH // 2:
                        positions(0)
                    if c == NCH - 2:
                        weights(0)
                positions(1)
                weights(1)

def deform(nc, ident, w, table_dram, X, IDX, CW, gn):
    with ExitStack() as stack:
        n = Names(nc, stack, "dcn")
        GT = 4
        NGR = TILES // GT
        GS = 9
        BATCH = 3
        VS = 6
        TS = 3
        BEHIND = 3
        cur_idx = n.sb("cur_idx", [P, 2, TAPS], I32)
        g = n.sb("gathered", [P, GS, 4 * C])
        tick = n.sb("tick", [P, 2])
        tick_set = n.sem("tick_set")
        ticked = n.sem("ticked")
        val = n.sb("val", [P, VS, C])
        vt = n.sb("val_turned", [P, 2, TAPS, CB, GT * P])
        ps_t = n.ps("ps_t", [P, TS, 2 * CB, P])
        ps_o = n.ps("ps_o", [P, 2, CB, CH])
        idx_ready = n.sem("idx_ready")
        got = [n.sem(f"gathered{i}") for i in range(GS)]
        first = n.sem("first_product")
        step = n.sem("step")
        turned = n.sem("turned")
        kept = n.sem("turned_moved")
        product = n.sem("product")
        added = n.sem("added")

        def groups(eng, body):
            body(0, 0)
            body(1, 1)
            with eng.Fori(0, NGR // 2 - 2) as i:
                for u in range(2):
                    body(i * 2 + (2 + u), u)
            body(NGR - 2, 0)
            body(NGR - 1, 1)

        def summed_up(m, n):
            return m * 3 + (5 if n % 2 else 3)

        def static(v):
            return isinstance(v, int)

        with nc.Block() as block:

            @block.gpsimd
            def _(pool):
                pool.memset(tick[:, :], 0.0).then_inc(tick_set, 1)
                pool.wait_ge(tick_set, 1)
                pool.tensor_tensor(tick[:, 1:2], tick[:, 0:1], tick[:, 0:1], ALU.add).then_inc(ticked, 1)

                TICKS = 2 + 2 * TAPS // BATCH

                def passed(t2, k, sem, value):
                    if not static(t2):
                        pool.wait_ge(ticked, (t2 - 1) * TICKS + (k + 1))
                        pool.wait_ge(sem, value)
                        pool.tensor_tensor(tick[:, 1:2], tick[:, 0:1], tick[:, 0:1], ALU.add).then_inc(ticked, 1)
                    else:
                        pool.wait_ge(sem, value)

                def gathers(t2):
                    for u in range(2):
                        passed(t2, u * (TICKS // 2), idx_ready, t2 * 2 + (u + 1))
                        for k in range(TAPS):
                            i = u * TAPS + k
                            if i % BATCH == 0 and (not static(t2) or i >= GS):
                                passed(t2, u * (TICKS // 2) + 1 + k // BATCH, step,
                                       summed_up(t2 * (2 * TAPS) + (i + BATCH - GS - 1), i + BATCH - GS))
                            pool.indirect_dma_start(g[:, i % GS, :], None, table_dram,
                                                    bass.IndirectOffsetOnAxis(ap=cur_idx[:, u, k:k + 1], axis=0)).then_inc(
                                                        got[i % GS], 16)
                gathers(0)
                with pool.Fori(0, TILES // 2 - 1) as t:
                    gathers(t + 1)

            def gather_count(t2, i):
                return (t2 * (2 * TAPS // GS) + (i // GS + 1)) * 16

            @block.scalar
            def _(act):
                def pair(t2, gt, gslot):
                    for u in range(2):
                        for k in range(TAPS):
                            i = u * TAPS + k
                            m = t2 * (2 * TAPS) + i
                            act.wait_ge(got[i % GS], gather_count(t2, i))
                            if not static(t2) or t2 * 2 * TAPS + i >= VS:
                                act.wait_ge(turned, m - (VS - 1))
                            if not static(t2):
                                apart(act, turned)
                            act.activation(val[:, i % VS, :], g[:, i % GS, 0:C], ACT.Identity,
                                           scale=CW[:, ds(m, 1), 0]).then_inc(first, 1)
                            if i >= BEHIND:
                                move(t2, i - BEHIND, gt, gslot)
                    for i in range(2 * TAPS - BEHIND, 2 * TAPS):
                        move(t2, i, gt, gslot)

                def move(t2, i, gt, gslot):
                    u, k = divmod(i, TAPS)
                    act.wait_ge(turned, t2 * (2 * TAPS) + (i + 1))
                    at = (gt + u) * P
                    act.activation(vt[:, gslot, k, :, at:at + P], ps_t[:, i % TS, 0:CB, :], ACT.Identity).then_inc(kept, 1)

                def group(gr, slot):
                    if not static(gr) or gr >= 2:
                        act.wait_ge(product, gr - 1)
                    for h in range(GT // 2):
                        pair(gr * (GT // 2) + h, 2 * h, slot)

                groups(act, group)

            @block.vector
            def _(dve):
                def put(t2, u):
                    if not static(t2) or t2:
                        dve.wait_ge(got[(u * TAPS + TAPS - 1) % GS],
                                    ((t2 - 1) * (2 * TAPS // GS) + ((u * TAPS + TAPS - 1) // GS + 1)) * 16)
                    dve.tensor_copy(cur_idx[:, u, :], IDX[:, ds(t2 * (2 * TAPS) + u * TAPS, TAPS)]).then_inc(idx_ready, 1)

                waiting = [(b, c) for c in range(NCH - 2) for b in range(CB)]

                def stats(b, c):
                    dve.wait_ge(added, CB * (c + 1))
                    gn.chunk_stats(dve, X, b, c)

                def pair(t2, last=False):
                    for i in range(0, 2 * TAPS, 2):
                        if i == TAPS + 1 and not last:
                            put(t2 + 1, 0)
                        if static(t2) and waiting and i % 4 == 2 and waiting[0][1] + 2 <= t2 // (GT // 2) >= NGR - 2:
                            stats(*waiting.pop(0))
                        m = t2 * (2 * TAPS) + i
                        for q in range(1, 4):
                            for k in range(2):
                                if q == 1:
                                    dve.wait_ge(first, m + (k + 1))
                                else:
                                    dve.wait_ge(step, m * 3 + (2 * q - 3 + k))
                                v = val[:, (i + k) % VS, :]
                                dve.scalar_tensor_tensor(out=v, in0=g[:, (i + k) % GS, q * C:(q + 1) * C],
                                                         scalar=CW[:, ds(m + k, 1), q], in1=v,
                                                         op0=ALU.mult, op1=ALU.add).then_inc(step, 1)
                    if not last:
                        put(t2 + 1, 1)

                def add(gr, slot):
                    for ob in range(CB):
                        dve.wait_ge(product, gr + 1)
                        xs = X[:, ob, ds(gr * CH, CH)]
                        dve.tensor_tensor(xs, ps_o[:, slot, ob, :], xs, ALU.add).then_inc(added, 1)

                def group(gr, slot):
                    for h in range(GT // 2):
                        t2 = gr * (GT // 2) + h
                        pair(t2, static(gr) and gr == NGR - 1 and h == 1)
                    if not static(gr) or gr:
                        add(gr - 1, 1 - slot)

                for u in range(2):
                    put(0, u)
                groups(dve, group)
                for b, c in waiting + [(b, NCH - 2) for b in range(CB)]:
                    stats(b, c)
                add(NGR - 1, 1)
                for b in range(CB):
                    stats(b, NCH - 1)
                gn.channel_moments(dve)
                gn.vector_moments(dve)

            @block.tensor
            def _(pe):
                def turn(gr, gt, k):
                    i = (gt % 2) * TAPS + k
                    m = gr * (GT * TAPS) + (gt * TAPS + k)
                    pe.wait_ge(step, summed_up(m, i + 1))
                    if not static(m) or m >= TS:
                        pe.wait_ge(kept, m - (TS - 1))
                    for b in range(CB):
                        mm = pe.transpose(ps_t[:, i % TS, b, :], val[:, i % VS, b * P:(b + 1) * P], ident[:, :])
                    mm.then_inc(turned, 1)

                def product_part(gr, slot, part, k):
                    ob, b = divmod(part, CB)
                    if part == 0 and k == 0:
                        pe.wait_ge(kept, (gr + 1) * (GT * TAPS))
                        if not static(gr) or gr >= 2:
                            pe.wait_ge(added, (gr - 1) * CB)
                    mm = pe.matmul(ps_o[:, slot, ob, :], w[:, b, k, ob * P:(ob + 1) * P], vt[:, slot, k, b, :],
                                   start=b == 0 and k == 0, stop=b == CB - 1 and k == TAPS - 1)
                    if part == GT - 1 and k == TAPS - 1:
                        mm.then_inc(product, 1)

                def last_products(gt):
                    pe.wait_ge(kept, ((NGR - 1) * GT + gt + 1) * TAPS)
                    if gt == 0:
                        pe.wait_ge(added, (NGR - 2) * CB)
                    at = slice(gt * P, (gt + 1) * P)
                    for ob in range(CB):
                        for b in range(CB):
                            for k in range(TAPS):
                                mm = pe.matmul(ps_o[:, 1, ob, at], w[:, b, k, ob * P:(ob + 1) * P], vt[:, 1, k, b, at],
                                               start=b == 0 and k == 0, stop=b == CB - 1 and k == TAPS - 1)
                    if gt == GT - 1:
                        mm.then_inc(product, 1)

                def group(gr, slot):
                    for gt in range(GT):
                        for k in range(TAPS):
                            turn(gr, gt, k)
                            if not static(gr) or gr:
                                product_part(gr - 1, 1 - slot, gt, k)
                            if static(gr) and gr == NGR - 1 and gt and k == BEHIND + 1:
                                last_products(gt - 1)

                groups(pe, group)
                last_products(GT - 1)

LT = 25
UNIT = 16
UNITS = SIDE // UNIT
LOCAL_BESIDE_LINEAR = 4
KEY_SCALE = float(HD) ** -0.5

class LocalConv:

    def __init__(self, n, V_, L):
        self.V_, self.L = V_, L
        self.w = n.sb("w_local", [P, CB, LT])
        self.bias = n.sb("b_local", [P, CB])
        self.done = n.sem("local_tap")
        self.count = 0
        chunks = [(b, c) for b in range(CB) for c in range(NCH)]
        self.left = [(b, c, LT // 2) for b, c in chunks]
        for i in range(0, len(chunks), 2):
            self.left += [(b, c, t) for t in range(LT) if t != LT // 2 for b, c in chunks[i:i + 2]]

    def centres_left(self):
        return sum(t == LT // 2 for _, _, t in self.left)

    def steps(self, dve, k):
        for b, c, t in self.left[:k]:
            dy, dx = t // 5 - 2, t % 5 - 2
            y0, y1 = max(c * ROWS, -dy), min((c + 1) * ROWS, SIDE - dy)
            x0, x1 = max(0, -dx), min(SIDE, SIDE - dx)
            out = padded(self.L[:, b, :], SIDE)[:, y0:y1, x0:x1]
            src = padded(self.V_[:, b, :], SIDE)[:, y0 + dy:y1 + dy, x0 + dx:x1 + dx]
            if t == LT // 2:
                ins = dve.tensor_scalar(out, src, self.w[:, b, t:t + 1], self.bias[:, b:b + 1], ALU.mult, ALU.add)
            else:
                dve.wait_ge(self.done, self.count - 1)
                ins = dve.scalar_tensor_tensor(out=out, in0=src, scalar=self.w[:, b, t:t + 1], in1=out,
                                               op0=ALU.mult, op1=ALU.add)
            ins.then_inc(self.done, 1)
            self.count += 1
        del self.left[:k]

def qkv_linear(nc, gm, w_dram, b_dram, wl_dram, bl_dram, x3_dram, X, Q, K, V_, local, gn, ahead):
    with ExitStack() as stack:
        n = Names(nc, stack, "lin")
        w = n.sb("w", [P, 3, CB, C])
        bias = n.sb("bias", [P, 3, CB])
        xn = n.sb("xn", [P, CB, PX])
        ps_gn = n.ps("ps_gn", [P, CB * 2])
        ps = n.ps("ps", [P, 4, CH])
        loaded = n.sem("loaded")
        aside = n.sem("x_aside")
        ahead_loaded = n.sem("ahead_loaded")
        normed = n.sem("normed")
        done = n.sem("product_done")
        moved = n.sem("moved")
        moved_act = n.sem("moved_by_act")
        work = [(c, 2, ob) for c in range(NCH) for ob in range(CB)]
        work += [(c, m, ob) for c in range(NCH) for ob in range(CB) for m in (0, 1)]
        by_act = [i for i, (c, m, ob) in enumerate(work) if m == 0 or (m == 2 and ob == 0)]
        by_dve = [i for i in range(len(work)) if i not in by_act]

        def wait_moved(eng, i):
            if i in by_act:
                eng.wait_ge(moved_act, by_act.index(i) + 1)
            else:
                eng.wait_ge(moved, by_dve.index(i) + 1)
        with nc.Block() as block:

            @block.sync
            def _(sp):
                for t, d in ((w[:, :, :, :], w_dram), (bias[:, :, :], b_dram),
                             (local.w[:, :, :], wl_dram), (local.bias[:, :], bl_dram)):
                    sp.dma_start(t, d).then_inc(loaded, 16)
                for b in range(CB):
                    sp.dma_start(x3_dram[:, b, :], X[:, b, :]).then_inc(aside, 16)
                load_ahead(sp, ahead, ahead_loaded)
                sp.wait_ge(aside, 16 * CB)
                sp.wait_ge(ahead_loaded, 16 * len(ahead))

            @block.scalar
            def _(act):
                gn.scalar_std(act)
                act.wait_ge(gn.ready, 1)
                for c in range(NCH):
                    for b in range(CB):
                        act.activation(xn[:, b, c * CH:(c + 1) * CH], X[:, b, c * CH:(c + 1) * CH], ACT.Identity,
                                       scale=gn.scale[:, b:b + 1], bias=gn.shift[:, b:b + 1]).then_inc(normed, 1)
                act.wait_ge(loaded, 16 * 4)
                for i in by_act:
                    c, m, ob = work[i]
                    act.wait_ge(done, i + 1)
                    act.activation((Q, K, V_)[m][:, ob, c * CH:(c + 1) * CH], ps[:, i % 4, :], ACT.Identity,
                                   bias=bias[:, m, ob:ob + 1]).then_inc(moved_act, 1)

            @block.tensor
            def _(pe):
                gn.tensor_join(pe, ps_gn[:, :], gm[:, :])
                pe.wait_ge(loaded, 16 * 4)
                for i, (c, m, ob) in enumerate(work):
                    pe.wait_ge(normed, CB * (c + 1))
                    if i >= 4:
                        wait_moved(pe, i - 4)
                    for b in range(CB):
                        mm = pe.matmul(ps[:, i % 4, :], w[:, m, b, ob * P:(ob + 1) * P], xn[:, b, c * CH:(c + 1) * CH],
                                       start=b == 0, stop=b == CB - 1)
                    mm.then_inc(done, 1)

            @block.vector
            def _(dve):
                gn.vector_affine(dve, ps_gn[:, :])
                dve.wait_ge(loaded, 16 * 4)
                for i in by_dve:
                    c, m, ob = work[i]
                    dve.wait_ge(done, i + 1)
                    out = (Q, K, V_)[m][:, ob, c * CH:(c + 1) * CH]
                    dve.tensor_scalar(out, ps[:, i % 4, :], bias[:, m, ob:ob + 1], KEY_SCALE if m == 1 else 1.0,
                                      ALU.add, ALU.mult).then_inc(moved, 1)
                    if m == 1:
                        if c == 0 and ob == 0:
                            dve.wait_ge(moved_act, by_act.index(CB * NCH - 2) + 1)
                            dve.wait_ge(moved, by_dve.index(CB * NCH - 1) + 1)
                            dve.wait_ge(aside, 16 * CB)
                            dve.wait_ge(normed, CB * NCH)
                        local.steps(dve, LOCAL_BESIDE_LINEAR)

def axial_attention(nc, ident, mask, x3_dram, Q, K, V_, L, local, ahead):
    with ExitStack() as stack:
        n = Names(nc, stack, "axial")
        R = 2
        turned_v = n.sb("turned_v", [P, TILES, P])
        v1 = n.sb("v1", [P, PX])
        s = n.sb("s", [P, R, CH])
        e = n.sb("e", [P, R, CH])
        pr = n.sb("prob", [P, R, CH])
        pt = n.sb("prob_turned", [P, R, CH])
        mx = n.sb("max", [P, R, 8])
        sm = n.sb("sum", [P, R, 8])
        ps_s = n.ps("ps_s", [P, HPB, CH])
        ps_t = n.ps("ps_t", [P, 2, CH])
        ps_v = n.ps("ps_v", [P, 2, CH])

        loaded = n.sem("loaded")
        scored = n.sem("scored")
        shifted = n.sem("dve_softmax")
        inverted = n.sem("inverted")
        exped = n.sem("exped")
        probs = n.sem("probs")
        turned = n.sem("turned")
        moved = n.sem("moved")
        v_turned = n.sem("v_turned")
        v_moved = n.sem("v_moved")
        product = n.sem("product")
        line = n.sem("lines_moved")
        added = n.sem("lines_added")

        passes = [(b, d) for b in range(CB) for d in range(2)]
        items = [(p, u, j) for p in range(len(passes)) for u in range(UNITS) for j in range(HPB)]
        NI = UNITS * HPB

        def group_line(u, g, r):
            return u * UNIT + 4 * (g // 2) + 2 * r + g % 2

        AHEAD = 3
        per_item = 5
        at_pass = 4

        with nc.Block() as block:

            @block.sync
            def _(sp):
                load_ahead(sp, ahead, loaded)
                sp.wait_ge(scored, len(items))
                sp.dma_start(K[:, :, :], x3_dram).then_inc(loaded, 16)
                sp.wait_ge(loaded, 16 * (len(ahead) + 1))

            @block.tensor
            def _(pe):
                def scores(i):
                    p, u, j = items[i]
                    b, d = passes[p]
                    if i >= HPB:
                        pe.wait_ge(shifted, 3 * (i - HPB) + 1)
                    hd = slice(j * HD, (j + 1) * HD)
                    for g in range(8):
                        for r in range(2):
                            at = group_line(u, g, r)
                            px = slice(at * SIDE, (at + 1) * SIDE) if d == 0 else slice(at, PX, SIDE)
                            mm = pe.matmul(ps_s[r * SIDE:(r + 1) * SIDE, j, g * SIDE:(g + 1) * SIDE],
                                           Q[hd, b, px], K[hd, b, px], start=True, stop=True)
                    mm.then_inc(scored, 1)

                def turn_v(p):
                    b, d = passes[p]
                    src = V_[:, b, :] if d == 0 else v1[:, :]
                    if d == 1:
                        pe.wait_ge(line, 2 * UNITS * (b + 1))
                    for g in range(TILES // 4):
                        k = p * (TILES // 4) + g
                        pe.wait_ge(moved, p * NI) if g == 0 and p else None
                        if g >= 2:
                            pe.wait_ge(v_moved, k - 1)
                        for t in range(4):
                            mm = pe.transpose(ps_t[:, g % 2, t * P:(t + 1) * P],
                                              src[:, (4 * g + t) * P:(4 * g + t + 1) * P], ident[:, :])
                        mm.then_inc(v_turned, 1)
                    pe.wait_ge(v_moved, (p + 1) * (TILES // 4))

                def turn(i):
                    pe.wait_ge(probs, i + 1)
                    if i >= 2:
                        pe.wait_ge(moved, i - 1)
                    for t in range(4):
                        mm = pe.transpose(ps_t[:, i % 2, t * P:(t + 1) * P], pr[:, i % R, t * P:(t + 1) * P], ident[:, :])
                    mm.then_inc(turned, 1)

                def values(i):
                    p, u, j = items[i]
                    b, d = passes[p]
                    pe.wait_ge(moved, i + 1)
                    if j == 0:
                        units = p * UNITS + u
                        rows = sum(1 for q in range(units) if passes[q // UNITS][1] == 0)
                        if rows:
                            pe.wait_ge(line, 2 * rows)
                        if units - rows:
                            pe.wait_ge(added, 2 * (units - rows))
                    for g in range(8):
                        for r in range(2):
                            at = group_line(u, g, r)
                            k = slice((at % 2) * SIDE, (at % 2 + 1) * SIDE)
                            slot = (at % UNIT) // 2
                            mm = pe.matmul(ps_v[j * HD:(j + 1) * HD, at % 2, slot * SIDE:(slot + 1) * SIDE],
                                           turned_v[k, at // 2, j * HD:(j + 1) * HD],
                                           pt[k, i % R, (g // 2) * P + r * SIDE:(g // 2) * P + (r + 1) * SIDE],
                                           start=True, stop=True)
                    mm.then_inc(product, 1)

                for i in range(AHEAD):
                    scores(i)
                for p in range(len(passes)):
                    turn_v(p)
                    for i in range(p * NI, (p + 1) * NI):
                        if i + AHEAD < len(items):
                            scores(i + AHEAD)
                        turn(i)
                        if i > p * NI:
                            values(i - 1)
                    values((p + 1) * NI - 1)

            @block.scalar
            def _(act):
                def exp(i):
                    act.wait_ge(shifted, 3 * (i + 1))
                    if i >= R:
                        act.wait_ge(probs, i - R + 1)
                    for g in range(8):
                        at = slice(g * SIDE, (g + 1) * SIDE)
                        ins = act.activation(e[:, i % R, at], s[:, i % R, at], ACT.Exp, bias=mx[:, i % R, g:g + 1],
                                             accum_out=sm[:, i % R, g:g + 1])
                    ins.then_inc(exped, 1)

                def move(i):
                    act.wait_ge(turned, i + 1)
                    if i >= R:
                        act.wait_ge(product, i - R + 1)
                    act.activation(pt[:, i % R, :], ps_t[:, i % 2, :], ACT.Identity).then_inc(moved, 1)

                def lines(i):
                    p, u, j = items[i]
                    act.wait_ge(product, i + 1)
                    for par in range(2):
                        dst = v1[:, :].rearrange("p (x y) -> p y x", y=SIDE)[:, u * UNIT + par:(u + 1) * UNIT:2, :]
                        act.activation(dst, ps_v[:, par, :].rearrange("p (y x) -> p y x", x=SIDE), ACT.Identity).then_inc(line, 1)

                for p in range(len(passes)):
                    b, d = passes[p]
                    exp(p * NI)
                    if p:
                        act.wait_ge(product, p * NI)
                    for g in range(TILES // 4):
                        act.wait_ge(v_turned, p * (TILES // 4) + g + 1)
                        act.activation(turned_v[:, 4 * g:4 * g + 4, :].rearrange("p t c -> p (t c)"), ps_t[:, g % 2, :],
                                       ACT.Identity).then_inc(v_moved, 1)
                    for i in range(p * NI, (p + 1) * NI):
                        if i > p * NI:
                            exp(i)
                            move(i - 1)
                            if items[i - 1][2] == 0 and d == 0 and i - 1 > p * NI:
                                lines(i - 2)
                    move((p + 1) * NI - 1)
                    if d == 0:
                        lines((p + 1) * NI - 1)

            @block.gpsimd
            def _(pool):
                for i in range(len(items)):
                    pool.wait_ge(inverted, i + 1)
                    if i >= R:
                        pool.wait_ge(turned, i - R + 1)
                    pool.tensor_tensor(pr[:, i % R, :].rearrange("p (g k) -> p g k", k=SIDE),
                                       e[:, i % R, :].rearrange("p (g k) -> p g k", k=SIDE),
                                       sm[:, i % R, :].unsqueeze(2).to_broadcast([P, 8, SIDE]), ALU.mult).then_inc(probs, 1)

            @block.vector
            def _(dve):
                def first(i):
                    p, u, j = items[i]
                    b, d = passes[p]
                    sv = s[:, i % R, :].rearrange("p (g k) -> p g k", k=SIDE)
                    dve.wait_ge(scored, i + 1)
                    if i >= R:
                        dve.wait_ge(exped, i - R + 1)
                    dve.tensor_tensor(sv, ps_s[:, j, :].rearrange("p (g k) -> p g k", k=SIDE),
                                      mask[:, d, b * HPB + j, :].unsqueeze(1).to_broadcast([P, 8, SIDE]), ALU.add).then_inc(shifted, 1)
                    local.steps(dve, 1)
                    dve.wait_ge(shifted, 3 * i + 1)
                    dve.reduce_max(mx[:, i % R, :], sv, AX.X).then_inc(shifted, 1)
                    local.steps(dve, 1)
                    dve.wait_ge(shifted, 3 * i + 2)
                    dve.tensor_scalar(mx[:, i % R, :], mx[:, i % R, :], -1.0, None, ALU.mult).then_inc(shifted, 1)

                def second(i):
                    dve.wait_ge(exped, i + 1)
                    dve.reciprocal(sm[:, i % R, :], sm[:, i % R, :]).then_inc(inverted, 1)

                def add_lines(i):
                    p, u, j = items[i]
                    b, d = passes[p]
                    local.steps(dve, local.centres_left())
                    dve.wait_ge(local.done, local.count)
                    dve.wait_ge(product, i + 1)
                    for par in range(2):
                        dst = L[:, b, :].rearrange("p (y x) -> p x y", x=SIDE)[:, u * UNIT + par:(u + 1) * UNIT:2, :]
                        dve.tensor_tensor(dst, ps_v[:, par, :].rearrange("p (x y) -> p x y", y=SIDE), dst, ALU.add).then_inc(added, 1)
                    dve.wait_ge(added, 2 * (b * UNITS + u + 1))

                for p in range(len(passes)):
                    b, d = passes[p]
                    for i in range(p * NI, (p + 1) * NI):
                        if i == 0:
                            local.steps(dve, at_pass)
                            first(i)
                            local.steps(dve, 2)
                        if i + 1 < len(items):
                            first(i + 1)
                        if i and i == p * NI:
                            local.steps(dve, at_pass)
                        second(i)
                        local.steps(dve, per_item - 2)
                        if d == 1 and i - p * NI >= HPB and (i - p * NI) % HPB == 1:
                            add_lines(i - 2)
                    if d == 1:
                        add_lines((p + 1) * NI - 1)
                local.steps(dve, len(local.left))

def output(nc, w, bias, out_dram, L, x, y):
    with ExitStack() as stack:
        n = Names(nc, stack, "out")
        ps = n.ps("ps", [P, 4, CH])
        done = n.sem("product_done")
        ready = n.sem("ready")
        stored = n.sem("stored")
        work = [(c, ob) for c in range(NCH) for ob in range(CB)]
        with nc.Block() as block:

            @block.sync
            def _(sp):
                for c in range(0, NCH, 2):
                    sp.wait_ge(ready, 2 * (c + 2))
                    sp.dma_start(out_dram.rearrange("(b p) n -> p b n", p=P)[:, :, c * CH:(c + 2) * CH],
                                 y[:, :, c * CH:(c + 2) * CH]).then_inc(stored, 16)
                sp.wait_ge(stored, 16 * (NCH // 2))

            @block.tensor
            def _(pe):
                for i, (c, ob) in enumerate(work):
                    if i >= 4:
                        pe.wait_ge(ready, i - 3)
                    for b in range(CB):
                        mm = pe.matmul(ps[:, i % 4, :], w[:, b, ob * P:(ob + 1) * P], L[:, b, c * CH:(c + 1) * CH],
                                       start=b == 0, stop=b == CB - 1)
                    mm.then_inc(done, 1)

            @block.vector
            def _(dve):
                for i, (c, ob) in enumerate(work):
                    dve.wait_ge(done, i + 1)
                    at = slice(c * CH, (c + 1) * CH)
                    dve.scalar_tensor_tensor(out=y[:, ob, at], in0=ps[:, i % 4, :], scalar=bias[:, ob:ob + 1],
                                             in1=x[:, ob, at], op0=ALU.add, op1=ALU.add).then_inc(ready, 1)

def conv_preact_kernel(nc, ins, out):
    dw = nc.dram_tensor("depthwise_out", (2 * CB, P, PX), F32, kind="Internal").ap()
    parts = nc.dram_tensor("unit_parts", (2, 2, C, PX), F16, kind="Internal").ap()
    vt = nc.dram_tensor("v_turned", (HEADS, P, MT * VW), F32, kind="Internal").ap()
    sums = nc.dram_tensor("attention_sums", (NG, VW, NB), F32, kind="Internal").ap()
    table = nc.dram_tensor("corner_table", (TAB * TAB, 4 * C), F32, kind="Internal").ap()
    x3 = nc.dram_tensor("image3", (P, CB, PX), F32, kind="Internal").ap()

    with ExitStack() as stack:
        n = Names(nc, stack, "padded")
        XH = n.sb("x_high", [P, CB, PAD5 * PAD5], F32R)
        XL = n.sb("x_low", [P, CB, PAD5 * PAD5], F32R)
        weights = ConvWeights(n, [ins["w_q"], ins["w_k"], ins["w_v"]])
        norm_and_split(nc, ins["x"], ins["group_mean"], XH, XL, weights)
        conv_qkv(nc, weights, ins["w_depthwise"], ins["head_sum"],
                 ins["identity"], dw, parts, vt, XH, XL)
    with ExitStack() as stack:
        n = Names(nc, stack, "image")
        X = n.sb("x", [P, CB, PX])
        gm = n.sb("group_mean", [P, P])
        ident = n.sb("identity", [P, P])
        attention(nc, parts, vt, ins["temperature"], sums,
                  [(X[:, b, :], ins["x"][b * P:(b + 1) * P, :]) for b in range(CB)] +
                  [(gm[:, :], ins["group_mean"]), (ident[:, :], ins["identity"])])
        gn = [GroupNorm(Names(nc, stack, f"layer{i}")) for i in (1, 2, 3)]
        project(nc, sums, ins["w_project"], ins["spread"], X, gn[0])
        covariance_gate(nc, gm, ins["eye"], ins["w_gate1"], ins["b_gate1"], ins["w_gate2"],
                        ins["b_gate2"], X, gn[0], gn[1])
        with ExitStack() as inner:
            n = Names(nc, inner, "corners")
            IDX = n.sb("index", [P, TILES * TAPS], I32)
            CW = n.sb("weight", [P, TILES * TAPS, 4])
            w = n.sb("w_deform", [P, CB, TAPS, C])
            offsets_and_table(nc, gm, ident, ins["w_offset"], ins["b_offset"], ins["positions"], table, X, IDX, CW,
                              gn[1], [(w[:, :, :, :], ins["w_deform"])])
            deform(nc, ident, w, table, X, IDX, CW, gn[2])
        with ExitStack() as inner:
            n = Names(nc, inner, "axial_in")
            Q = n.sb("q", [P, CB, PX])
            K = n.sb("k", [P, CB, PX])
            V = n.sb("v", [P, CB, PX])
            local = LocalConv(n, V, X)
            mask = n.sb("mask", [P, 2, HEADS, SIDE])
            w_out = n.sb("w_out", [P, CB, C])
            b_out = n.sb("b_out", [P, CB])
            qkv_linear(nc, gm, ins["w_linear"], ins["b_linear"], ins["w_local"], ins["b_local"],
                       x3, X, Q, K, V, local, gn[2], [(mask[:, :, :, :], ins["masks"])])
            axial_attention(nc, ident, mask, x3, Q, K, V, X, local,
                            [(w_out[:, :, :], ins["w_out"]), (b_out[:, :], ins["b_out"])])
            output(nc, w_out, b_out, out, X, K, Q)

def _laid_out(a):
    def conv(w):
        taps = w.shape[2] * w.shape[3]
        return w.reshape(CB, P, CB, P, taps).transpose(0, 2, 3, 4, 1).reshape(CB, CB, P, taps * P)

    def linear(w):
        return w.reshape(CB, P, C).transpose(1, 0, 2)

    def channel(v):
        return v.reshape(CB, P).T

    tile, part, tap = np.meshgrid(np.arange(TILES), np.arange(P), np.arange(TAPS))
    positions = np.stack([2 * tile + part // SIDE + tap // 3, part % SIDE + tap % 3], 1)
    masks = np.stack([a["L3_conv_mask_w"], a["L3_conv_mask_h"]], 0).transpose(2, 0, 1, 3)
    spread = np.zeros((NG, NNB * CB, P), np.float32)
    for g in range(NG):
        head, nb = divmod(g, NNB)
        spread[g, nb * CB + head // HPB, head % HPB * HD:(head % HPB + 1) * HD] = 1.0
    ins = {
        "spread": spread,
        "x": a["x"].reshape(PX, C).T,
        "group_mean": np.kron(np.eye(P // GROUP), np.full((GROUP, GROUP), 1.0 / GROUP)).astype(np.float32),
        "head_sum": np.kron(np.eye(HPB), np.ones((HD, HD))).astype(np.float32),
        "identity": np.eye(P, dtype=np.float32),
        "eye": linear(np.eye(C, dtype=np.float32)),
        "positions": positions.reshape(P, 2, TILES * TAPS).astype(np.float32),
        "w_q": conv(a["L0_conv_W1"]), "w_k": conv(a["L0_conv_W3"]), "w_v": conv(a["L0_conv_W5"]),
        "w_depthwise": a["L0_conv_Wdw"].reshape(3 * CB, P, 9).transpose(1, 0, 2),
        "temperature": np.broadcast_to(np.repeat(a["L0_conv_temperature"].reshape(HEADS), NNB)[None], (P, NG)),
        "w_project": linear(a["L0_conv_Wproj"][:, :, 0, 0].T),
        "w_gate1": linear(a["L1_conv_w1"][1, 1]), "b_gate1": channel(a["L1_conv_b1"]),
        "w_gate2": linear(a["L1_conv_w2"][1, 1]), "b_gate2": channel(a["L1_conv_b2"]),
        "w_offset": a["L2_conv_offset_w"].reshape(TAPS, CB, P, OM).transpose(2, 1, 0, 3).reshape(P, CB, TAPS * OM),
        "b_offset": a["L2_conv_offset_b"].reshape(OM, 1),
        "w_deform": a["L2_conv_dcn_weight"].reshape(C, CB, P, TAPS).transpose(2, 1, 3, 0),
        "w_linear": np.stack([linear(a["L3_conv_" + k].T) for k in ("Wq", "Wk", "Wv")], 1),
        "b_linear": np.stack([channel(a["L3_conv_" + k]) for k in ("bq", "bk", "bv")], 1),
        "masks": np.concatenate([masks, masks], 0),
        "w_local": a["L3_conv_Wlepe"].reshape(LT, CB, P).transpose(2, 1, 0), "b_local": channel(a["L3_conv_blepe"]),
        "w_out": linear(a["L3_conv_Wo"].T), "b_out": channel(a["L3_conv_bo"]),
    }
    return {k: np.ascontiguousarray(v) for k, v in ins.items()}

def kernel(**inputs):
    from concourse import bacc
    from concourse.bass_utils import run_bass_kernel_spmd

    nc = bacc.Bacc("TRN2", target_bir_lowering=False, num_devices=1)
    arrays = _laid_out({k: np.asarray(v) for k, v in inputs.items()})
    ins = {k: nc.dram_tensor(f"in_{k}", v.shape, mybir.dt.from_np(v.dtype), kind="ExternalInput").ap()
           for k, v in arrays.items()}
    out = nc.dram_tensor("out", (C, PX), F32, kind="ExternalOutput").ap()
    conv_preact_kernel(nc, ins, out)
    result = run_bass_kernel_spmd(nc, [{f"in_{k}": v for k, v in arrays.items()}], core_ids=[0])
    return result.results[0]["out"].T.reshape(1, SIDE, SIDE, C)
```
